# Optimizing a Trainium2 kernel written in Bass

```python
import numpy as np
import jax
import jax.numpy as jnp

def _softmax(x, axis=-1):
    return jax.nn.softmax(x, axis=axis)

def _gelu(x):
    return jax.nn.gelu(x, approximate=True)

def _silu(x):
    return jax.nn.silu(x)

def _sigmoid(x):
    return jax.nn.sigmoid(x)

def _layernorm(x, axis=-1, eps=1e-05):
    m = jnp.mean(x, axis=axis, keepdims=True)
    v = jnp.var(x, axis=axis, keepdims=True)
    return (x - m) / jnp.sqrt(v + eps)

def _scatter_add(tgt, idx, src, axis=0):
    return tgt.at[idx].add(src)

def _segment_sum(src, seg, n):
    return jax.ops.segment_sum(src, seg, n)
kernel_name = 'mk_xattn_seq_d4_seqx_r4_2b202d'

def setup_inputs(seed: int=0):
    np.random.seed(seed)
    _w = jnp.asarray

    def _rec_inputs():
        import jax
        import jax.numpy as jnp
        _rk = jax.random.key(seed)
        x = -0.0002928 + 1 * jax.random.normal(jax.random.fold_in(_rk, 1), (4, 1024, 256), jnp.float32)
        _lenS = 1024 - jax.random.randint(jax.random.fold_in(_rk, 7), (4,), 0, max(1, 1024 // 4) + 1, jnp.int32)
        _lenS2 = 77 - jax.random.randint(jax.random.fold_in(_rk, 8), (4,), 0, max(1, 77 // 4) + 1, jnp.int32)
        _ctx_1024P = jax.random.normal(jax.random.fold_in(_rk, 11), (4, 16, 256), jnp.float32)
        _ctx_1024c = jax.random.dirichlet(jax.random.fold_in(_rk, 511), 0.3 * jnp.ones((16,), jnp.float32), (4, 77))
        _ctx_1024t = jnp.einsum('bsk,bkd->bsd', _ctx_1024c, _ctx_1024P)
        _ctx_1024t = _ctx_1024t * jax.lax.rsqrt(jnp.mean(jnp.square(_ctx_1024t)) + 1e-12) * 0.953939
        ctx_1024 = 0.000227908 + 0.99994 * (_ctx_1024t + 0.3 * jax.random.normal(jax.random.fold_in(_rk, 611), (4, 77, 256), jnp.float32))
        fside_Bx16xSxS2_0 = jax.random.uniform(jax.random.fold_in(_rk, 13), (4, 16, 1024, 77), jnp.float32, 0.0, 1)
        _validS = jnp.arange(1024)[None, :] < _lenS[:, None]
        _validS2 = jnp.arange(77)[None, :] < _lenS2[:, None]
        _causal = jnp.tril(jnp.ones((1024, 1024), dtype=bool))
        mask_Bx16xSxS2_bk0 = jnp.logical_not(jnp.broadcast_to(_validS2[:, None, None, :], (4, 16, 1024, 77)))
        return (x, ctx_1024, fside_Bx16xSxS2_0, mask_Bx16xSxS2_bk0)
    x, ctx_1024, fside_Bx16xSxS2_0, mask_Bx16xSxS2_bk0 = _rec_inputs()

    def _L0_xattn_setup():
        import jax, jax.numpy as jnp
        import numpy as np
        B, T, S, D, H, F = (2, 512, 128, 256, 16, 1024)
        DH = D // H
        EPS = 1e-05

        def _ln(x, g, b):
            m = x.mean(-1, keepdims=True)
            v = ((x - m) ** 2).mean(-1, keepdims=True)
            return (x - m) * jax.lax.rsqrt(v + EPS) * g + b
        key = jax.random.key(seed)
        ks = jax.random.split(key, 8)
        w = lambda k, shape: jax.random.normal(k, shape, dtype=jnp.float32) * 0.02
        return {'x': jax.random.normal(ks[0], (B, T, D), dtype=jnp.float32), 'context': jax.random.normal(ks[1], (B, S, D), dtype=jnp.float32), 'w_qkv': w(ks[2], (D, 3 * D)), 'b_qkv': jnp.zeros((3 * D,), jnp.float32), 'w_ckv': w(ks[3], (D, 2 * D)), 'b_ckv': jnp.zeros((2 * D,), jnp.float32), 'g1': jnp.ones((D,), jnp.float32), 'be1': jnp.zeros((D,), jnp.float32), 'g2': jnp.ones((D,), jnp.float32), 'be2': jnp.zeros((D,), jnp.float32), 'gf': jnp.ones((D,), jnp.float32), 'bf': jnp.zeros((D,), jnp.float32), 'w1': w(ks[4], (D, F)), 'b1': jnp.zeros((F,), jnp.float32), 'w2': w(ks[5], (F, D)), 'b2': jnp.zeros((D,), jnp.float32)}
    _L0_xattn_all = _L0_xattn_setup()
    _L0_xattn_in = {k: v for k, v in _L0_xattn_all.items() if k in ('w_qkv', 'b_qkv', 'w_ckv', 'b_ckv', 'g1', 'be1', 'g2', 'be2', 'gf', 'bf', 'w1', 'b1', 'w2', 'b2')}
    del _L0_xattn_all

    def _L1_xattn_setup():
        import math
        import jax, jax.numpy as jnp
        import numpy as np
        D_MODEL = 256
        N_HEADS = 16
        HEAD_DIM = D_MODEL // N_HEADS
        FEATURE_DIM = 16
        WINDOW = 64
        EPS_NORM = 1e-06
        EPS_DEN = 1e-06
        _TRIU_I, _TRIU_J = np.triu_indices(FEATURE_DIM)

        def taylor_feature_map(x):
            B, T, H, d = x.shape
            ones = jnp.ones((B, T, H, 1), dtype=x.dtype)
            outer = jnp.einsum('bthd,bthe->bthde', x, x)
            scale = jnp.full((d, d), 1.0 / math.sqrt(2), dtype=x.dtype)
            scale = scale.at[jnp.arange(d), jnp.arange(d)].set(0.5)
            outer = outer * scale
            quadratic = outer[..., _TRIU_I, _TRIU_J]
            return jnp.concatenate([ones, x, quadratic], axis=-1)

        def rmsnorm(x, w):
            var = jnp.mean(x * x, axis=-1, keepdims=True)
            return x * jax.lax.rsqrt(var + EPS_NORM) * w

        def _forward(x, encoder_out, norm_w, Wq, Wkv, Wqf, Wkf, Wwin, Wout):
            residual = x
            xn = rmsnorm(x, norm_w)
            B, T_dec, _ = xn.shape
            T_enc = encoder_out.shape[1]
            H, hd = (N_HEADS, HEAD_DIM)
            q = (xn @ Wq).reshape(B, T_dec, H, hd)
            kv = (encoder_out @ Wkv).reshape(B, T_enc, 2, H, hd)
            k, v = (kv[:, :, 0], kv[:, :, 1])
            q_phi = taylor_feature_map(q @ Wqf)
            k_phi = taylor_feature_map(k @ Wkf)
            kv_state = jnp.einsum('bshf,bshd->bhfd', k_phi, v)
            k_state = k_phi.sum(axis=1)
            linear_out = jnp.einsum('bthf,bhfd->bthd', q_phi, kv_state)
            normalizer = jnp.einsum('bthf,bhf->bth', q_phi, k_state)[..., None]
            linear_out = (linear_out / (normalizer + EPS_DEN)).reshape(B, T_dec, D_MODEL)
            kv_win = (xn @ Wwin).reshape(B, T_dec, 2, H, hd)
            k_win, v_win = (kv_win[:, :, 0], kv_win[:, :, 1])
            scores = jnp.einsum('bthd,bshd->bhts', q, k_win) * (1.0 / math.sqrt(hd))
            i = jnp.arange(T_dec)[:, None]
            j = jnp.arange(T_dec)[None, :]
            allowed = (j <= i) & (j >= i - WINDOW)
            scores = jnp.where(allowed, scores, jnp.finfo(scores.dtype).min)
            probs = jax.nn.softmax(scores, axis=-1)
            window_out = jnp.einsum('bhts,bshd->bthd', probs, v_win).reshape(B, T_dec, D_MODEL)
            combined = jnp.concatenate([linear_out, window_out], axis=-1)
            return residual + combined @ Wout
        key = jax.random.key(seed)
        ks = jax.random.split(key, 9)
        B, T = (2, 512)
        std = 0.02
        return {'x': jax.random.normal(ks[0], (B, T, D_MODEL), jnp.float32), 'encoder_out': jax.random.normal(ks[1], (B, T, D_MODEL), jnp.float32), 'norm_w': jnp.ones((D_MODEL,), jnp.float32), 'Wq': jax.random.normal(ks[2], (D_MODEL, D_MODEL), jnp.float32) * std, 'Wkv': jax.random.normal(ks[3], (D_MODEL, 2 * D_MODEL), jnp.float32) * std, 'Wqf': jax.random.normal(ks[4], (HEAD_DIM, FEATURE_DIM), jnp.float32) * std, 'Wkf': jax.random.normal(ks[5], (HEAD_DIM, FEATURE_DIM), jnp.float32) * std, 'Wwin': jax.random.normal(ks[6], (D_MODEL, 2 * D_MODEL), jnp.float32) * std, 'Wout': jax.random.normal(ks[7], (2 * D_MODEL, D_MODEL), jnp.float32) * std}
    _L1_xattn_all = _L1_xattn_setup()
    _L1_xattn_in = {k: v for k, v in _L1_xattn_all.items() if k in ('norm_w', 'Wq', 'Wkv', 'Wqf', 'Wkf', 'Wwin', 'Wout')}
    del _L1_xattn_all

    def _L2_xattn_setup():
        import jax, jax.numpy as jnp
        import numpy as np
        D_MODEL = 256
        N_HEADS = 16
        D_HEAD = D_MODEL // N_HEADS
        LN_EPS = 1e-05

        def _xavier(key, shape):
            lim = float(np.sqrt(6.0 / (shape[0] + shape[1])))
            return jax.random.uniform(key, shape, jnp.float32, -lim, lim)
        key = jax.random.key(seed)
        ks = jax.random.split(key, 10)
        B, Nq, Nk = (2, 512, 512)
        queries = jax.random.normal(ks[0], (B, Nq, D_MODEL), jnp.float32)
        keys = jax.random.normal(ks[1], (B, Nk, D_MODEL), jnp.float32)
        values = jax.random.normal(ks[2], (B, Nk, D_MODEL), jnp.float32)
        attention_mask = jax.random.bernoulli(ks[3], 0.1, (B, N_HEADS, Nq, Nk))
        attention_weights = jax.random.uniform(ks[4], (B, N_HEADS, Nq, Nk), jnp.float32)
        Wq = _xavier(ks[5], (D_MODEL, D_MODEL))
        Wk = _xavier(ks[6], (D_MODEL, D_MODEL))
        Wv = _xavier(ks[7], (D_MODEL, D_MODEL))
        Wo = _xavier(ks[8], (D_MODEL, D_MODEL))
        b = jnp.zeros((D_MODEL,), jnp.float32)
        gamma = jnp.ones((D_MODEL,), jnp.float32)
        beta = jnp.zeros((D_MODEL,), jnp.float32)
        return {'queries': queries, 'keys': keys, 'values': values, 'attention_mask': attention_mask, 'attention_weights': attention_weights, 'Wq': Wq, 'bq': b, 'Wk': Wk, 'bk': b, 'Wv': Wv, 'bv': b, 'Wo': Wo, 'bo': b, 'gamma': gamma, 'beta': beta}
    _L2_xattn_all = _L2_xattn_setup()
    _L2_xattn_in = {k: v for k, v in _L2_xattn_all.items() if k in ('Wq', 'bq', 'Wk', 'bk', 'Wv', 'bv', 'Wo', 'bo', 'gamma', 'beta')}
    del _L2_xattn_all

    def _L3_xattn_setup():
        import jax, jax.numpy as jnp
        import numpy as np
        B, Q, KV = (2, 512, 512)
        D_MODEL = 256
        N_HEADS = 16
        D_KV = 64
        EPS = 1e-06
        key = jax.random.key(seed)
        ks = jax.random.split(key, 7)
        s = 0.02
        return {'hidden_states': jax.random.normal(ks[0], (B, Q, D_MODEL), jnp.float32), 'key_value_states': jax.random.normal(ks[1], (B, KV, D_MODEL), jnp.float32), 'wq': jax.random.normal(ks[2], (D_MODEL, N_HEADS * D_KV), jnp.float32) * s, 'wk': jax.random.normal(ks[3], (D_MODEL, N_HEADS * D_KV), jnp.float32) * s, 'wv': jax.random.normal(ks[4], (D_MODEL, N_HEADS * D_KV), jnp.float32) * s, 'wo': jax.random.normal(ks[5], (N_HEADS * D_KV, D_MODEL), jnp.float32) * s, 'norm_w': jnp.ones((D_MODEL,), jnp.float32)}
    _L3_xattn_all = _L3_xattn_setup()
    _L3_xattn_in = {k: v for k, v in _L3_xattn_all.items() if k in ('wq', 'wk', 'wv', 'wo', 'norm_w')}
    del _L3_xattn_all
    return {'x': x, 'ctx_1024': ctx_1024, 'fside_Bx16xSxS2_0': fside_Bx16xSxS2_0, 'mask_Bx16xSxS2_bk0': mask_Bx16xSxS2_bk0, 'L0_xattn_w_qkv': _L0_xattn_in['w_qkv'], 'L0_xattn_b_qkv': _L0_xattn_in['b_qkv'], 'L0_xattn_w_ckv': _L0_xattn_in['w_ckv'], 'L0_xattn_b_ckv': _L0_xattn_in['b_ckv'], 'L0_xattn_g1': _L0_xattn_in['g1'], 'L0_xattn_be1': _L0_xattn_in['be1'], 'L0_xattn_g2': _L0_xattn_in['g2'], 'L0_xattn_be2': _L0_xattn_in['be2'], 'L0_xattn_gf': _L0_xattn_in['gf'], 'L0_xattn_bf': _L0_xattn_in['bf'], 'L0_xattn_w1': _L0_xattn_in['w1'], 'L0_xattn_b1': _L0_xattn_in['b1'], 'L0_xattn_w2': _L0_xattn_in['w2'], 'L0_xattn_b2': _L0_xattn_in['b2'], 'L1_xattn_norm_w': _L1_xattn_in['norm_w'], 'L1_xattn_Wq': _L1_xattn_in['Wq'], 'L1_xattn_Wkv': _L1_xattn_in['Wkv'], 'L1_xattn_Wqf': _L1_xattn_in['Wqf'], 'L1_xattn_Wkf': _L1_xattn_in['Wkf'], 'L1_xattn_Wwin': _L1_xattn_in['Wwin'], 'L1_xattn_Wout': _L1_xattn_in['Wout'], 'L2_xattn_Wq': _L2_xattn_in['Wq'], 'L2_xattn_bq': _L2_xattn_in['bq'], 'L2_xattn_Wk': _L2_xattn_in['Wk'], 'L2_xattn_bk': _L2_xattn_in['bk'], 'L2_xattn_Wv': _L2_xattn_in['Wv'], 'L2_xattn_bv': _L2_xattn_in['bv'], 'L2_xattn_Wo': _L2_xattn_in['Wo'], 'L2_xattn_bo': _L2_xattn_in['bo'], 'L2_xattn_gamma': _L2_xattn_in['gamma'], 'L2_xattn_beta': _L2_xattn_in['beta'], 'L3_xattn_wq': _L3_xattn_in['wq'], 'L3_xattn_wk': _L3_xattn_in['wk'], 'L3_xattn_wv': _L3_xattn_in['wv'], 'L3_xattn_wo': _L3_xattn_in['wo'], 'L3_xattn_norm_w': _L3_xattn_in['norm_w']}

def reference(x, ctx_1024, fside_Bx16xSxS2_0, mask_Bx16xSxS2_bk0, L0_xattn_w_qkv, L0_xattn_b_qkv, L0_xattn_w_ckv, L0_xattn_b_ckv, L0_xattn_g1, L0_xattn_be1, L0_xattn_g2, L0_xattn_be2, L0_xattn_gf, L0_xattn_bf, L0_xattn_w1, L0_xattn_b1, L0_xattn_w2, L0_xattn_b2, L1_xattn_norm_w, L1_xattn_Wq, L1_xattn_Wkv, L1_xattn_Wqf, L1_xattn_Wkf, L1_xattn_Wwin, L1_xattn_Wout, L2_xattn_Wq, L2_xattn_bq, L2_xattn_Wk, L2_xattn_bk, L2_xattn_Wv, L2_xattn_bv, L2_xattn_Wo, L2_xattn_bo, L2_xattn_gamma, L2_xattn_beta, L3_xattn_wq, L3_xattn_wk, L3_xattn_wv, L3_xattn_wo, L3_xattn_norm_w):
    import jax
    import jax.numpy as jnp

    def _L0_xattn_ref(x, context, w_qkv, b_qkv, w_ckv, b_ckv, g1, be1, g2, be2, gf, bf, w1, b1, w2, b2):
        import jax, jax.numpy as jnp
        import numpy as np
        B, T, S, D, H, F = (2, 512, 128, 256, 16, 1024)
        DH = D // H
        EPS = 1e-05

        def _ln(x, g, b):
            m = x.mean(-1, keepdims=True)
            v = ((x - m) ** 2).mean(-1, keepdims=True)
            return (x - m) * jax.lax.rsqrt(v + EPS) * g + b
        b, t, d = x.shape
        s = context.shape[1]
        h, dh = (H, d // H)
        qkv = (_ln(x, g1, be1) @ w_qkv + b_qkv).reshape(b, t, 3, h, dh)
        q, k_self, v_self = (qkv[:, :, 0], qkv[:, :, 1], qkv[:, :, 2])
        ckv = (context @ w_ckv + b_ckv).reshape(b, s, 2, h, dh)
        k_ctx, v_ctx = (ckv[:, :, 0], ckv[:, :, 1])
        k = jnp.concatenate([k_self, k_ctx], axis=1)
        v = jnp.concatenate([v_self, v_ctx], axis=1)
        scale = 1.0 / jnp.sqrt(jnp.float32(dh))
        scores = jnp.einsum('bthd,bshd->bhts', q, k) * scale
        i = jnp.arange(t)[:, None]
        j = jnp.arange(t + s)[None, :]
        mask = (j >= t) | (j <= i)
        scores = jnp.where(mask, scores, -jnp.inf)
        attn = jax.nn.softmax(scores, axis=-1)
        attn_out = jnp.einsum('bhts,bshd->bthd', attn, v).reshape(b, t, d)
        x = x + attn_out
        hdn = _ln(_ln(x, g2, be2), gf, bf) @ w1 + b1
        hdn = jax.nn.gelu(hdn, approximate=False)
        x = x + (hdn @ w2 + b2)
        return x

    def _L1_xattn_ref(x, encoder_out, norm_w, Wq, Wkv, Wqf, Wkf, Wwin, Wout):
        import math
        import jax, jax.numpy as jnp
        import numpy as np
        D_MODEL = 256
        N_HEADS = 16
        HEAD_DIM = D_MODEL // N_HEADS
        FEATURE_DIM = 16
        WINDOW = 64
        EPS_NORM = 1e-06
        EPS_DEN = 1e-06
        _TRIU_I, _TRIU_J = np.triu_indices(FEATURE_DIM)

        def taylor_feature_map(x):
            B, T, H, d = x.shape
            ones = jnp.ones((B, T, H, 1), dtype=x.dtype)
            outer = jnp.einsum('bthd,bthe->bthde', x, x)
            scale = jnp.full((d, d), 1.0 / math.sqrt(2), dtype=x.dtype)
            scale = scale.at[jnp.arange(d), jnp.arange(d)].set(0.5)
            outer = outer * scale
            quadratic = outer[..., _TRIU_I, _TRIU_J]
            return jnp.concatenate([ones, x, quadratic], axis=-1)

        def rmsnorm(x, w):
            var = jnp.mean(x * x, axis=-1, keepdims=True)
            return x * jax.lax.rsqrt(var + EPS_NORM) * w

        def _forward(x, encoder_out, norm_w, Wq, Wkv, Wqf, Wkf, Wwin, Wout):
            residual = x
            xn = rmsnorm(x, norm_w)
            B, T_dec, _ = xn.shape
            T_enc = encoder_out.shape[1]
            H, hd = (N_HEADS, HEAD_DIM)
            q = (xn @ Wq).reshape(B, T_dec, H, hd)
            kv = (encoder_out @ Wkv).reshape(B, T_enc, 2, H, hd)
            k, v = (kv[:, :, 0], kv[:, :, 1])
            q_phi = taylor_feature_map(q @ Wqf)
            k_phi = taylor_feature_map(k @ Wkf)
            kv_state = jnp.einsum('bshf,bshd->bhfd', k_phi, v)
            k_state = k_phi.sum(axis=1)
            linear_out = jnp.einsum('bthf,bhfd->bthd', q_phi, kv_state)
            normalizer = jnp.einsum('bthf,bhf->bth', q_phi, k_state)[..., None]
            linear_out = (linear_out / (normalizer + EPS_DEN)).reshape(B, T_dec, D_MODEL)
            kv_win = (xn @ Wwin).reshape(B, T_dec, 2, H, hd)
            k_win, v_win = (kv_win[:, :, 0], kv_win[:, :, 1])
            scores = jnp.einsum('bthd,bshd->bhts', q, k_win) * (1.0 / math.sqrt(hd))
            i = jnp.arange(T_dec)[:, None]
            j = jnp.arange(T_dec)[None, :]
            allowed = (j <= i) & (j >= i - WINDOW)
            scores = jnp.where(allowed, scores, jnp.finfo(scores.dtype).min)
            probs = jax.nn.softmax(scores, axis=-1)
            window_out = jnp.einsum('bhts,bshd->bthd', probs, v_win).reshape(B, T_dec, D_MODEL)
            combined = jnp.concatenate([linear_out, window_out], axis=-1)
            return residual + combined @ Wout
        return _forward(x, encoder_out, norm_w, Wq, Wkv, Wqf, Wkf, Wwin, Wout)

    def _L2_xattn_ref(queries, keys, values, attention_mask, attention_weights, Wq, bq, Wk, bk, Wv, bv, Wo, bo, gamma, beta):
        import jax, jax.numpy as jnp
        import numpy as np
        D_MODEL = 256
        N_HEADS = 16
        D_HEAD = D_MODEL // N_HEADS
        LN_EPS = 1e-05

        def _xavier(key, shape):
            lim = float(np.sqrt(6.0 / (shape[0] + shape[1])))
            return jax.random.uniform(key, shape, jnp.float32, -lim, lim)
        B, Nq, D = queries.shape
        h, d = (N_HEADS, D_HEAD)
        q = (queries @ Wq.T + bq).reshape(B, Nq, h, d).transpose(0, 2, 1, 3)
        k = (keys @ Wk.T + bk).reshape(B, -1, h, d).transpose(0, 2, 1, 3)
        v = (values @ Wv.T + bv).reshape(B, -1, h, d).transpose(0, 2, 1, 3)
        scores = jnp.einsum('bhqd,bhkd->bhqk', q, k) / jnp.sqrt(jnp.float32(d))
        scores = scores * attention_weights
        scores = jnp.where(attention_mask, -jnp.inf, scores)
        p_attn = jax.nn.softmax(scores, axis=-1)
        out = jnp.einsum('bhqk,bhkd->bhqd', p_attn, v)
        out = out.transpose(0, 2, 1, 3).reshape(B, Nq, D)
        out = out @ Wo.T + bo
        x = queries + out
        mu = jnp.mean(x, axis=-1, keepdims=True)
        var = jnp.mean(jnp.square(x - mu), axis=-1, keepdims=True)
        return (x - mu) * jax.lax.rsqrt(var + LN_EPS) * gamma + beta

    def _L3_xattn_ref(hidden_states, key_value_states, wq, wk, wv, wo, norm_w):
        import jax, jax.numpy as jnp
        import numpy as np
        B, Q, KV = (2, 512, 512)
        D_MODEL = 256
        N_HEADS = 16
        D_KV = 64
        EPS = 1e-06
        var = jnp.mean(jnp.square(hidden_states), axis=-1, keepdims=True)
        normed = hidden_states * jax.lax.rsqrt(var + EPS) * norm_w
        b, q_len, _ = hidden_states.shape
        kv_len = key_value_states.shape[1]

        def split_heads(x):
            return x.reshape(b, -1, N_HEADS, D_KV).transpose(0, 2, 1, 3)
        q = split_heads(normed @ wq)
        k = split_heads(key_value_states @ wk)
        v = split_heads(key_value_states @ wv)
        scores = jnp.einsum('bhqd,bhkd->bhqk', q, k)
        attn = jax.nn.softmax(scores.astype(jnp.float32), axis=-1).astype(scores.dtype)
        ctx = jnp.einsum('bhqk,bhkd->bhqd', attn, v)
        ctx = ctx.transpose(0, 2, 1, 3).reshape(b, q_len, N_HEADS * D_KV)
        attn_out = ctx @ wo
        return hidden_states + attn_out
    x = _L0_xattn_ref(x, ctx_1024, L0_xattn_w_qkv, L0_xattn_b_qkv, L0_xattn_w_ckv, L0_xattn_b_ckv, L0_xattn_g1, L0_xattn_be1, L0_xattn_g2, L0_xattn_be2, L0_xattn_gf, L0_xattn_bf, L0_xattn_w1, L0_xattn_b1, L0_xattn_w2, L0_xattn_b2)
    x = _L1_xattn_ref(x, ctx_1024, L1_xattn_norm_w, L1_xattn_Wq, L1_xattn_Wkv, L1_xattn_Wqf, L1_xattn_Wkf, L1_xattn_Wwin, L1_xattn_Wout)
    x = _L2_xattn_ref(x, ctx_1024, ctx_1024, mask_Bx16xSxS2_bk0, fside_Bx16xSxS2_0, L2_xattn_Wq, L2_xattn_bq, L2_xattn_Wk, L2_xattn_bk, L2_xattn_Wv, L2_xattn_bv, L2_xattn_Wo, L2_xattn_bo, L2_xattn_gamma, L2_xattn_beta)
    x = _L3_xattn_ref(x, ctx_1024, L3_xattn_wq, L3_xattn_wk, L3_xattn_wv, L3_xattn_wo, L3_xattn_norm_w)
    return x

_drawn_inputs = setup_inputs


def setup_inputs(seed=0):
    import zlib

    import numpy as np

    out = dict(_drawn_inputs(seed))
    spreads = {'L0_xattn_b_qkv': (0.0, 0.1),
     'L0_xattn_b_ckv': (0.0, 0.395),
     'L0_xattn_g1': (1.0, 0.6),
     'L0_xattn_be1': (0.0, 0.359),
     'L0_xattn_g2': (1.0, 0.6),
     'L0_xattn_be2': (0.0, 0.731),
     'L0_xattn_gf': (1.0, 0.6),
     'L0_xattn_bf': (0.0, 0.782),
     'L0_xattn_b1': (0.0, 0.1),
     'L0_xattn_b2': (0.0, 0.1),
     'L1_xattn_norm_w': (1.0, 0.6),
     'L2_xattn_bq': (0.0, 0.702),
     'L2_xattn_bk': (0.0, 0.8),
     'L2_xattn_bv': (0.0, 0.1),
     'L2_xattn_bo': (0.0, 0.1),
     'L2_xattn_gamma': (1.0, 0.2),
     'L2_xattn_beta': (0.0, 0.1),
     'L3_xattn_norm_w': (1.0, 0.6)}
    factors = {'L1_xattn_Wq': 8.0, 'L1_xattn_Wqf': 8.0, 'L1_xattn_Wkf': 8.0, 'L1_xattn_Wwin': 3.08}
    for name, (base, spread) in spreads.items():
        noise = np.random.default_rng([zlib.crc32(name.encode()), seed]).standard_normal(out[name].shape)
        drawn = base * np.exp(spread * noise) if base else spread * noise
        out[name] = jnp.asarray(drawn.astype(out[name].dtype))
    for name, factor in factors.items():
        out[name] = (out[name] * factor).astype(out[name].dtype)
    return out
```

```python
from contextlib import ExitStack

import concourse.bass as bass
from concourse import mybir

F32 = mybir.dt.float32
BF16 = mybir.dt.bfloat16
U8 = mybir.dt.uint8
ALU = mybir.AluOpType
ACT = mybir.ActivationFunctionType
AX = mybir.AxisListType

P = 128
B, T, D, H, S = 4, 1024, 256, 16, 77
NT, ND = T // P, D // P
DH = D // H
HS = H * S
FF = 1024
WINDOW = 64
MASKED = -1e30
UNUSED = 3e38

QH = 4
NQ = H // QH
KW = S + T
TERMS_Q = (0, 0, 0, 1, 1, 2)
TERMS_K = (0, 1, 2, 0, 1, 0)
KR = DH * len(TERMS_Q)
CH = 256
NCH = T // CH
BANK = 512


def causal_ring_jobs():
    jobs = []
    for i in range(NT):
        end = S + P * (i + 1)
        for slot, c0 in enumerate(range(0, end, BANK)):
            n = min(BANK, end - c0)
            m0 = max(c0, end - P)
            mask = (m0 - (end - P), m0 - c0, c0 + n - m0) if m0 < c0 + n else None
            jobs.append((1, n, i, slot, [(i, 0, c0, n, mask)]))
    return jobs


def window_ring_jobs():
    w = P + WINDOW
    jobs = [(1, P, 0, 0, [(0, 0, S, P, (WINDOW, 0, P))])]
    for i in range(1, NT, 2):
        tiles = [i, i + 1] if i + 1 < NT else [i]
        jobs.append((len(tiles), w, i, 0,
                     [(t, w * n, S + P * t - WINDOW, w, (0, w * n, w)) for n, t in enumerate(tiles)]))
    return jobs


def causal_steps(c):
    steps = [("exp", 0, 0, CH, None)]
    steps.append(("exp", 2 + 2 * c, P, P, (0, P, P)))
    steps += [("exp", 1 + j, 0, CH, None) for j in range(2 * c)]
    steps.append(("exp", 1 + 2 * c, 0, CH, (0, 0, P)))
    return steps


def window_steps(c):
    steps = [("square", 0, 0, CH, None), ("exp", 2 + 2 * c, 0, CH, (0, 0, CH))]
    if c:
        steps.append(("exp", 2 * c, 0, WINDOW, (2 * P, 0, WINDOW)))
    return steps + [("exp", 1 + 2 * c, 0, CH, (P, 0, CH))]


def attention_schedule(ring_jobs, steps_of):
    steps = [(c, n, step) for c in range(NCH) for n, step in enumerate(steps_of(c))]
    last = {c: max(k for k, s in enumerate(steps) if s[0] == c) for c in range(NCH)}
    order = []
    jobs = [(h, j) for h in range(QH) for j in ring_jobs]
    for q in range(-1, NQ):
        ahead = [("ring", q + 1, *job) for job in jobs] if q + 1 < NQ else []
        if q < 0:
            order += ahead + [("shift", 0)]
            continue
        lead = len(ahead) // 8
        order += ahead[:lead]
        ahead = ahead[lead:]
        span = len(steps) - 2
        for k, (c, n, step) in enumerate(steps):
            order.append(("scores", q, c, n, step))
            order += ahead[len(ahead) * min(k, span) // span:len(ahead) * min(k + 1, span) // span]
            if k:
                order.append(("values", q, *steps[k - 1]))
            if k >= 2 and steps[k - 2][0] != steps[k - 1][0]:
                order.append(("turn", q, steps[k - 2][0]))
        order.append(("values", q, *steps[-1]))
        if q + 1 < NQ:
            order.append(("shift", q + 1))
        order.append(("turn", q, NCH - 1))
    return order


def build(nc, a, out, upto=5, only=None):
    with ExitStack() as whole:
        sems = {}

        def sem(name):
            if name not in sems:
                sems[name] = whole.enter_context(nc.semaphore(name))
            return sems[name]

        def sb(stack, name, shape, dt=F32):
            return stack.enter_context(nc.sbuf_tensor(name, shape, dt))

        x = sb(whole, "x_tokens", [P, B, NT, D])
        ident = sb(whole, "ident", [P, P])
        identb = sb(whole, "identb", [P, P], BF16)
        mask_q = sb(whole, "mask_q", [P, P], BF16)
        mask_k = sb(whole, "mask_k", [P, P], BF16)
        win_q = sb(whole, "win_q", [P, P + WINDOW], BF16)
        win_k = sb(whole, "win_k", [P, P + CH], BF16)
        ctxT = sb(whole, "ctxT", [P, B, ND, S])
        banks = whole.enter_context(nc.psum_tensor("banks", [P, 8, BANK], F32))

        setup(nc, a, sem, x, ident, identb, mask_q, mask_k, win_q, win_k, ctxT)
        if only in (None, 1):
            attention_layer(nc, a, sem, sb, x, ident, identb, mask_q, mask_k, ctxT, banks, True)
        if upto >= 2 and only in (None, 2):
            mlp(nc, a, sem, sb, x, ident, banks)
        if upto >= 3 and only in (None, 3):
            attention_layer(nc, a, sem, sb, x, ident, identb, win_q, win_k, ctxT, banks, False)
        if upto >= 4 and only in (None, 4):
            context_attention(nc, a, sem, sb, x, ident, ctxT, banks, False)
        if upto >= 5 and only in (None, 5):
            context_attention(nc, a, sem, sb, x, ident, ctxT, banks, True)
        store(nc, sem, x, out)


def clear(nc, sems):
    numbers = [one.num for one in sems]
    nc.all_engine_barrier(sems_to_clear=range(min(numbers), max(numbers) + 1))


def setup(nc, a, sem, x, ident, identb, mask_q, mask_k, win_q, win_k, ctxT):
    loaded, filled, const_ready = sem("loaded"), sem("filled"), sem("const_ready")
    with nc.Block() as block:
        @block.sync
        def _(sp):
            for b in range(B):
                sp.dma_start(x[:, b], a["x"][b].rearrange("(i p) d -> p i d", p=P)).then_inc(loaded, 16)
            for b in range(B):
                sp.dma_start(ctxT[:, b], a["ctxT"][b].rearrange("(k p) s -> p k s", p=P)).then_inc(loaded, 16)
            sp.wait_ge(loaded, 2 * B * 16)

        @block.gpsimd
        def _(pool):
            pool.memset(ident[:], 0.0).then_inc(filled, 1)
            pool.memset(identb[:], 0.0).then_inc(filled, 1)
            for m in (mask_q, mask_k, win_q, win_k):
                pool.memset(m[:], 0.0).then_inc(filled, 1)
            pool.wait_ge(filled, 6)
            for m in (ident, identb):
                pool.affine_select(out=m[:], in_=m[:], compare_op=ALU.not_equal, fill=1.0, base=0,
                                   pattern=[[-1, P]], channel_multiplier=1).then_inc(const_ready, 1)
            pool.affine_select(out=mask_q[:], in_=mask_q[:], compare_op=ALU.is_ge, fill=MASKED, base=0,
                               pattern=[[-1, P]], channel_multiplier=1).then_inc(const_ready, 1)
            pool.affine_select(out=mask_k[:], in_=mask_k[:], compare_op=ALU.is_ge, fill=MASKED, base=0,
                               pattern=[[1, P]], channel_multiplier=-1).then_inc(const_ready, 1)
            pool.affine_select(out=win_q[:], in_=win_q[:], compare_op=ALU.is_ge, fill=MASKED, base=0,
                               pattern=[[1, P + WINDOW]], channel_multiplier=-1).then_inc(const_ready, 1)
            pool.wait_ge(const_ready, 5)
            pool.affine_select(out=win_q[:], in_=win_q[:], compare_op=ALU.is_ge, fill=MASKED, base=WINDOW,
                               pattern=[[-1, P + WINDOW]], channel_multiplier=1).then_inc(const_ready, 1)
            pool.affine_select(out=win_k[:], in_=win_k[:], compare_op=ALU.is_ge, fill=MASKED, base=-P,
                               pattern=[[1, P + CH]], channel_multiplier=-1).then_inc(const_ready, 1)
            pool.wait_ge(const_ready, 7)
            pool.affine_select(out=win_k[:], in_=win_k[:], compare_op=ALU.is_ge, fill=MASKED, base=WINDOW + P,
                               pattern=[[-1, P + CH]], channel_multiplier=1).then_inc(const_ready, 1)
    clear(nc, [loaded, filled, const_ready])


def store(nc, sem, x, out):
    stored = sem("stored")
    with nc.Block() as block:
        @block.sync
        def _(sp):
            for b in range(B):
                sp.dma_start(out[b].rearrange("(i p) d -> p i d", p=P), x[:, b]).then_inc(stored, 16)
            sp.wait_ge(stored, 16 * B)
    clear(nc, [stored])


def load_weight(eng, tile, src, done):
    eng.dma_start(tile[:], src.rearrange("(k p) n -> p k n", p=P)).then_inc(done, 16)


def load_column(eng, tile, src, done):
    eng.dma_start(tile[:], src.rearrange("(k p) -> p k", p=P), allow_slow_non_contiguous=True).then_inc(done, 16)


def load_row(eng, tile, src, done):
    eng.dma_start(tile[:], src.partition_broadcast(P)).then_inc(done, 16)


class Chain:

    def __init__(self, eng, sem):
        self.eng, self.sem, self.n = eng, sem, 0

    def __call__(self, ins):
        self.n += 1
        ins.then_inc(self.sem, 1)
        self.eng.wait_ge(self.sem, self.n)


def normalise(dve, sem, xin, xhat, st, mv, sd, chain, normed, eps, centred, time=0, ready=None):
    for i in range(NT):
        if ready:
            dve.wait_ge(ready, i + 1)
        dve.bn_stats(st[:, i, :], xin(i)).then_inc(sem("stats"), 1)
    for i in range(NT):
        dve.wait_ge(sem("stats"), time * NT + i + 1)
        dve.bn_aggr(mv[:, i, :], st[:, i, :]).then_inc(sem("moments"), 1)
    dve.wait_ge(sem("moments"), (time + 1) * NT)
    if centred:
        dve.tensor_scalar(sd[:, 0, :], mv[:, :, 1], eps, None, ALU.add).then_inc(sem("spread"), 1)
    else:
        chain(dve.tensor_tensor(sd[:, 1, :], mv[:, :, 0], mv[:, :, 0], ALU.mult))
        chain(dve.tensor_tensor(sd[:, 2, :], sd[:, 1, :], mv[:, :, 1], ALU.add))
        dve.tensor_scalar(sd[:, 0, :], sd[:, 2, :], eps, None, ALU.add).then_inc(sem("spread"), 1)
    dve.wait_ge(sem("root"), time + 1)
    chain(dve.reciprocal(sd[:, 2, :], sd[:, 1, :]))
    for i in range(NT):
        if centred:
            ins = dve.tensor_scalar(xhat(i), xin(i), mv[:, i, 0:1], sd[:, 2, i:i + 1], ALU.subtract, ALU.mult)
        else:
            ins = dve.tensor_scalar(xhat(i), xin(i), sd[:, 2, i:i + 1], None, ALU.mult)
        ins.then_inc(normed, 1)


def root_of(act, sem, sd, time=0):
    act.wait_ge(sem("spread"), time + 1)
    act.activation(sd[:, 1, :], sd[:, 0, :], ACT.Sqrt).then_inc(sem("root"), 1)


def turn_tiles(pe, bank, xh, half, k, ident):
    for n in range(4):
        ins = pe.transpose(bank[:, n * P:(n + 1) * P], xh[:, 4 * half + n, k * P:(k + 1) * P], ident[:])
    return ins


class Ring:

    def __init__(self, jobs, nbanks, done):
        self.jobs, self.nbanks, self.done = jobs, nbanks, done
        self.at = {job[:-1]: n for n, job in enumerate(jobs)}

    def emptied(self, n):
        who = self.jobs[n][-1]
        return self.done[who], sum(j[-1] == who for j in self.jobs[:n + 1])

    def wait_free(self, eng, n):
        if n >= self.nbanks:
            eng.wait_ge(*self.emptied(n - self.nbanks))

    def wait_emptied(self, eng, name):
        eng.wait_ge(*self.emptied(self.at[name]))


def attention_layer(nc, a, sem, sb, x, ident, identb, mq, mk, ctxT, banks, first):
    eps = 1e-5 if first else 1e-6
    ring_jobs = causal_ring_jobs() if first else window_ring_jobs()
    steps_of = causal_steps if first else window_steps
    order = attention_schedule(ring_jobs, steps_of)
    per_quad = sum(len(steps_of(c)) for c in range(NCH))
    on_ring = [token for token in order if token[0] in ("ring", "shift")]
    shift_at = [on_ring.index(("shift", q)) for q in range(NQ)]
    slots = 3 if first else 1
    zk = nc.dram_tensor(f"zk{int(first)}", [3, D, KW], BF16, kind="Internal").ap()
    zq = nc.dram_tensor(f"zq{int(first)}", [3, D, T], BF16, kind="Internal").ap()
    units = [(0, 0), (0, 1), (1, 0), (1, 1)]
    jobs = [("turn", 0, 0, "v"), ("turn", 0, 1, "s"), ("turn", 1, 0, "v"), ("turn", 1, 1, "s")]
    if not first:
        jobs += [("ke", 0, "s"), ("ke", 1, "v")]
    jobs += [("kc", 0, "s"), ("kc", 1, "s"), ("vc", "v")]
    jobs += [("qk", u, half, "s") for u in range(4) for half in range(2)]
    jobs += [("v", i, "v") for i in range(NT)]
    done = {"v": sem("moved_v"), "s": sem("moved_s")}
    ring = Ring(jobs, 4, done)
    with ExitStack() as own:
        n_ = lambda s: f"{s}_{int(first)}"
        w = sb(own, n_("w"), [P, ND, 3 * D])
        wc = sb(own, n_("wc"), [P, ND, 2 * D])
        xh = sb(own, n_("xh"), [P, NT, D])
        xnT = sb(own, n_("xnT"), [P, ND, T])
        whole = sb(own, n_("whole"), [P, 4, KW])
        parts = sb(own, n_("parts"), [P, 4, 3, KW], BF16)
        qs = sb(own, n_("qs"), [KR + 1, 3, QH, T], BF16)
        ks = sb(own, n_("ks"), [KR + 1, 3, QH, KW], BF16)
        v1 = sb(own, n_("v1"), [P, 1 + NT, H, 32])
        probs = sb(own, n_("probs"), [P, 3, QH * CH])
        oT = sb(own, n_("oT"), [P, 2, 2 * CH])
        nmx = sb(own, n_("nmx"), [P, 2, QH * NT, slots])
        nmb = sb(own, n_("nmb"), [P, 2, QH * NT], BF16)
        nmT = sb(own, n_("nmT"), [QH * NT, 2, P], BF16)
        st = sb(own, n_("st"), [P, NT, 6])
        mv = sb(own, n_("mv"), [P, NT, 2])
        sd = sb(own, n_("sd"), [P, 3, NT])
        den = sb(own, n_("den"), [P, 2, 2, QH])
        rcp = sb(own, n_("rcp"), [P, 2, 2, QH])
        g = sb(own, n_("g"), [P, ND])
        ctxb = sb(own, n_("ctxb"), [P, ND, S])
        wm = D if first else 2 * D
        mixed = whole[:].rearrange("p u c -> p (u c)")[:, 0:NT * wm].rearrange("p (i d) -> p i d", d=wm)
        if first:
            be = sb(own, "be", [P, ND])
            bcol = sb(own, "bcol", [P, 4])
            bcc = sb(own, "bcc", [P, ND])
            vrow, vcrow = sb(own, "vrow", [P, D]), sb(own, "vcrow", [P, D])
        else:
            wout = sb(own, "wout", [P, 4, D])
            wf = sb(own, "wf", [DH, 2, DH])
            both = sb(own, "both", [P, P])
            ke = sb(own, "ke", [P, ND, S])
            blockd = sb(own, "blockd", [P, P])
            mixedT = sb(own, "mixedT", [P, 2, 4, P])
        loaded, ready = sem("loaded"), sem("const_ready")
        folded, tiled = sem("folded"), sem("tiled")
        with nc.Block() as block:
            nload = 0

            @block.sync
            def _(sp):
                nonlocal nload
                if first:
                    load_weight(sp, w, a["L0_xattn_w_qkv"], loaded)
                    load_weight(sp, wc, a["L0_xattn_w_ckv"], loaded)
                    load_column(sp, g, a["L0_xattn_g1"], loaded)
                    load_column(sp, be, a["L0_xattn_be1"], loaded)
                    load_column(sp, bcol, a["L0_xattn_b_qkv"][0:2 * D], loaded)
                    load_column(sp, bcc, a["L0_xattn_b_ckv"][0:D], loaded)
                    load_row(sp, vrow, a["L0_xattn_b_qkv"][2 * D:3 * D], loaded)
                    load_row(sp, vcrow, a["L0_xattn_b_ckv"][D:2 * D], loaded)
                    nload = 8
                else:
                    load_weight(sp, w[:, :, 0:D], a["L1_xattn_Wq"], loaded)
                    load_weight(sp, w[:, :, D:3 * D], a["L1_xattn_Wwin"], loaded)
                    load_weight(sp, wc, a["L1_xattn_Wkv"], loaded)
                    load_column(sp, g, a["L1_xattn_norm_w"], loaded)
                    load_weight(sp, wout, a["L1_xattn_Wout"], loaded)
                    sp.dma_start(wf[:, 0, :], a["L1_xattn_Wkf"]).then_inc(loaded, 16)
                    sp.dma_start(wf[:, 1, :], a["L1_xattn_Wqf"]).then_inc(loaded, 16)
                    nload = 7
                sp.wait_ge(loaded, 16 * nload)

            @block.gpsimd
            def _(pool):
                pool.memset(v1[:], 0.0).then_inc(ready, 1)
                pool.wait_ge(ready, 1)
                pool.memset(v1[:, :, :, DH:DH + 1], 1.0).then_inc(ready, 1)
                if not first:
                    pool.memset(blockd[:], 1.0).then_inc(folded, 1)
                    pool.wait_ge(folded, 1)
                    v = blockd[:].rearrange("p (h d) -> p h d", d=DH)
                    pool.affine_select(out=v, in_=v, compare_op=ALU.is_ge, fill=0.0, base=0,
                                       pattern=[[-DH, P // DH], [0, DH]], channel_multiplier=1).then_inc(folded, 1)
                    pool.wait_ge(folded, 2)
                    pool.affine_select(out=v, in_=v, compare_op=ALU.is_ge, fill=0.0, base=DH - 1,
                                       pattern=[[DH, P // DH], [0, DH]], channel_multiplier=-1).then_inc(folded, 1)

            if not first:
                @block.tensor
                def _(pe):
                    pe.wait_ge(tiled, 1)
                    pe.matmul(banks[:, 0, 0:P], whole[0:DH, 0, 0:P], whole[0:DH, 0, P:2 * P],
                              start=True, stop=True).then_inc(sem("both_ready"), 1)

            @block.vector
            def _(dve):
                dve.memset(ks[KR:KR + 1], 1.0).then_inc(sem("filled"), 1)
                dve.memset(nmx[:], UNUSED).then_inc(sem("filled"), 1)
                if not first:
                    dve.wait_ge(loaded, 16 * nload)
                    n = P // DH
                    src = wf[:].unsqueeze(2).broadcast_to([DH, 2, n, DH])
                    dve.tensor_copy(whole[0:DH, 0, 0:2 * P].rearrange("p (a n d) -> p a n d", a=2, n=n),
                                    src).then_inc(tiled, 1)
                    dve.wait_ge(sem("both_ready"), 1)
                    dve.wait_ge(folded, 3)
                    dve.tensor_tensor(both[:], banks[:, 0, 0:P], blockd[:], ALU.mult).then_inc(tiled, 1)
        clear(nc, [loaded, ready, folded, tiled, sem("both_ready"), sem("filled")])

        with nc.Fori(0, B) as b:
            with nc.Block() as block:
                proj_ready = sem("proj_ready")
                normed = sem("normed")
                scores_ready, probs_ready, probs_used = sem("scores_ready"), sem("probs_ready"), sem("probs_used")
                ring_ready, ring_freed = sem("ring_ready"), sem("ring_freed")
                out_copied, turned, turn_freed = sem("out_copied"), sem("turned"), sem("turn_freed")
                high, rest, middle, low = sem("high"), sem("rest"), sem("middle"), sem("low")
                max_ready, shift_loaded = sem("max_ready"), sem("shift_loaded")
                written = sem("written")
                stacked = [sem(f"stacked{n}") for n in range(3)]
                added = sem("added")
                used = [proj_ready, normed, scores_ready, probs_ready, probs_used, ring_ready, ring_freed,
                        out_copied, turned, turn_freed, high, rest, middle, low, max_ready,
                        shift_loaded, written, *stacked, added, done["v"], done["s"],
                        sem("stats"), sem("moments"), sem("spread"), sem("root"), sem("chain"),
                        sem("mixT_ready"), sem("mixT_copied"), sem("outs_ready")]

                @block.sync
                def _(sp):
                    for u, (is_q, m) in enumerate(units):
                        for part, cut in enumerate((high, middle, low)):
                            sp.wait_ge(cut, u + 1)
                            z = zq if is_q else zk
                            sp.dma_start(z[part, m * P:(m + 1) * P, :],
                                         parts[:, u, part, 0:T if is_q else KW]).then_inc(written, 16)
                    sp.wait_ge(written, 16 * 12)

                    def stack(q):
                        rows = slice(q * QH * DH, (q + 1) * QH * DH)
                        for dst, z, terms in ((qs, zq, TERMS_Q), (ks, zk, TERMS_K)):
                            for j, part in enumerate(terms):
                                sp.dma_start(dst[j * DH:(j + 1) * DH, q % 3],
                                             z[part, rows, :].rearrange("(h d) t -> d h t", d=DH)).then_inc(stacked[q % 3], 16)

                    for q in range(3):
                        stack(q)
                    for q in range(NQ):
                        sp.wait_ge(ring_freed, shift_at[q] + 1)
                        sp.dma_start(qs[KR:KR + 1, q % 3].rearrange("o h t -> o (h t)"),
                                     nmT[:, q % 2, :]).then_inc(shift_loaded, 16)
                        if 1 <= q < NQ - 2:
                            sp.wait_ge(scores_ready, q * per_quad)
                            stack(q + 2)
                    sp.wait_ge(shift_loaded, 16 * NQ)

                @block.gpsimd
                def _(pool):
                    def cut(u, part, before, after):
                        n = T if units[u][0] else KW
                        out = whole[:, u, 0:n] if part == 0 else parts[:, u, 2, 0:n]
                        pool.wait_ge(before, u + 1)
                        pool.tensor_tensor(out, whole[:, u, 0:n], parts[:, u, part, 0:n], ALU.subtract).then_inc(after, 1)

                    for u in range(5):
                        if u < 4:
                            cut(u, 0, high, rest)
                        if u >= 1:
                            cut(u - 1, 1, middle, low)
                    if first:
                        for q in range(NQ):
                            pool.wait_ge(turn_freed, NCH * (q + 1))
                            cols = slice(q * QH * DH, (q + 1) * QH * DH)
                            pool.tensor_tensor(x[:, b, :, cols], x[:, b, :, cols], mixed[:, :, cols], ALU.add).then_inc(added, 1)

                @block.tensor
                def _(pe):
                    def bank(n):
                        pe_bank = banks[:, n % 4, :]
                        ring.wait_free(pe, n)
                        return pe_bank

                    for n, job in enumerate(jobs):
                        bk = bank(n)
                        kind = job[0]
                        if kind == "turn":
                            _, half, k, _ = job
                            pe.wait_ge(normed, 4 * (half + 1))
                            ins = turn_tiles(pe, bk, xh, half, k, ident)
                        elif kind in ("ke", "kc") and (kind == "ke" or first):
                            for k in range(ND):
                                ins = pe.matmul(bk[:, 0:S], wc[:, k, job[1] * P:(job[1] + 1) * P], ctxb[:, k, :],
                                                start=k == 0, stop=k == ND - 1)
                        elif kind == "kc":
                            ring.wait_emptied(pe, ("ke", job[1]))
                            ins = pe.matmul(bk[:, 0:S], both[:], ke[:, job[1], :], start=True, stop=True)
                        elif kind == "vc":
                            for k in range(ND):
                                ins = pe.matmul(bk[0:S, 0:D], ctxb[:, k, :], wc[:, k, D:2 * D],
                                                start=k == 0, stop=k == ND - 1)
                        elif kind == "qk":
                            _, u, half, _ = job
                            for k in range(ND):
                                ring.wait_emptied(pe, ("turn", half, k))
                            is_q, m = units[u]
                            c0 = (0 if is_q else D) + m * P
                            for k in range(ND):
                                ins = pe.matmul(bk[:, :], w[:, k, c0:c0 + P], xnT[:, k, half * BANK:(half + 1) * BANK],
                                                start=k == 0, stop=k == ND - 1)
                        elif kind == "v":
                            i = job[1]
                            for k in range(ND):
                                ins = pe.matmul(bk[:, 0:D], xnT[:, k, i * P:(i + 1) * P], w[:, k, 2 * D:3 * D],
                                                start=k == 0, stop=k == ND - 1)
                        ins.then_inc(proj_ready, 1)
                    for n in range(len(jobs) - 4, len(jobs)):
                        pe.wait_ge(*ring.emptied(n))

                    rings = steps = mixed_steps = 0
                    for what, q, *args in order:
                        if what == "ring":
                            h, (tiles, n, i0, slot, pieces) = args
                            if (h, pieces) == (0, ring_jobs[0][4]):
                                pe.wait_ge(stacked[q % 3], 16 * 12 * (q // 3 + 1))
                            if rings >= 2:
                                pe.wait_ge(ring_freed, rings - 1)
                            bk = banks[:, rings % 2, :]
                            for t, c, key, m, mask in pieces:
                                if mask:
                                    m0, at, mn = mask
                                    pe.matmul(bk[:, at:at + mn], identb[:], mq[:, m0:m0 + mn], start=True,
                                              stop=False, skip_group_check=True)
                                ins = pe.matmul(bk[:, c:c + m], qs[0:KR, q % 3, h, t * P:(t + 1) * P],
                                                ks[0:KR, q % 3, h, key:key + m], start=mask is None, stop=True,
                                                skip_group_check=True)
                            ins.then_inc(ring_ready, 1)
                            rings += 1
                        elif what == "shift":
                            pe.wait_ge(ring_freed, rings - 1)
                            pe.wait_ge(max_ready, q + 1)
                            pe.transpose(banks[0:QH * NT, rings % 2, 0:P // 2].bitcast(BF16), nmb[:, q % 2, :],
                                         identb[:]).then_inc(ring_ready, 1)
                            rings += 1
                        elif what == "scores":
                            c, s, (func, blk, c0, n, mask) = args
                            if c == 0 and s == 0:
                                pe.wait_ge(shift_loaded, 16 * (q + 1))
                            if steps >= 2:
                                pe.wait_ge(probs_ready, steps - 1)
                            r = 2 + 2 * (steps % 2)
                            rows = S if blk == 0 else P
                            key = 0 if blk == 0 else S + P * (blk - 1)
                            kr = KR + (func == "exp")
                            for h in range(QH):
                                bk = banks[:, r + h // 2, h % 2 * CH:(h % 2 + 1) * CH]
                                if mask:
                                    m0, at, mn = mask
                                    pe.matmul(bk[:, at:at + mn], identb[:], mk[:, m0:m0 + mn], start=True, stop=False,
                                              skip_group_check=True)
                                ins = pe.matmul(bk[0:rows, c0:c0 + n], ks[0:kr, q % 3, h, key:key + rows],
                                                qs[0:kr, q % 3, h, c * CH + c0:c * CH + c0 + n],
                                                start=mask is None, stop=True, skip_group_check=True)
                            ins.then_inc(scores_ready, 1)
                            steps += 1
                        elif what == "values":
                            c, s, (func, blk, c0, n, mask) = args
                            k = mixed_steps
                            if s == 0 and (q or c):
                                pe.wait_ge(out_copied, q * NCH + c)
                            pe.wait_ge(probs_ready, k + 1)
                            rows = S if blk == 0 else P
                            o0 = CH if func == "square" else 0
                            lin = func == "square"
                            firsts = 0 if first else 1
                            for h in range(QH):
                                ins = pe.matmul(banks[32 * h:32 * h + 32, 6, o0 + c0:o0 + c0 + n],
                                                v1[0:rows, blk, QH * q + h, :],
                                                probs[0:rows, k % 3, h * CH + c0:h * CH + c0 + n],
                                                start=lin or s == firsts, stop=lin or s == len(steps_of(c)) - 1)
                            ins.then_inc(probs_used, 1)
                            mixed_steps += 1
                        elif what == "turn":
                            c = args[0]
                            k = q * NCH + c
                            pe.wait_ge(out_copied, k + 1)
                            if k:
                                pe.wait_ge(turn_freed, k)
                            for n in range(2 if first else 4):
                                ins = pe.transpose(banks[:, 7, n * P:(n + 1) * P], oT[:, k % 2, n * P:(n + 1) * P], ident[:])
                            ins.then_inc(turned, 1)
                    if not first:
                        for i in range(NT + 1):
                            if i < NT:
                                if i == 0:
                                    pe.wait_ge(turn_freed, NCH * NQ)
                                if i >= 2:
                                    pe.wait_ge(sem("mixT_copied"), i - 1)
                                for k in range(4):
                                    ins = pe.transpose(banks[:, i % 2, k * P:(k + 1) * P], mixed[:, i, k * P:(k + 1) * P], ident[:])
                                ins.then_inc(sem("mixT_ready"), 1)
                            if i >= 1:
                                j = i - 1
                                pe.wait_ge(sem("mixT_copied"), j + 1)
                                if j >= 2:
                                    pe.wait_ge(added, j - 1)
                                for k in range(4):
                                    ins = pe.matmul(banks[:, 2 + j % 2, 0:D], mixedT[:, j % 2, k, :], wout[:, k, :],
                                                    start=k == 0, stop=k == 3)
                                ins.then_inc(sem("outs_ready"), 1)

                @block.scalar
                def _(act):
                    root_of(act, sem, sd)
                    for n, job in enumerate(jobs):
                        if job[-1] != "s":
                            continue
                        act.wait_ge(proj_ready, n + 1)
                        bk = banks[:, n % 4, :]
                        if job[0] == "turn":
                            _, half, k, _ = job
                            dst = xnT[:, k, half * BANK:(half + 1) * BANK]
                            if first:
                                ins = act.activation(dst, bk, ACT.Identity, scale=g[:, k:k + 1], bias=be[:, k:k + 1])
                            else:
                                ins = act.activation(dst, bk, ACT.Copy, scale=g[:, k:k + 1])
                        elif job[0] == "ke":
                            ins = act.activation(ke[:, job[1], :], bk[:, 0:S], ACT.Copy)
                        elif job[0] == "kc":
                            dst = whole[:, job[1], 0:S]
                            if first:
                                ins = act.activation(dst, bk[:, 0:S], ACT.Identity, bias=bcc[:, job[1]:job[1] + 1])
                            else:
                                ins = act.activation(dst, bk[:, 0:S], ACT.Copy)
                        else:
                            _, u, half, _ = job
                            is_q, m = units[u]
                            o = (0 if is_q else S) + half * BANK
                            dst = whole[:, u, o:o + BANK]
                            if first:
                                col = 2 * (1 - is_q) + m
                                ins = act.activation(dst, bk, ACT.Identity, bias=bcol[:, col:col + 1])
                            else:
                                ins = act.activation(dst, bk, ACT.Copy)
                        ins.then_inc(done["s"], 1)
                    steps = 0
                    for what, q, *args in order:
                        if what == "scores":
                            c, s, (func, blk, c0, n, mask) = args
                            act.wait_ge(scores_ready, steps + 1)
                            if steps >= 3:
                                act.wait_ge(probs_used, steps - 2)
                            rows = S if blk == 0 else P
                            r = 2 + 2 * (steps % 2)
                            src = banks[0:rows, r:r + 2, :].rearrange("p a (g n) -> p (a g) n", g=2)[:, :, c0:c0 + n]
                            dst = probs[0:rows, steps % 3, :].rearrange("p (h n) -> p h n", h=QH)[:, :, c0:c0 + n]
                            if func == "exp":
                                ins = act.activation(dst, src, ACT.Exp, scale=DH ** -0.5)
                            else:
                                ins = act.activation(dst, src, ACT.Square, scale=0.5, bias=1.0)
                            ins.then_inc(probs_ready, 1)
                            steps += 1
                        elif what == "values" and args[1] == len(steps_of(args[0])) - 1:
                            k = q * NCH + args[0]
                            act.wait_ge(probs_used, q * per_quad + sum(len(steps_of(c)) for c in range(args[0] + 1)))
                            if k >= 2:
                                act.wait_ge(turned, k - 1)
                            wd = CH if first else 2 * CH
                            act.activation(oT[:, k % 2, 0:wd], banks[:, 6, 0:wd], ACT.Copy).then_inc(out_copied, 1)
                    if not first:
                        for i in range(NT):
                            act.wait_ge(sem("mixT_ready"), i + 1)
                            if i >= 2:
                                act.wait_ge(sem("outs_ready"), i - 1)
                            act.activation(mixedT[:, i % 2].rearrange("p k c -> p (k c)"), banks[:, i % 2, :],
                                           ACT.Copy).then_inc(sem("mixT_copied"), 1)

                @block.vector
                def _(dve):
                    chain = Chain(dve, sem("chain"))
                    chain(dve.tensor_copy(ctxb[:], ctxT[:, b]))
                    normalise(dve, sem, lambda i: x[:, b, i, :], lambda i: xh[:, i, :], st, mv, sd, chain, normed,
                              eps, first)

                    def cut_high(u):
                        n = T if units[u][0] else KW
                        for half in range(2):
                            ring.wait_emptied(dve, ("qk", u, half))
                        dve.tensor_copy(parts[:, u, 0, 0:n], whole[:, u, 0:n]).then_inc(high, 1)

                    def cut_middle(u):
                        n = T if units[u][0] else KW
                        dve.wait_ge(rest, u + 1)
                        dve.tensor_copy(parts[:, u, 1, 0:n], whole[:, u, 0:n]).then_inc(middle, 1)

                    for n, job in enumerate(jobs):
                        if job[-1] != "v":
                            continue
                        if job == ("v", 0, "v"):
                            for u in range(5):
                                if u < 4:
                                    cut_high(u)
                                if u >= 1:
                                    cut_middle(u - 1)
                        dve.wait_ge(proj_ready, n + 1)
                        bk = banks[:, n % 4, :]
                        if job[0] == "turn":
                            _, half, k, _ = job
                            dst = xnT[:, k, half * BANK:(half + 1) * BANK]
                            if first:
                                ins = dve.tensor_scalar(dst, bk, g[:, k:k + 1], be[:, k:k + 1], ALU.mult, ALU.add)
                            else:
                                ins = dve.tensor_scalar(dst, bk, g[:, k:k + 1], None, ALU.mult)
                        elif job[0] == "ke":
                            ins = dve.tensor_copy(ke[:, job[1], :], bk[:, 0:S])
                        else:
                            rows, blk = (S, 0) if job[0] == "vc" else (P, 1 + job[1])
                            dst = v1[0:rows, blk, :, 0:DH]
                            src = bk[0:rows, 0:D].rearrange("p (h d) -> p h d", d=DH)
                            if first:
                                row = (vcrow if job[0] == "vc" else vrow)[0:rows, :].rearrange("p (h d) -> p h d", d=DH)
                                ins = dve.tensor_tensor(dst, src, row, ALU.add)
                            else:
                                ins = dve.tensor_copy(dst, src)
                        ins.then_inc(done["v"], 1)

                    rings = turns = 0
                    for what, q, *args in order:
                        if what == "ring":
                            h, (tiles, n, i0, slot, pieces) = args
                            dve.wait_ge(ring_ready, rings + 1)
                            dst = nmx[:, q % 2, h * NT + i0:h * NT + i0 + tiles, slot]
                            src = banks[:, rings % 2, 0:tiles * n].rearrange("p (t n) -> p t n", t=tiles)
                            dve.tensor_reduce(dst, src, AX.X, ALU.max, negate=True).then_inc(ring_freed, 1)
                            rings += 1
                            if h == QH - 1 and pieces == ring_jobs[-1][4]:
                                dve.wait_ge(ring_freed, rings)
                                dve.tensor_reduce(nmb[:, q % 2, :], nmx[:, q % 2], AX.X, ALU.min).then_inc(max_ready, 1)
                        elif what == "shift":
                            dve.wait_ge(ring_ready, rings + 1)
                            if q >= 2:
                                dve.wait_ge(shift_loaded, 16 * (q - 1))
                            dve.tensor_copy(nmT[:, q % 2, :], banks[0:QH * NT, rings % 2, 0:P // 2].bitcast(BF16))\
                               .then_inc(ring_freed, 1)
                            rings += 1
                        elif what == "turn":
                            c = args[0]
                            k = q * NCH + c
                            dve.wait_ge(turned, k + 1)
                            nt = 1 if first else 2
                            tv = banks[:, 7, 0:nt * 2 * P].rearrange("p (w i h d) -> p w i h d", w=nt, i=2, h=QH)
                            for wlin in range(nt):
                                s_ = tv[:, wlin, :, :, DH]
                                if wlin:
                                    chain(dve.tensor_scalar(den[:, k % 2], s_, 1e-6, None, ALU.add))
                                    s_ = den[:, k % 2]
                                chain(dve.reciprocal(rcp[:, wlin], s_))
                                cols = slice((D if not first and not wlin else 0) + q * QH * DH,
                                             (D if not first and not wlin else 0) + (q + 1) * QH * DH)
                                dst = mixed[:, 2 * c:2 * c + 2, cols].rearrange("p i (h d) -> p i h d", d=DH)
                                ins = dve.tensor_tensor(dst, tv[:, wlin, :, :, 0:DH],
                                                        rcp[:, wlin].unsqueeze(3).broadcast_to([P, 2, QH, DH]), ALU.mult)
                                if wlin < nt - 1:
                                    chain(ins)
                            ins.then_inc(turn_freed, 1)
                    if not first:
                        for j in range(NT):
                            dve.wait_ge(sem("outs_ready"), j + 1)
                            dve.tensor_tensor(x[:, b, j, :], banks[:, 2 + j % 2, 0:D], x[:, b, j, :], ALU.add)\
                               .then_inc(added, 1)
            clear(nc, used)


def mlp(nc, a, sem, sb, x, ident, banks):
    nf = FF // P
    jobs = [("turn", half, k, "sv"[k]) for half in range(2) for k in range(ND)]
    jobs += [("up", f, half, "s") for half in range(2) for f in range(nf)]
    jobs += [("down", i, "v") for i in range(NT)]
    done = {"v": sem("moved_v"), "s": sem("moved_s")}
    ring = Ring(jobs, 8, done)
    with ExitStack() as own:
        w1 = sb(own, "w1", [P, ND, FF])
        w2 = sb(own, "w2", [P, nf, D])
        g2, be2, b2 = (sb(own, n, [P, D]) for n in ("g2", "be2", "b2"))
        gf, bf, b1 = sb(own, "gf", [P, ND]), sb(own, "bf", [P, ND]), sb(own, "b1", [P, nf])
        xh = sb(own, "xh_mlp", [P, NT, D])
        xnT = sb(own, "xnT_mlp", [P, ND, T])
        hT = sb(own, "hT", [P, nf, T])
        st, mv, sd = sb(own, "st_mlp", [P, NT, 6]), sb(own, "mv_mlp", [P, NT, 2]), sb(own, "sd_mlp", [P, 3, NT])
        loaded = sem("loaded")
        with nc.Block() as block:
            @block.sync
            def _(sp):
                load_weight(sp, w1, a["L0_xattn_w1"], loaded)
                load_weight(sp, w2, a["L0_xattn_w2"], loaded)
                for tile, name in ((gf, "gf"), (bf, "bf"), (b1, "b1")):
                    load_column(sp, tile, a["L0_xattn_" + name], loaded)
                for tile, name in ((g2, "g2"), (be2, "be2"), (b2, "b2")):
                    load_row(sp, tile, a["L0_xattn_" + name], loaded)
                sp.wait_ge(loaded, 16 * 8)
        clear(nc, [loaded])
        with nc.Fori(0, B) as b:
            with nc.Block() as block:
                proj_ready, normed, scaled, shifted, added = (
                    sem(n) for n in ("proj_ready", "normed", "scaled", "shifted", "added"))
                used = [proj_ready, normed, scaled, shifted, added, done["v"], done["s"],
                        sem("stats"), sem("moments"), sem("spread"), sem("root"), sem("chain")]

                @block.gpsimd
                def _(pool):
                    for i in range(NT):
                        pool.wait_ge(normed, i + 1)
                        pool.tensor_tensor(xh[:, i, :], xh[:, i, :], g2[:], ALU.mult).then_inc(scaled, 1)
                        pool.wait_ge(scaled, i + 1)
                        pool.tensor_tensor(xh[:, i, :], xh[:, i, :], be2[:], ALU.add).then_inc(shifted, 1)
                    for i in range(NT):
                        pool.tensor_tensor(x[:, b, i, :], x[:, b, i, :], b2[:], ALU.add).then_inc(added, 1)

                @block.tensor
                def _(pe):
                    for n, job in enumerate(jobs):
                        ring.wait_free(pe, n)
                        bk = banks[:, n % 8, :]
                        if job[0] == "turn":
                            _, half, k, _ = job
                            pe.wait_ge(normed, NT + 4 * (half + 1))
                            ins = turn_tiles(pe, bk, xh, half, k, ident)
                        elif job[0] == "up":
                            _, f, half, _ = job
                            for k in range(ND):
                                ring.wait_emptied(pe, ("turn", half, k))
                            for k in range(ND):
                                ins = pe.matmul(bk, w1[:, k, f * P:(f + 1) * P], xnT[:, k, half * BANK:(half + 1) * BANK],
                                                start=k == 0, stop=k == ND - 1)
                        else:
                            i = job[1]
                            ring.wait_emptied(pe, ("up", nf - 1, i // 4))
                            for f in range(nf):
                                ins = pe.matmul(bk[:, 0:D], hT[:, f, i * P:(i + 1) * P], w2[:, f, :],
                                                start=f == 0, stop=f == nf - 1)
                        ins.then_inc(proj_ready, 1)

                @block.scalar
                def _(act):
                    root_of(act, sem, sd, 0)
                    root_of(act, sem, sd, 1)
                    for n, job in enumerate(jobs):
                        if job[-1] != "s":
                            continue
                        act.wait_ge(proj_ready, n + 1)
                        bk = banks[:, n % 8, :]
                        if job[0] == "turn":
                            _, half, k, _ = job
                            ins = act.activation(xnT[:, k, half * BANK:(half + 1) * BANK], bk, ACT.Identity,
                                                 scale=gf[:, k:k + 1], bias=bf[:, k:k + 1])
                        else:
                            _, f, half, _ = job
                            ins = act.activation(hT[:, f, half * BANK:(half + 1) * BANK], bk, ACT.Gelu,
                                                 bias=b1[:, f:f + 1])
                        ins.then_inc(done["s"], 1)

                @block.vector
                def _(dve):
                    chain = Chain(dve, sem("chain"))
                    normalise(dve, sem, lambda i: x[:, b, i, :], lambda i: xh[:, i, :], st, mv, sd, chain, normed,
                              1e-5, True, 0)
                    normalise(dve, sem, lambda i: xh[:, i, :], lambda i: xh[:, i, :], st, mv, sd, chain, normed,
                              1e-5, True, 1, shifted)
                    for n, job in enumerate(jobs):
                        if job[-1] != "v":
                            continue
                        dve.wait_ge(proj_ready, n + 1)
                        bk = banks[:, n % 8, :]
                        if job[0] == "turn":
                            _, half, k, _ = job
                            ins = dve.tensor_scalar(xnT[:, k, half * BANK:(half + 1) * BANK], bk, gf[:, k:k + 1],
                                                    bf[:, k:k + 1], ALU.mult, ALU.add)
                        else:
                            i = job[1]
                            dve.wait_ge(added, i + 1)
                            ins = dve.tensor_tensor(x[:, b, i, :], bk[:, 0:D], x[:, b, i, :], ALU.add)
                        ins.then_inc(done["v"], 1)
            clear(nc, used)


def context_attention(nc, a, sem, sb, x, ident, ctxT, banks, last):
    dk = 64 if last else DH
    hk = P // dk
    nk = H // hk
    wk_ = hk * S
    nu = 2
    UH = H // nu
    UW = UH * S
    npc = -(-HS // P)
    prefix = "L3_xattn_" if last else "L2_xattn_"
    weights = {k[len(prefix):].lower(): v for k, v in a.items() if k.startswith(prefix)}
    jobs = [("turn", half, k, "sv"[k]) for half in range(2) for k in range(ND)]
    per = 4 if last else 2
    jobs += [(what, n, "v") for what in ("k", "v") for n in range(nk // per)]
    if last:
        jobs += [("fold", kk, pp, "sv"[pp % 2]) for kk in range(ND) for pp in range(4)]
    else:
        jobs += [("q", m, half, "s") for half in range(2) for m in range(ND)]
    jobs += [("vw", c, "sv"[c % 2]) for c in range(npc // 2)]
    done = {"v": sem("moved_v"), "s": sem("moved_s")}
    ring = Ring(jobs, 4, done)
    units = [(i, m) for i in range(NT) for m in range(nu)]
    nbuf = 4
    with ExitStack() as own:
        n_ = lambda s: f"{s}_ctx{int(last)}"
        wq = sb(own, n_("wq"), [P, nk if last else ND, D])
        wk = sb(own, n_("wk"), [P, ND, nk * P])
        wv = sb(own, n_("wv"), [P, ND, nk * P])
        wo = sb(own, n_("wo"), [P, nk, D])
        xh = sb(own, n_("xh"), [P, NT, D])
        xT = sb(own, n_("xT"), [P, ND, T])
        ctxb = sb(own, n_("ctxb"), [P, ND, S])
        kbd = sb(own, n_("kbd"), [P, nk, wk_])
        vbd = sb(own, n_("vbd"), [P, nk, wk_ + 2 * P])
        vw = sb(own, n_("vw"), [P, npc, D])
        pr = sb(own, n_("pr"), [P, nbuf, npc * P])
        pT = sb(own, n_("pT"), [P, 2, npc, P])
        st, mv, sd = sb(own, n_("st"), [P, NT, 6]), sb(own, n_("mv"), [P, NT, 2]), sb(own, n_("sd"), [P, 3, NT])
        top = sb(own, n_("top"), [P, 2, UH])
        tot = sb(own, n_("tot"), [P, 2, UH])
        inv = sb(own, n_("inv"), [P, 4, UH])
        if last:
            g = sb(own, n_("g"), [P, ND])
            fold = sb(own, n_("fold"), [P, ND, HS])
        else:
            fs = sb(own, n_("fs"), [P, nbuf, HS])
            mk = sb(own, n_("mk"), [P, nbuf, HS], U8)
            low = sb(own, n_("low"), [P, nbuf, HS])
            qT = sb(own, n_("qT"), [P, ND, T])
            bq, bk_, bv = (sb(own, n_(n), [P, ND]) for n in ("bq", "bk", "bv"))
            bo, gamma, beta = (sb(own, n_(n), [P, D]) for n in ("bo", "gamma", "beta"))
            heads = sb(own, n_("heads"), [P, UH])
            kv = sb(own, n_("kv"), [P, 2, ND, S])
        loaded, ready = sem("loaded"), sem("const_ready")
        with nc.Block() as block:
            @block.sync
            def _(sp):
                load_weight(sp, wq, weights["wq"], loaded)
                load_weight(sp, wk, weights["wk"], loaded)
                load_weight(sp, wv, weights["wv"], loaded)
                load_weight(sp, wo, weights["wo"], loaded)
                n = 4
                if last:
                    load_column(sp, g, weights["norm_w"], loaded)
                    n += 1
                else:
                    for tile, name in ((bq, "bq"), (bk_, "bk"), (bv, "bv")):
                        load_column(sp, tile, weights[name], loaded)
                    for tile, name in ((bo, "bo"), (gamma, "gamma"), (beta, "beta")):
                        load_row(sp, tile, weights[name], loaded)
                    n += 6
                sp.wait_ge(loaded, 16 * n)

            @block.gpsimd
            def _(pool):
                pool.memset(pr[:], 0.0).then_inc(ready, 1)
                pool.memset(vbd[:], 0.0).then_inc(ready, 1)
                pool.memset(kbd[:], 0.0).then_inc(ready, 1)
                if not last:
                    pool.memset(heads[:], 1.0).then_inc(ready, 1)
                    pool.wait_ge(ready, 4)
                    pool.affine_select(out=heads[:], in_=heads[:], compare_op=ALU.is_ge, fill=0.0, base=0,
                                       pattern=[[-dk, UH]], channel_multiplier=1).then_inc(ready, 1)
                    pool.wait_ge(ready, 5)
                    pool.affine_select(out=heads[:], in_=heads[:], compare_op=ALU.is_ge, fill=0.0, base=dk - 1,
                                       pattern=[[dk, UH]], channel_multiplier=-1).then_inc(ready, 1)
        clear(nc, [loaded, ready])

        with nc.Fori(0, B) as b:
            with nc.Block() as block:
                names = ("proj_ready", "normed", "scored", "taken", "masked", "lowered", "shifted", "exped",
                         "inverted", "weighted", "pt_ready", "pt_copied", "outs_ready", "added", "biased",
                         "copied", "scaled", "closed", "ctx_ready")
                (proj_ready, normed, scored, taken, masked, lowered, shifted, exped, inverted, weighted,
                 pt_ready, pt_copied, outs_ready, added, biased, copied, scaled, closed, ctx_ready) = map(sem, names)
                side = [sem(f"side{n}") for n in range(nbuf)]
                used = [sem(n) for n in names] + side + [done["v"], done["s"], sem("stats"), sem("moments"),
                                                         sem("spread"), sem("root"), sem("chain")]

                def half_of(tile, m):
                    return tile[:, m * UW:(m + 1) * UW]

                def by_head(ap):
                    return ap.rearrange("p (h s) -> p h s", s=S)

                def in_banks(n):
                    r = 2 * (n % 2)
                    return banks[:, r:r + 2, 0:UW // 2]

                def turns(i):
                    return [(3 * i + j, range(4 * j, min(4 * j + 4, npc))) for j in range(3)]

                if not last:
                    @block.sync
                    def _(sp):
                        for i in range(NT):
                            if i >= nbuf:
                                sp.wait_ge(taken, 2 * (i - nbuf + 1))
                                sp.wait_ge(lowered, i - nbuf + 1)
                            sp.dma_start(fs[:, i % nbuf, :], a["fside"][b, i * P:(i + 1) * P, :]).then_inc(side[i % nbuf], 16)
                            sp.dma_start(mk[:, i % nbuf, :], a["mask"][b, i * P:(i + 1) * P, :]).then_inc(side[i % nbuf], 16)
                        sp.wait_ge(lowered, NT)

                @block.gpsimd
                def _(pool):
                    def lower(i):
                        pool.wait_ge(side[i % nbuf], 32 * (i // nbuf + 1))
                        if i >= nbuf:
                            pool.wait_ge(masked, 2 * (i - nbuf + 1))
                        pool.tensor_scalar(low[:, i % nbuf, :], mk[:, i % nbuf, :], MASKED, 0.0, ALU.mult,
                                           ALU.add).then_inc(lowered, 1)

                    if not last:
                        pool.wait_ge(copied, 1)
                        for i in range(NT):
                            pool.tensor_tensor(x[:, b, i, :], x[:, b, i, :], bo[:], ALU.add).then_inc(biased, 1)
                        lower(0)
                    for n in range(len(units) + 3):
                        if n < len(units) and not last:
                            i, m = units[n]
                            if m == 0 and i + 1 < NT:
                                lower(i + 1)
                            pool.wait_ge(taken, n + 1)
                            pool.wait_ge(lowered, i + 1)
                            s_ = half_of(pr[:, i % nbuf, :], m)
                            pool.tensor_tensor(s_, s_, half_of(low[:, i % nbuf, :], m), ALU.add).then_inc(masked, 1)
                        if n >= 3:
                            k = n - 3
                            i, m = units[k]
                            pool.wait_ge(inverted, k + 1)
                            s_ = by_head(half_of(pr[:, i % nbuf, :], m))
                            pool.tensor_tensor(s_, s_, inv[:, k % 4, :].unsqueeze(2).broadcast_to([P, UH, S]),
                                               ALU.mult).then_inc(weighted, 1)
                    if not last:
                        for i in range(NT):
                            pool.wait_ge(normed, i + 1)
                            pool.tensor_tensor(x[:, b, i, :], x[:, b, i, :], gamma[:], ALU.mult).then_inc(scaled, 1)
                            pool.wait_ge(scaled, i + 1)
                            pool.tensor_tensor(x[:, b, i, :], x[:, b, i, :], beta[:], ALU.add).then_inc(closed, 1)

                @block.tensor
                def _(pe):
                    for n, job in enumerate(jobs):
                        ring.wait_free(pe, n)
                        bk = banks[:, n % 4, :]
                        what = job[0]
                        if what == "turn":
                            _, half, k, _ = job
                            pe.wait_ge(normed if last else copied, 4 * (half + 1) if last else 1)
                            ins = turn_tiles(pe, bk, xh, half, k, ident)
                        elif what in ("k", "v"):
                            w = wk if what == "k" else wv
                            pe.wait_ge(ctx_ready, 1)
                            for j in range(per):
                                m = job[1] * per + j
                                for k in range(ND):
                                    ins = pe.matmul(bk[:, j * S:(j + 1) * S], w[:, k, m * P:(m + 1) * P], ctxb[:, k, :],
                                                    start=k == 0, stop=k == ND - 1)
                        elif what == "fold":
                            _, kk, pp, _ = job
                            ring.wait_emptied(pe, ("k", pp // 2))
                            for j in range(2):
                                p_ = 2 * pp + j
                                ins = pe.matmul(bk[:, j * wk_:(j + 1) * wk_], wq[:, p_, kk * P:(kk + 1) * P], kbd[:, p_, :],
                                                start=True, stop=True)
                        elif what == "q":
                            _, m, half, _ = job
                            for k in range(ND):
                                ring.wait_emptied(pe, ("turn", half, k))
                            for k in range(ND):
                                ins = pe.matmul(bk, wq[:, k, m * P:(m + 1) * P], xT[:, k, half * BANK:(half + 1) * BANK],
                                                start=k == 0, stop=k == ND - 1)
                        else:
                            ring.wait_emptied(pe, ("v", nk // per - 1))
                            for j in range(2):
                                c = 2 * job[1] + j
                                over = [m for m in range(nk) if m * wk_ < (c + 1) * P and (m + 1) * wk_ > c * P]
                                for m in over:
                                    at = P + c * P - m * wk_
                                    ins = pe.matmul(bk[:, j * D:(j + 1) * D], vbd[:, m, at:at + P], wo[:, m, :],
                                                    start=m == over[0], stop=m == over[-1])
                        ins.then_inc(proj_ready, 1)
                    for n in range(len(jobs) - 8, len(jobs)):
                        pe.wait_ge(*ring.emptied(n))
                    for k in range(ND):
                        ring.wait_emptied(pe, ("turn", 1, k))

                    def scores(n):
                        i, m = units[n]
                        if n >= 2:
                            pe.wait_ge(taken, n - 1)
                        for j in range(2):
                            dst = banks[:, 2 * (n % 2) + j, 0:UW // 2]
                            if last:
                                for k in range(ND):
                                    c0 = m * UW + j * UW // 2
                                    ins = pe.matmul(dst, xT[:, k, i * P:(i + 1) * P], fold[:, k, c0:c0 + UW // 2],
                                                    start=k == 0, stop=k == ND - 1)
                            else:
                                ins = pe.matmul(dst, qT[:, m, i * P:(i + 1) * P],
                                                kbd[:, m, j * UW // 2:(j + 1) * UW // 2], start=True, stop=True)
                        ins.then_inc(scored, 1)

                    for i in range(NT + 3):
                        if i < NT:
                            scores(2 * i)
                            scores(2 * i + 1)
                        if 2 <= i < NT + 2:
                            pe.wait_ge(weighted, 2 * (i - 1))
                            for n, chunks in turns(i - 2):
                                if n >= 2:
                                    pe.wait_ge(pt_copied, n - 1)
                                for c in chunks:
                                    ins = pe.transpose(banks[:, 4 + n % 2, (c % 4) * P:(c % 4 + 1) * P],
                                                       pr[:, (i - 2) % nbuf, c * P:(c + 1) * P], ident[:])
                                ins.then_inc(pt_ready, 1)
                        if i >= 3:
                            j = i - 3
                            pe.wait_ge(pt_copied, 3 * (j + 1))
                            if j >= 2:
                                pe.wait_ge(added, j - 1)
                            for c in range(npc):
                                ins = pe.matmul(banks[:, 6 + j % 2, 0:D], pT[:, j % 2, c, :], vw[:, c, :],
                                                start=c == 0, stop=c == npc - 1)
                            ins.then_inc(outs_ready, 1)

                @block.scalar
                def _(act):
                    if last:
                        root_of(act, sem, sd)
                    else:
                        act.activation(xh[:], x[:, b], ACT.Copy).then_inc(copied, 1)
                    for n, job in enumerate(jobs):
                        if job[-1] != "s":
                            continue
                        act.wait_ge(proj_ready, n + 1)
                        bk = banks[:, n % 4, :]
                        if job[0] == "turn":
                            _, half, k, _ = job
                            dst = xT[:, k, half * BANK:(half + 1) * BANK]
                            ins = act.activation(dst, bk, ACT.Copy, scale=g[:, k:k + 1] if last else 1.0)
                        elif job[0] == "fold":
                            _, kk, pp, _ = job
                            ins = act.activation(fold[:, kk, 2 * wk_ * pp:2 * wk_ * (pp + 1)], bk[:, 0:2 * wk_], ACT.Copy)
                        elif job[0] == "q":
                            _, m, half, _ = job
                            ins = act.activation(qT[:, m, half * BANK:(half + 1) * BANK], bk, ACT.Identity,
                                                 bias=bq[:, m:m + 1])
                        else:
                            c = 2 * job[1]
                            ins = act.activation(vw[:, c:c + 2, :].rearrange("p c d -> p (c d)"), bk, ACT.Copy)
                        ins.then_inc(done["s"], 1)

                    def exps(n):
                        i, m = units[n]
                        act.wait_ge(taken if last else shifted, n + 1)
                        s_ = half_of(pr[:, i % nbuf, :], m)
                        act.activation(s_, s_, ACT.Exp, scale=1.0 if last else DH ** -0.5).then_inc(exped, 1)

                    for i in range(NT + 2):
                        for n in (2 * i - 1, 2 * i):
                            if 0 <= n < len(units):
                                exps(n)
                        if i >= 2:
                            for n, chunks in turns(i - 2):
                                act.wait_ge(pt_ready, n + 1)
                                if i >= 4 and n == 3 * (i - 2):
                                    act.wait_ge(outs_ready, i - 3)
                                w = len(chunks) * P
                                act.activation(pT[:, i % 2, chunks[0]:chunks[-1] + 1, :].rearrange("p c t -> p (c t)"),
                                               banks[:, 4 + n % 2, 0:w], ACT.Copy).then_inc(pt_copied, 1)
                    if not last:
                        root_of(act, sem, sd)

                @block.vector
                def _(dve):
                    chain = Chain(dve, sem("chain"))
                    dve.tensor_copy(ctxb[:], ctxT[:, b]).then_inc(ctx_ready, 1)
                    if last:
                        normalise(dve, sem, lambda i: x[:, b, i, :], lambda i: xh[:, i, :], st, mv, sd, chain,
                                  normed, 1e-6, False)
                    for n, job in enumerate(jobs):
                        if job[-1] != "v":
                            continue
                        dve.wait_ge(proj_ready, n + 1)
                        bk = banks[:, n % 4, :]
                        what = job[0]
                        if what == "turn":
                            _, half, k, _ = job
                            dst = xT[:, k, half * BANK:(half + 1) * BANK]
                            if last:
                                ins = dve.tensor_scalar(dst, bk, g[:, k:k + 1], None, ALU.mult)
                            else:
                                ins = dve.tensor_copy(dst, bk)
                        elif what in ("k", "v"):
                            dst, o = (kbd, 0) if what == "k" else (vbd, P)
                            if last:
                                for h in range(hk):
                                    rows = slice(h * dk, (h + 1) * dk)
                                    ins = dve.tensor_copy(
                                        dst[rows, per * job[1]:per * (job[1] + 1), o + h * S:o + (h + 1) * S],
                                        bk[rows, 0:per * S].rearrange("p (c s) -> p c s", s=S))
                            else:
                                for m in range(ND):
                                    t = kv[:, int(what == "v"), m, :]
                                    bias = (bk_ if what == "k" else bv)[:, m:m + 1]
                                    chain(dve.tensor_scalar(t, bk[:, m * S:(m + 1) * S], bias, None, ALU.add))
                                    ins = dve.tensor_tensor(by_head(dst[:, m, o:o + wk_]),
                                                            t.unsqueeze(1).broadcast_to([P, UH, S]),
                                                            heads[:].unsqueeze(2).broadcast_to([P, UH, S]), ALU.mult)
                        elif what == "fold":
                            _, kk, pp, _ = job
                            ins = dve.tensor_copy(fold[:, kk, 2 * wk_ * pp:2 * wk_ * (pp + 1)], bk[:, 0:2 * wk_])
                        else:
                            c = 2 * job[1]
                            ins = dve.tensor_copy(vw[:, c:c + 2, :].rearrange("p c d -> p (c d)"), bk)
                        ins.then_inc(done["v"], 1)

                    def two(ap):
                        return ap.rearrange("p (a c) -> p a c", a=2)

                    def take(n):
                        i, m = units[n]
                        dve.wait_ge(scored, n + 1)
                        dve.wait_ge(side[i % nbuf], 32 * (i // nbuf + 1))
                        if i >= nbuf:
                            dve.wait_ge(pt_ready, 3 * (i - nbuf + 1))
                        dve.tensor_tensor(two(half_of(pr[:, i % nbuf, :], m)), in_banks(n),
                                          two(half_of(fs[:, i % nbuf, :], m)), ALU.mult).then_inc(taken, 1)

                    def shift(n):
                        i, m = units[n]
                        if last:
                            dve.wait_ge(scored, n + 1)
                            if i >= nbuf:
                                dve.wait_ge(pt_ready, 3 * (i - nbuf + 1))
                            src = in_banks(n).rearrange("p a (h s) -> p a h s", s=S)
                            chain(dve.tensor_reduce(top[:, n % 2, :].rearrange("p (a h) -> p a h", a=2), src, AX.X, ALU.max))
                            for j in range(2):
                                hs = slice(j * UH // 2, (j + 1) * UH // 2)
                                ins = dve.tensor_tensor(
                                    by_head(half_of(pr[:, i % nbuf, :], m))[:, hs, :], src[:, j],
                                    top[:, n % 2, hs].unsqueeze(2).broadcast_to([P, UH // 2, S]), ALU.subtract)
                                ins.then_inc(taken if j else sem("chain"), 1)
                                if not j:
                                    chain.n += 1
                        else:
                            dve.wait_ge(masked, n + 1)
                            s_ = by_head(half_of(pr[:, i % nbuf, :], m))
                            chain(dve.tensor_reduce(top[:, n % 2, :], s_, AX.X, ALU.max))
                            dve.tensor_tensor(s_, s_, top[:, n % 2, :].unsqueeze(2).broadcast_to([P, UH, S]),
                                              ALU.subtract).then_inc(shifted, 1)

                    def invert(n):
                        i, m = units[n]
                        dve.wait_ge(exped, n + 1)
                        chain(dve.tensor_reduce(tot[:, n % 2, :], by_head(half_of(pr[:, i % nbuf, :], m)), AX.X, ALU.add))
                        if n >= 4:
                            dve.wait_ge(weighted, n - 3)
                        dve.reciprocal(inv[:, n % 4, :], tot[:, n % 2, :]).then_inc(inverted, 1)

                    def add(i):
                        dve.wait_ge(outs_ready, i + 1)
                        if not last:
                            dve.wait_ge(biased, i + 1)
                        dve.tensor_tensor(x[:, b, i, :], banks[:, 6 + i % 2, 0:D], x[:, b, i, :], ALU.add).then_inc(added, 1)

                    for n in range(len(units) + 2):
                        if n < len(units):
                            shift(n) if last else take(n)
                        if not last and 1 <= n <= len(units):
                            shift(n - 1)
                        if n >= 2:
                            invert(n - 2)
                        if n % 2 == 1 and 9 <= n < len(units):
                            add((n - 9) // 2)
                    for i in range(NT - 4, NT):
                        add(i)
                    if not last:
                        normalise(dve, sem, lambda i: x[:, b, i, :], lambda i: x[:, b, i, :], st, mv, sd, chain,
                                  normed, 1e-5, True, ready=added)
            clear(nc, used)


def arrays(inputs):
    import numpy as np
    t = lambda v, *axes: np.ascontiguousarray(np.transpose(v, axes or None))
    out = {k: np.ascontiguousarray(v) for k, v in inputs.items() if k[0:2] in ("L0", "L1", "L2", "L3")}
    out["x"] = np.ascontiguousarray(inputs["x"])
    out["ctxT"] = t(inputs["ctx_1024"], 0, 2, 1)
    out["fside"] = t(inputs["fside_Bx16xSxS2_0"], 0, 2, 1, 3).reshape(B, T, HS)
    out["mask"] = t(inputs["mask_Bx16xSxS2_bk0"], 0, 2, 1, 3).reshape(B, T, HS)
    for name in ("L1_xattn_Wqf", "L1_xattn_Wkf", "L2_xattn_Wq", "L2_xattn_Wk", "L2_xattn_Wv", "L2_xattn_Wo",
                 "L3_xattn_wq"):
        out[name] = t(inputs[name])
    return out


def kernel(**inputs):
    import numpy as np
    import concourse.bacc as bacc
    from concourse.bass_utils import run_bass_kernel_spmd

    nc = bacc.Bacc("TRN2", target_bir_lowering=False, num_devices=1)
    sent = {f"in_{k}": v for k, v in arrays(inputs).items()}
    a = {k[3:]: nc.dram_tensor(k, v.shape, mybir.dt.from_np(v.dtype), kind="ExternalInput").ap()
         for k, v in sent.items()}
    out = nc.dram_tensor("out", [B, T, D], F32, kind="ExternalOutput").ap()
    build(nc, a, out)
    return run_bass_kernel_spmd(nc, [sent], core_ids=[0]).results[0]["out"]
```

```python
from contextlib import ExitStack

import concourse.bass as bass
from concourse import mybir

F32 = mybir.dt.float32
BF16 = mybir.dt.bfloat16
U8 = mybir.dt.uint8
ALU = mybir.AluOpType
ACT = mybir.ActivationFunctionType
AX = mybir.AxisListType

P = 128
B, T, D, H, S = 4, 1024, 256, 16, 77
NT, ND = T // P, D // P
DH = D // H
HS = H * S
FF = 1024
WINDOW = 64
MASKED = -1e30
UNUSED = 3e38

QH = 4
NQ = H // QH
KW = S + T
TERMS_Q = (0, 0, 0, 1, 1, 2)
TERMS_K = (0, 1, 2, 0, 1, 0)
KR = DH * len(TERMS_Q)
CH = 256
NCH = T // CH
BANK = 512
VW_JOBS = -(-HS // P) // 2


def causal_ring_jobs():
    jobs = []
    for i in range(NT):
        end = S + P * (i + 1)
        for slot, c0 in enumerate(range(0, end, BANK)):
            n = min(BANK, end - c0)
            m0 = max(c0, end - P)
            mask = (m0 - (end - P), m0 - c0, c0 + n - m0) if m0 < c0 + n else None
            jobs.append((1, n, i, slot, ((i, 0, c0, n, mask),)))
    return jobs


def window_ring_jobs():
    w = P + WINDOW
    jobs = [(1, P, 0, 0, ((0, 0, S, P, (WINDOW, 0, P)),))]
    for i in range(1, NT, 2):
        tiles = [i, i + 1] if i + 1 < NT else [i]
        jobs.append((len(tiles), w, i, 0,
                     tuple((t, w * n, S + P * t - WINDOW, w, (0, w * n, w)) for n, t in enumerate(tiles))))
    return jobs


def causal_steps(c):
    steps = [("exp", 0, 0, CH, None)]
    steps.append(("exp", 2 + 2 * c, P, P, (0, P, P)))
    steps += [("exp", 1 + j, 0, CH, None) for j in range(2 * c)]
    steps.append(("exp", 1 + 2 * c, 0, CH, (0, 0, P)))
    return steps


def window_steps(c):
    steps = [("square", 0, 0, CH, None), ("exp", 2 + 2 * c, 0, CH, (0, 0, CH))]
    if c:
        steps.append(("exp", 2 * c, 0, WINDOW, (2 * P, 0, WINDOW)))
    return steps + [("exp", 1 + 2 * c, 0, CH, (P, 0, CH))]


def spread(main, extra, start, stop):
    out, n = list(main[:start]), stop - start
    for k in range(n):
        out.append(main[start + k])
        out += extra[len(extra) * k // n:len(extra) * (k + 1) // n]
    return out + list(main[stop:])


def project_tokens(first):
    tokens = [("stats",), ("root",), ("norm",)]
    tokens += [("flip", half, k) for half in range(2) for k in range(ND)]
    tokens += [("context",)] + ([] if first else [("ke", 0), ("ke", 1)]) + [("kc", 0), ("kc", 1)]
    for u in range(4):
        tokens += [("qk", u, 0), ("qk", u, 1), ("high", u)]
        if u:
            tokens.append(("middle", u - 1))
    return tokens + [("middle", 3)]


def attention_tokens(ring_jobs, steps_of, first, this, following):
    jobs = [(h, j) for h in range(QH) for j in ring_jobs]
    if not this:
        return project_tokens(first) + [("stack", NQ), ("stack", NQ + 1)] \
            + [("ring", NQ, *job) for job in jobs] + [("shift", NQ)]
    steps = [(c, n, step) for c in range(NCH) for n, step in enumerate(steps_of(c))]
    order = [("stack", 2), ("stack", 3)]
    ends = []
    for q in range(NQ):
        main = []
        for k, (c, n, step) in enumerate(steps):
            main.append(("scores", q, c, n, step))
            if k:
                main.append(("values", q, *steps[k - 1]))
            elif q == 0:
                main += [("vals", i) for i in range(-1, NT)]
            if k >= 2 and steps[k - 2][0] != steps[k - 1][0]:
                main.append(("turn", q, steps[k - 2][0]))
        main.append(("values", q, *steps[-1]))
        main.append(("turn", q, NCH - 1))
        if q + 1 < NQ or following and first:
            ring = [("ring", q + 1, *job) for job in jobs]
            main = spread(main, ring, 0, len(main) - 4)
            main.insert(len(main) - 1, ("shift", q + 1))
        order += main
        ends.append(len(order))
    if not first:
        tail = [t for i in range(NT + 1) for t in ([("mix", i)] * (i < NT) + [("out", i - 1)] * (i > 0))]
        if following:
            tail = spread(tail, [("ring", NQ, *job) for job in jobs] + [("shift", NQ)], 0, len(tail))
        order += tail
    if following:
        extra = project_tokens(first)
        order = spread(order, extra, ends[0] // 3 if first else ends[0] // 3, ends[2 if first else 2] - 10)
        last_of = lambda q: max(n for n, t in enumerate(order) if t[0] == "scores" and t[1] == q)
        at = 1 + max(n for n, t in enumerate(order) if t[0] == "middle")
        at = max(at, last_of(1) + 1)
        order[at:at] = [("stack", NQ), ("stack", NQ + 1)]
    return order


def build(nc, a, out, upto=5, only=None):
    with ExitStack() as whole:
        sems = {}

        def sem(name):
            if name not in sems:
                sems[name] = whole.enter_context(nc.semaphore(name))
            return sems[name]

        def sb(stack, name, shape, dt=F32):
            return stack.enter_context(nc.sbuf_tensor(name, shape, dt))

        x = sb(whole, "x_tokens", [P, B, NT, D])
        ident = sb(whole, "ident", [P, P])
        identb = sb(whole, "identb", [P, P], BF16)
        mask_q = sb(whole, "mask_q", [P, P], BF16)
        mask_k = sb(whole, "mask_k", [P, P], BF16)
        win_q = sb(whole, "win_q", [P, P + WINDOW], BF16)
        win_k = sb(whole, "win_k", [P, P + CH], BF16)
        ctxT = sb(whole, "ctxT", [P, B, ND, S])
        banks = whole.enter_context(nc.psum_tensor("banks", [P, 8, BANK], F32))

        setup(nc, a, sem, x, ident, identb, mask_q, mask_k, win_q, win_k, ctxT)
        if only in (None, 1):
            attention_layer(nc, a, sem, sb, x, ident, identb, mask_q, mask_k, ctxT, banks, True)
        if upto >= 2 and only in (None, 2):
            mlp(nc, a, sem, sb, x, ident, banks)
        if upto >= 3 and only in (None, 3):
            attention_layer(nc, a, sem, sb, x, ident, identb, win_q, win_k, ctxT, banks, False)
        if upto >= 4 and only in (None, 4):
            context_attention(nc, a, sem, sb, x, ident, ctxT, banks, False)
        if upto >= 5 and only in (None, 5):
            context_attention(nc, a, sem, sb, x, ident, ctxT, banks, True)
        store(nc, sem, x, out)


def clear(nc, sems):
    numbers = [one.num for one in sems]
    nc.all_engine_barrier(sems_to_clear=range(min(numbers), max(numbers) + 1))


def setup(nc, a, sem, x, ident, identb, mask_q, mask_k, win_q, win_k, ctxT):
    loaded, filled, const_ready = sem("loaded"), sem("filled"), sem("const_ready")
    with nc.Block() as block:
        @block.sync
        def _(sp):
            for b in range(B):
                sp.dma_start(x[:, b], a["x"][b].rearrange("(i p) d -> p i d", p=P)).then_inc(loaded, 16)
            for b in range(B):
                sp.dma_start(ctxT[:, b], a["ctxT"][b].rearrange("(k p) s -> p k s", p=P)).then_inc(loaded, 16)
            sp.wait_ge(loaded, 2 * B * 16)

        @block.gpsimd
        def _(pool):
            pool.memset(ident[:], 0.0).then_inc(filled, 1)
            pool.memset(identb[:], 0.0).then_inc(filled, 1)
            for m in (mask_q, mask_k, win_q, win_k):
                pool.memset(m[:], 0.0).then_inc(filled, 1)
            pool.wait_ge(filled, 6)
            for m in (ident, identb):
                pool.affine_select(out=m[:], in_=m[:], compare_op=ALU.not_equal, fill=1.0, base=0,
                                   pattern=[[-1, P]], channel_multiplier=1).then_inc(const_ready, 1)
            pool.affine_select(out=mask_q[:], in_=mask_q[:], compare_op=ALU.is_ge, fill=MASKED, base=0,
                               pattern=[[-1, P]], channel_multiplier=1).then_inc(const_ready, 1)
            pool.affine_select(out=mask_k[:], in_=mask_k[:], compare_op=ALU.is_ge, fill=MASKED, base=0,
                               pattern=[[1, P]], channel_multiplier=-1).then_inc(const_ready, 1)
            pool.affine_select(out=win_q[:], in_=win_q[:], compare_op=ALU.is_ge, fill=MASKED, base=0,
                               pattern=[[1, P + WINDOW]], channel_multiplier=-1).then_inc(const_ready, 1)
            pool.wait_ge(const_ready, 5)
            pool.affine_select(out=win_q[:], in_=win_q[:], compare_op=ALU.is_ge, fill=MASKED, base=WINDOW,
                               pattern=[[-1, P + WINDOW]], channel_multiplier=1).then_inc(const_ready, 1)
            pool.affine_select(out=win_k[:], in_=win_k[:], compare_op=ALU.is_ge, fill=MASKED, base=-P,
                               pattern=[[1, P + CH]], channel_multiplier=-1).then_inc(const_ready, 1)
            pool.wait_ge(const_ready, 7)
            pool.affine_select(out=win_k[:], in_=win_k[:], compare_op=ALU.is_ge, fill=MASKED, base=WINDOW + P,
                               pattern=[[-1, P + CH]], channel_multiplier=1).then_inc(const_ready, 1)
    clear(nc, [loaded, filled, const_ready])


def store(nc, sem, x, out):
    stored = sem("stored")
    with nc.Block() as block:
        @block.sync
        def _(sp):
            for b in range(B):
                sp.dma_start(out[b].rearrange("(i p) d -> p i d", p=P), x[:, b]).then_inc(stored, 16)
            sp.wait_ge(stored, 16 * B)
    clear(nc, [stored])


def load_weight(eng, tile, src, done):
    eng.dma_start(tile[:], src.rearrange("(k p) n -> p k n", p=P)).then_inc(done, 16)


def load_column(eng, tile, src, done):
    eng.dma_start(tile[:], src.rearrange("(k p) -> p k", p=P), allow_slow_non_contiguous=True).then_inc(done, 16)


def load_row(eng, tile, src, done):
    eng.dma_start(tile[:], src.partition_broadcast(P)).then_inc(done, 16)


class Chain:

    def __init__(self, eng, sem):
        self.eng, self.sem, self.n = eng, sem, 0

    def __call__(self, ins):
        self.n += 1
        ins.then_inc(self.sem, 1)
        self.eng.wait_ge(self.sem, self.n)


def take_stats(dve, sem, xin, st, tiles):
    for i in tiles:
        dve.bn_stats(st[:, i, :], xin(i)).then_inc(sem("stats"), 1)


def take_spread(dve, sem, st, mv, sd, chain, eps, centred, time=0):
    for i in range(NT):
        dve.wait_ge(sem("stats"), time * NT + i + 1)
        dve.bn_aggr(mv[:, i, :], st[:, i, :]).then_inc(sem("moments"), 1)
    dve.wait_ge(sem("moments"), (time + 1) * NT)
    if centred:
        dve.tensor_scalar(sd[:, 0, :], mv[:, :, 1], eps, None, ALU.add).then_inc(sem("spread"), 1)
    else:
        chain(dve.tensor_tensor(sd[:, 1, :], mv[:, :, 0], mv[:, :, 0], ALU.mult))
        chain(dve.tensor_tensor(sd[:, 2, :], sd[:, 1, :], mv[:, :, 1], ALU.add))
        dve.tensor_scalar(sd[:, 0, :], sd[:, 2, :], eps, None, ALU.add).then_inc(sem("spread"), 1)


def take_moments(dve, sem, xin, st, mv, sd, chain, eps, centred, time=0, ready=None):
    for i in range(NT):
        if ready:
            dve.wait_ge(ready, i + 1)
        take_stats(dve, sem, xin, st, [i])
    take_spread(dve, sem, st, mv, sd, chain, eps, centred, time)


def normalise_tiles(dve, sem, xin, xhat, mv, sd, chain, normed, centred, time=0, tiles=range(NT)):
    if 0 in tiles:
        dve.wait_ge(sem("root"), time + 1)
        chain(dve.reciprocal(sd[:, 2, :], sd[:, 1, :]))
    for i in tiles:
        if centred:
            ins = dve.tensor_scalar(xhat(i), xin(i), mv[:, i, 0:1], sd[:, 2, i:i + 1], ALU.subtract, ALU.mult)
        else:
            ins = dve.tensor_scalar(xhat(i), xin(i), sd[:, 2, i:i + 1], None, ALU.mult)
        ins.then_inc(normed, 1)


def root_of(act, sem, sd, time=0):
    act.wait_ge(sem("spread"), time + 1)
    act.activation(sd[:, 1, :], sd[:, 0, :], ACT.Sqrt).then_inc(sem("root"), 1)


def turn_tiles(pe, bank, xh, half, k, ident):
    for n in range(4):
        ins = pe.transpose(bank[:, n * P:(n + 1) * P], xh[:, 4 * half + n, k * P:(k + 1) * P], ident[:])
    return ins


class Ring:

    def __init__(self, banks, where, order, emptier, done):
        self.banks, self.where, self.emptier = banks, where, emptier
        tokens = [t for t in order if emptier(t)]
        self.at = {t: n for n, t in enumerate(tokens)}
        count, self.counts = dict.fromkeys(done, 0), []
        for t in tokens:
            count[emptier(t)] += 1
            self.counts.append((done[emptier(t)], count[emptier(t)]))

    def bank(self, token):
        return self.banks[:, self.where[self.at[token] % len(self.where)], :]

    def filled(self, token):
        return self.at[token] + 1

    def emptied(self, token):
        return self.counts[self.at[token]]

    def wait_free(self, pe, token):
        n = self.at[token] - len(self.where)
        if n >= 0:
            pe.wait_ge(*self.counts[n])


def attention_layer(nc, a, sem, sb, x, ident, identb, mq, mk, ctxT, banks, first):
    eps = 1e-5 if first else 1e-6
    ring_jobs = causal_ring_jobs() if first else window_ring_jobs()
    steps_of = causal_steps if first else window_steps
    per_quad = sum(len(steps_of(c)) for c in range(NCH))
    slots = 3 if first else 1
    zk = nc.dram_tensor(f"zk{int(first)}", [B, 3, D, KW], BF16, kind="Internal").ap()
    zq = nc.dram_tensor(f"zq{int(first)}", [B, 3, D, T], BF16, kind="Internal").ap()
    units = [(0, 0), (0, 1), (1, 0), (1, 1)]
    RING, PAIRS, OUT = (0, 1, 7), (2, 4), 6
    with ExitStack() as own:
        n_ = lambda s: f"{s}_{int(first)}"
        w = sb(own, n_("w"), [P, ND, 3 * D])
        wc = sb(own, n_("wc"), [P, ND, 2 * D])
        xh = sb(own, n_("xh"), [P, NT, D])
        xnT = sb(own, n_("xnT"), [P, ND, T])
        whole = sb(own, n_("whole"), [P, 2, KW])
        parts = sb(own, n_("parts"), [P, 2, 3, KW], BF16)
        qs = sb(own, n_("qs"), [KR + 1, NQ, QH, T], BF16)
        ks = sb(own, n_("ks"), [KR + 1, NQ, QH, KW], BF16)
        v1 = sb(own, n_("v1"), [P, 1 + NT, H, DH + 1])
        probs = sb(own, n_("probs"), [P, 3, QH * CH])
        oT = sb(own, n_("oT"), [P, 2, 2 * CH])
        nmx = sb(own, n_("nmx"), [P, 2, QH * NT, slots])
        nmb = sb(own, n_("nmb"), [P, 2, QH * NT], BF16)
        nmT = sb(own, n_("nmT"), [QH * NT, 2, P], BF16)
        st = sb(own, n_("st"), [P, NT, 6])
        mv = sb(own, n_("mv"), [P, NT, 2])
        sd = sb(own, n_("sd"), [P, 3, NT])
        den = sb(own, n_("den"), [P, 2, 2, QH])
        rcp = sb(own, n_("rcp"), [P, 2, 2, 2, QH])
        g = sb(own, n_("g"), [P, ND])
        ctxb = sb(own, n_("ctxb"), [P, ND, S])
        mixed = sb(own, n_("mixed"), [P, NT, D if first else 2 * D])
        if first:
            be = sb(own, "be", [P, ND])
            bcol = sb(own, "bcol", [P, 4])
            bcc = sb(own, "bcc", [P, ND])
            vrow, vcrow = sb(own, "vrow", [P, D]), sb(own, "vcrow", [P, D])
        else:
            wout = sb(own, "wout", [P, 4, D])
            wf = sb(own, "wf", [DH, 2, DH])
            both = sb(own, "both", [P, P])
            ke = sb(own, "ke", [P, ND, S])
            blockd = sb(own, "blockd", [P, P])
            mixedT = sb(own, "mixedT", [P, 2, 4, P])
        loaded, ready = sem("loaded"), sem("const_ready")
        folded, tiled = sem("folded"), sem("tiled")
        with nc.Block() as block:
            nload = 0

            @block.sync
            def _(sp):
                nonlocal nload
                if first:
                    load_weight(sp, w, a["L0_xattn_w_qkv"], loaded)
                    load_weight(sp, wc, a["L0_xattn_w_ckv"], loaded)
                    load_column(sp, g, a["L0_xattn_g1"], loaded)
                    load_column(sp, be, a["L0_xattn_be1"], loaded)
                    load_column(sp, bcol, a["L0_xattn_b_qkv"][0:2 * D], loaded)
                    load_column(sp, bcc, a["L0_xattn_b_ckv"][0:D], loaded)
                    load_row(sp, vrow, a["L0_xattn_b_qkv"][2 * D:3 * D], loaded)
                    load_row(sp, vcrow, a["L0_xattn_b_ckv"][D:2 * D], loaded)
                    nload = 8
                else:
                    load_weight(sp, w[:, :, 0:D], a["L1_xattn_Wq"], loaded)
                    load_weight(sp, w[:, :, D:3 * D], a["L1_xattn_Wwin"], loaded)
                    load_weight(sp, wc, a["L1_xattn_Wkv"], loaded)
                    load_column(sp, g, a["L1_xattn_norm_w"], loaded)
                    load_weight(sp, wout, a["L1_xattn_Wout"], loaded)
                    sp.dma_start(wf[:, 0, :], a["L1_xattn_Wkf"]).then_inc(loaded, 16)
                    sp.dma_start(wf[:, 1, :], a["L1_xattn_Wqf"]).then_inc(loaded, 16)
                    nload = 7
                sp.wait_ge(loaded, 16 * nload)

            @block.gpsimd
            def _(pool):
                pool.memset(v1[:], 0.0).then_inc(ready, 1)
                pool.wait_ge(ready, 1)
                pool.memset(v1[:, :, :, DH:DH + 1], 1.0).then_inc(ready, 1)
                if not first:
                    pool.memset(blockd[:], 1.0).then_inc(folded, 1)
                    pool.wait_ge(folded, 1)
                    v = blockd[:].rearrange("p (h d) -> p h d", d=DH)
                    pool.affine_select(out=v, in_=v, compare_op=ALU.is_ge, fill=0.0, base=0,
                                       pattern=[[-DH, P // DH], [0, DH]], channel_multiplier=1).then_inc(folded, 1)
                    pool.wait_ge(folded, 2)
                    pool.affine_select(out=v, in_=v, compare_op=ALU.is_ge, fill=0.0, base=DH - 1,
                                       pattern=[[DH, P // DH], [0, DH]], channel_multiplier=-1).then_inc(folded, 1)

            if not first:
                @block.tensor
                def _(pe):
                    pe.wait_ge(tiled, 1)
                    pe.matmul(banks[:, 0, 0:P], whole[0:DH, 0, 0:P], whole[0:DH, 0, P:2 * P],
                              start=True, stop=True).then_inc(sem("both_ready"), 1)

            @block.vector
            def _(dve):
                dve.memset(ks[KR:KR + 1], 1.0).then_inc(sem("filled"), 1)
                dve.memset(nmx[:], UNUSED).then_inc(sem("filled"), 1)
                dve.memset(banks[:, OUT, :], 0.0).then_inc(sem("filled"), 1)
                if not first:
                    dve.wait_ge(loaded, 16 * nload)
                    n = P // DH
                    src = wf[:].unsqueeze(2).broadcast_to([DH, 2, n, DH])
                    dve.tensor_copy(whole[0:DH, 0, 0:2 * P].rearrange("p (a n d) -> p a n d", a=2, n=n),
                                    src).then_inc(tiled, 1)
                    dve.wait_ge(sem("both_ready"), 1)
                    dve.wait_ge(folded, 3)
                    dve.tensor_tensor(both[:], banks[:, 0, 0:P], blockd[:], ALU.mult).then_inc(tiled, 1)
        clear(nc, [loaded, ready, folded, tiled, sem("both_ready"), sem("filled")])

        def emptier(token):
            what = token[0]
            if what in ("ring", "shift", "turn", "vals", "out"):
                return "v"
            if what in ("ke", "kc", "qk", "mix"):
                return "s"
            if what == "flip":
                return "vs"[token[2]]
            return None

        def run(b, nxt, following):
            order = attention_tokens(ring_jobs, steps_of, first, b is not None, following)
            names = ("ring_ready", "emptied_v", "emptied_s", "normed", "scores_ready", "probs_ready", "probs_used",
                     "out_copied", "high", "rest", "middle", "low", "max_ready", "shift_loaded", "added",
                     "ctx_ready", "stats", "moments", "spread", "root", "chain")
            (ring_ready, emptied_v, emptied_s, normed, scores_ready, probs_ready, probs_used, out_copied, high, rest,
             middle, low, max_ready, shift_loaded, added, ctx_ready) = map(sem, names[:16])
            written = [sem("written0"), sem("written1")]
            stacked = [sem(f"stacked{q}") for q in range(NQ)]
            used = [sem(n) for n in names] + stacked + written
            ring = Ring(banks, RING, order, emptier, {"v": emptied_v, "s": emptied_s})

            def slot(q):
                return q % NQ

            shifts = [t[1] for t in order if t[0] == "shift"]
            turns_to = lambda q, c: ring.emptied(("turn", q, c))

            with nc.Block() as block:
                @block.sync
                def _(sp):
                    nwritten = 0

                    def write(u, part, cut):
                        is_q, m = units[u]
                        sp.wait_ge(cut, u + 1)
                        n = T if is_q else KW
                        sp.dma_start((zq if is_q else zk)[nxt, part, m * P:(m + 1) * P, :],
                                     parts[:, u % 2, part, 0:n]).then_inc(written[u % 2], 16)

                    for token in order:
                        what = token[0]
                        if what == "high":
                            if token[1] >= 2:
                                write(token[1] - 2, 2, low)
                            write(token[1], 0, high)
                        elif what == "middle":
                            write(token[1], 1, middle)
                            if token[1] == 3:
                                write(2, 2, low)
                                write(3, 2, low)
                        elif what == "stack":
                            q = token[1]
                            of = b if q < NQ else nxt
                            if q == NQ:
                                for done in written:
                                    sp.wait_ge(done, 16 * 6)
                            if q >= NQ and b is not None:
                                sp.wait_ge(scores_ready, (q - NQ + 1) * per_quad)
                            rows = slice(slot(q) * QH * DH, (slot(q) + 1) * QH * DH)
                            for dst, z, terms in ((qs, zq, TERMS_Q), (ks, zk, TERMS_K)):
                                for j, part in enumerate(terms):
                                    sp.dma_start(dst[j * DH:(j + 1) * DH, slot(q)],
                                                 z[of, part, rows, :].rearrange("(h d) t -> d h t", d=DH))\
                                        .then_inc(stacked[slot(q)], 16)
                    for q in range(NQ):
                        n = sum(t[0] == "stack" and slot(t[1]) == q for t in order)
                        if n:
                            sp.wait_ge(stacked[q], 16 * 12 * n)
                    if following:
                        for done in written:
                            sp.wait_ge(done, 16 * 6)

                @block.gpsimd
                def _(pool):
                    for token in order:
                        what = token[0]
                        if what in ("high", "middle"):
                            u = token[1]
                            n = T if units[u][0] else KW
                            part = int(what == "middle")
                            out = parts[:, u % 2, 2, 0:n] if part else whole[:, u % 2, 0:n]
                            pool.wait_ge(middle if part else high, u + 1)
                            if part and u >= 2:
                                pool.wait_ge(written[u % 2], 16 * 3)
                            pool.tensor_tensor(out, whole[:, u % 2, 0:n], parts[:, u % 2, part, 0:n],
                                               ALU.subtract).then_inc(low if part else rest, 1)
                        elif what == "turn" and first and token[2] == NCH - 1:
                            q = token[1]
                            pool.wait_ge(*turns_to(q, NCH - 1))
                            cols = slice(q * QH * DH, (q + 1) * QH * DH)
                            pool.tensor_tensor(x[:, b, :, cols], x[:, b, :, cols], mixed[:, :, cols],
                                               ALU.add).then_inc(added, 1)

                @block.tensor
                def _(pe):
                    steps = mixed_steps = 0
                    started = set()
                    for token in order:
                        what, *args = token
                        if emptier(token):
                            ring.wait_free(pe, token)
                            bk = ring.bank(token)
                        if what == "flip":
                            half, k = args
                            pe.wait_ge(normed, 4 * (half + 1))
                            ins = turn_tiles(pe, bk, xh, half, k, ident)
                        elif what == "ke" or what == "kc" and first:
                            pe.wait_ge(ctx_ready, 1)
                            for k in range(ND):
                                ins = pe.matmul(bk[:, 0:S], wc[:, k, args[0] * P:(args[0] + 1) * P], ctxb[:, k, :],
                                                start=k == 0, stop=k == ND - 1)
                        elif what == "kc":
                            pe.wait_ge(*ring.emptied(("ke", args[0])))
                            ins = pe.matmul(bk[:, 0:S], both[:], ke[:, args[0], :], start=True, stop=True)
                        elif what == "qk":
                            u, half = args
                            for k in range(ND):
                                pe.wait_ge(*ring.emptied(("flip", half, k)))
                            is_q, m = units[u]
                            c0 = (0 if is_q else D) + m * P
                            for k in range(ND):
                                ins = pe.matmul(bk, w[:, k, c0:c0 + P], xnT[:, k, half * BANK:(half + 1) * BANK],
                                                start=k == 0, stop=k == ND - 1)
                        elif what == "vals":
                            i, = args
                            rows = S if i < 0 else P
                            for k in range(ND):
                                tokens_, wv = (ctxb[:, k, :], wc[:, k, D:2 * D]) if i < 0 else \
                                    (xnT[:, k, i * P:(i + 1) * P], w[:, k, 2 * D:3 * D])
                                ins = pe.matmul(bk[0:rows, 0:D], tokens_, wv, start=k == 0, stop=k == ND - 1)
                        elif what == "ring":
                            q, h, (tiles, n, i0, piece, pieces) = args
                            if q not in started and (q >= NQ or q >= 2):
                                pe.wait_ge(stacked[slot(q)], 16 * 12 * sum(
                                    t[0] == "stack" and slot(t[1]) == slot(q) and t[1] <= q for t in order))
                            started.add(q)
                            for t, c, key, m, mask in pieces:
                                if mask:
                                    m0, to, mn = mask
                                    pe.matmul(bk[:, to:to + mn], identb[:], mq[:, m0:m0 + mn], start=True,
                                              stop=False, skip_group_check=True)
                                ins = pe.matmul(bk[:, c:c + m], qs[0:KR, slot(q), h, t * P:(t + 1) * P],
                                                ks[0:KR, slot(q), h, key:key + m], start=mask is None, stop=True,
                                                skip_group_check=True)
                        elif what == "shift":
                            q, = args
                            pe.wait_ge(max_ready, shifts.index(q) + 1)
                            ins = pe.transpose(bk[0:QH * NT, 0:P // 2].bitcast(BF16), nmb[:, q % 2, :], identb[:])
                        elif what == "scores":
                            q, c, s, (func, blk, c0, n, mask) = args
                            if c == 0 and s == 0 and q:
                                pe.wait_ge(shift_loaded, 16 * (shifts.index(q) + 1))
                            if steps >= 2:
                                pe.wait_ge(probs_ready, steps - 1)
                            pair = PAIRS[steps % 2]
                            rows = S if blk == 0 else P
                            key = 0 if blk == 0 else S + P * (blk - 1)
                            kr = KR + (func == "exp")
                            for h in range(QH):
                                bk = banks[:, pair + h // 2, h % 2 * CH:(h % 2 + 1) * CH]
                                if mask:
                                    m0, to, mn = mask
                                    pe.matmul(bk[:, to:to + mn], identb[:], mk[:, m0:m0 + mn], start=True, stop=False,
                                              skip_group_check=True)
                                ins = pe.matmul(bk[0:rows, c0:c0 + n], ks[0:kr, slot(q), h, key:key + rows],
                                                qs[0:kr, slot(q), h, c * CH + c0:c * CH + c0 + n],
                                                start=mask is None, stop=True, skip_group_check=True)
                            ins.then_inc(scores_ready, 1)
                            steps += 1
                        elif what == "values":
                            q, c, s, (func, blk, c0, n, mask) = args
                            if s == 0 and (q or c):
                                pe.wait_ge(out_copied, q * NCH + c)
                            if (q, c, s) == (0, 0, 0):
                                pe.wait_ge(*ring.emptied(("vals", NT - 1)))
                            pe.wait_ge(probs_ready, mixed_steps + 1)
                            rows = S if blk == 0 else P
                            lin = func == "square"
                            o0 = (CH if lin else 0) + c0
                            begins = s == (0 if first else 1)
                            for h in range(QH):
                                ins = pe.matmul(banks[32 * h:32 * h + DH + 1, OUT, o0:o0 + n],
                                                v1[0:rows, blk, QH * q + h, :],
                                                probs[0:rows, mixed_steps % 3, h * CH + c0:h * CH + c0 + n],
                                                start=lin or begins, stop=lin or s == len(steps_of(c)) - 1)
                            ins.then_inc(probs_used, 1)
                            mixed_steps += 1
                        elif what == "turn":
                            q, c = args
                            k = q * NCH + c
                            pe.wait_ge(out_copied, k + 1)
                            for n in range(2 if first else 4):
                                ins = pe.transpose(bk[:, n * P:(n + 1) * P], oT[:, k % 2, n * P:(n + 1) * P], ident[:])
                        elif what == "mix":
                            i, = args
                            if i == 0:
                                pe.wait_ge(*turns_to(NQ - 1, NCH - 1))
                            for k in range(4):
                                ins = pe.transpose(bk[:, k * P:(k + 1) * P], mixed[:, i, k * P:(k + 1) * P], ident[:])
                        elif what == "out":
                            i, = args
                            pe.wait_ge(*ring.emptied(("mix", i)))
                            for k in range(4):
                                ins = pe.matmul(bk[:, 0:D], mixedT[:, i % 2, k, :], wout[:, k, :],
                                                start=k == 0, stop=k == 3)
                        if emptier(token):
                            ins.then_inc(ring_ready, 1)

                @block.scalar
                def _(act):
                    steps = 0
                    for token in order:
                        what, *args = token
                        if emptier(token) == "s":
                            act.wait_ge(ring_ready, ring.filled(token))
                            bk = ring.bank(token)
                        if what == "root":
                            root_of(act, sem, sd)
                        elif what == "shift":
                            q = token[1]
                            act.wait_ge(*ring.emptied(token))
                            if q >= NQ and b is not None:
                                act.wait_ge(scores_ready, (q - NQ + 1) * per_quad)
                            act.dma_start(qs[KR:KR + 1, slot(q)].rearrange("o h t -> o (h t)"),
                                           nmT[:, q % 2, :]).then_inc(shift_loaded, 16)
                        elif what == "flip" and args[1]:
                            half, k = args
                            dst = xnT[:, k, half * BANK:(half + 1) * BANK]
                            if first:
                                ins = act.activation(dst, bk, ACT.Identity, scale=g[:, k:k + 1], bias=be[:, k:k + 1])
                            else:
                                ins = act.activation(dst, bk, ACT.Copy, scale=g[:, k:k + 1])
                            ins.then_inc(emptied_s, 1)
                        elif what == "ke":
                            act.activation(ke[:, args[0], :], bk[:, 0:S], ACT.Copy).then_inc(emptied_s, 1)
                        elif what in ("kc", "qk"):
                            u = args[0]
                            is_q, m = units[u]
                            if what == "qk" and u >= 2:
                                act.wait_ge(low, u - 1)
                            if what == "kc":
                                dst, src, bias = whole[:, u, 0:S], bk[:, 0:S], (bcc if first else None, u)
                            else:
                                o = (0 if is_q else S) + args[1] * BANK
                                dst, src, bias = whole[:, u % 2, o:o + BANK], bk, (bcol if first else None,
                                                                                  2 * (1 - is_q) + m)
                            if first:
                                ins = act.activation(dst, src, ACT.Identity, bias=bias[0][:, bias[1]:bias[1] + 1])
                            else:
                                ins = act.activation(dst, src, ACT.Copy)
                            ins.then_inc(emptied_s, 1)
                        elif what == "mix":
                            i = args[0]
                            if i >= 2:
                                act.wait_ge(ring_ready, ring.filled(("out", i - 2)))
                            act.activation(mixedT[:, i % 2].rearrange("p k c -> p (k c)"), bk,
                                           ACT.Copy).then_inc(emptied_s, 1)
                        elif what == "scores":
                            q, c, s, (func, blk, c0, n, mask) = args
                            act.wait_ge(scores_ready, steps + 1)
                            if steps >= 3:
                                act.wait_ge(probs_used, steps - 2)
                            rows = S if blk == 0 else P
                            pair = PAIRS[steps % 2]
                            src = banks[0:rows, pair:pair + 2, :].rearrange("p a (g n) -> p (a g) n", g=2)[:, :, c0:c0 + n]
                            dst = probs[0:rows, steps % 3, :].rearrange("p (h n) -> p h n", h=QH)[:, :, c0:c0 + n]
                            if func == "exp":
                                ins = act.activation(dst, src, ACT.Exp, scale=DH ** -0.5)
                            else:
                                ins = act.activation(dst, src, ACT.Square, scale=0.5, bias=1.0)
                            ins.then_inc(probs_ready, 1)
                            steps += 1
                        elif what == "values" and args[2] == len(steps_of(args[1])) - 1:
                            q, c = args[0:2]
                            k = q * NCH + c
                            act.wait_ge(probs_used, q * per_quad + sum(len(steps_of(j)) for j in range(c + 1)))
                            if k >= 2:
                                act.wait_ge(ring_ready, ring.filled(("turn", (k - 2) // NCH, (k - 2) % NCH)))
                            wd = CH if first else 2 * CH
                            act.activation(oT[:, k % 2, 0:wd], banks[:, OUT, 0:wd], ACT.Copy).then_inc(out_copied, 1)
                    if shifts:
                        act.wait_ge(shift_loaded, 16 * len(shifts))

                @block.vector
                def _(dve):
                    chain = Chain(dve, sem("chain"))
                    for token in order:
                        what, *args = token
                        if emptier(token) == "v":
                            dve.wait_ge(ring_ready, ring.filled(token))
                            bk = ring.bank(token)
                        if what == "stats":
                            take_moments(dve, sem, lambda i: x[:, nxt, i, :], st, mv, sd, chain, eps, first)
                        elif what == "norm":
                            normalise_tiles(dve, sem, lambda i: x[:, nxt, i, :], lambda i: xh[:, i, :], mv, sd, chain,
                                            normed, first)
                        elif what == "context":
                            if b is not None:
                                dve.wait_ge(*ring.emptied(("vals", -1)))
                            dve.tensor_copy(ctxb[:], ctxT[:, nxt]).then_inc(ctx_ready, 1)
                        elif what == "flip" and not args[1]:
                            half, k = args
                            dst = xnT[:, k, half * BANK:(half + 1) * BANK]
                            if first:
                                ins = dve.tensor_scalar(dst, bk, g[:, k:k + 1], be[:, k:k + 1], ALU.mult, ALU.add)
                            else:
                                ins = dve.tensor_scalar(dst, bk, g[:, k:k + 1], None, ALU.mult)
                            ins.then_inc(emptied_v, 1)
                        elif what == "vals":
                            i, = args
                            rows = S if i < 0 else P
                            dst = v1[0:rows, 1 + i, :, 0:DH]
                            src = bk[0:rows, 0:D].rearrange("p (h d) -> p h d", d=DH)
                            if first:
                                row = (vcrow if i < 0 else vrow)[0:rows, :].rearrange("p (h d) -> p h d", d=DH)
                                ins = dve.tensor_tensor(dst, src, row, ALU.add)
                            else:
                                ins = dve.tensor_copy(dst, src)
                            ins.then_inc(emptied_v, 1)
                        elif what == "high":
                            u, = args
                            n = T if units[u][0] else KW
                            for half in range(2):
                                dve.wait_ge(*ring.emptied(("qk", u, half)))
                            if u >= 2:
                                dve.wait_ge(written[u % 2], 16 * 3)
                            dve.tensor_copy(parts[:, u % 2, 0, 0:n], whole[:, u % 2, 0:n]).then_inc(high, 1)
                        elif what == "middle":
                            u, = args
                            n = T if units[u][0] else KW
                            dve.wait_ge(rest, u + 1)
                            dve.tensor_copy(parts[:, u % 2, 1, 0:n], whole[:, u % 2, 0:n]).then_inc(middle, 1)
                        elif what == "ring":
                            q, h, (tiles, n, i0, piece, pieces) = args
                            dst = nmx[:, q % 2, h * NT + i0:h * NT + i0 + tiles, piece]
                            src = bk[:, 0:tiles * n].rearrange("p (t n) -> p t n", t=tiles)
                            dve.tensor_reduce(dst, src, AX.X, ALU.max, negate=True).then_inc(emptied_v, 1)
                            if h == QH - 1 and pieces == ring_jobs[-1][4]:
                                dve.wait_ge(*ring.emptied(token))
                                dve.tensor_reduce(nmb[:, q % 2, :], nmx[:, q % 2], AX.X, ALU.min).then_inc(max_ready, 1)
                        elif what == "shift":
                            q, = args
                            if shifts.index(q) >= 2:
                                dve.wait_ge(shift_loaded, 16 * (shifts.index(q) - 1))
                            dve.tensor_copy(nmT[:, q % 2, :], bk[0:QH * NT, 0:P // 2].bitcast(BF16))\
                               .then_inc(emptied_v, 1)
                        elif what == "turn":
                            q, c = args
                            nt = 1 if first else 2
                            tv = bk[:, 0:nt * 2 * P].rearrange("p (w i h d) -> p w i h d", w=nt, i=2, h=QH)
                            for linear in range(nt):
                                s_ = tv[:, linear, :, :, DH]
                                if linear:
                                    chain(dve.tensor_scalar(den[:, c % 2], s_, 1e-6, None, ALU.add))
                                    s_ = den[:, c % 2]
                                chain(dve.reciprocal(rcp[:, c % 2, linear], s_))
                                c0 = (D if not first and not linear else 0) + q * QH * DH
                                dst = mixed[:, 2 * c:2 * c + 2, c0:c0 + QH * DH].rearrange("p i (h d) -> p i h d", d=DH)
                                ins = dve.tensor_tensor(dst, tv[:, linear, :, :, 0:DH],
                                                        rcp[:, c % 2, linear].unsqueeze(3).broadcast_to([P, 2, QH, DH]), ALU.mult)
                                if linear < nt - 1:
                                    chain(ins)
                            ins.then_inc(emptied_v, 1)
                        elif what == "out":
                            i, = args
                            dve.tensor_tensor(x[:, b, i, :], bk[:, 0:D], x[:, b, i, :], ALU.add).then_inc(emptied_v, 1)
            clear(nc, used)

        run(None, 0, True)
        with nc.Fori(0, B - 1) as b:
            run(b, b + 1, True)
        run(B - 1, None, False)


def mlp_tokens(this, following):
    nf = FF // P
    turns = [("turn", half, k) for half in range(2) for k in range(ND)]
    norm = [("stats", 0), ("root", 0), ("norm", 0), ("stats", 1), ("root", 1), ("norm", 1)]
    if not this:
        return norm + turns
    up = [[("up", f, half) for f in range(nf)] for half in range(2)]
    down = [("down", i) for i in range(NT)]
    if not following:
        return up[0] + down[:NT // 2] + up[1] + down[NT // 2:]
    return norm[:1] + up[0][:4] + norm[1:4] + up[0][4:] + down[:2] + norm[4:] + down[2:NT // 2] \
        + up[1][:3] + turns[:1] + up[1][3:5] + turns[1:2] + up[1][5:] \
        + down[NT // 2:-3] + turns[2:3] + down[-3:-2] + turns[3:] + down[-2:]


def mlp(nc, a, sem, sb, x, ident, banks):
    nf = FF // P
    with ExitStack() as own:
        w1 = sb(own, "w1", [P, ND, FF])
        w2 = sb(own, "w2", [P, nf, D])
        g2, be2, b2 = (sb(own, n, [P, D]) for n in ("g2", "be2", "b2"))
        gf, bf, b1 = sb(own, "gf", [P, ND]), sb(own, "bf", [P, ND]), sb(own, "b1", [P, nf])
        xh = sb(own, "xh_mlp", [P, NT, D])
        xnT = sb(own, "xnT_mlp", [P, ND, T])
        hT = sb(own, "hT", [P, nf, T])
        st, mv, sd = sb(own, "st_mlp", [P, NT, 6]), sb(own, "mv_mlp", [P, NT, 2]), sb(own, "sd_mlp", [P, 3, NT])
        loaded = sem("loaded")
        with nc.Block() as block:
            @block.sync
            def _(sp):
                load_weight(sp, w1, a["L0_xattn_w1"], loaded)
                load_weight(sp, w2, a["L0_xattn_w2"], loaded)
                for tile, name in ((gf, "gf"), (bf, "bf"), (b1, "b1")):
                    load_column(sp, tile, a["L0_xattn_" + name], loaded)
                for tile, name in ((g2, "g2"), (be2, "be2"), (b2, "b2")):
                    load_row(sp, tile, a["L0_xattn_" + name], loaded)
                sp.wait_ge(loaded, 16 * 8)
        clear(nc, [loaded])

        def emptier(token):
            return {"turn": "sv"[token[-1] % 2], "up": "s", "down": "v"}.get(token[0])

        def run(b, nxt, following):
            order = mlp_tokens(b is not None, following)
            names = ("ring_ready", "emptied_v", "emptied_s", "normed", "scaled", "shifted", "added",
                     "stats", "moments", "spread", "root", "chain")
            ring_ready, emptied_v, emptied_s, normed, scaled, shifted, added = map(sem, names[:7])
            ring = Ring(banks, range(8), order, emptier, {"v": emptied_v, "s": emptied_s})
            with nc.Block() as block:
                @block.gpsimd
                def _(pool):
                    for token in order:
                        if token == ("norm", 0):
                            for i in range(NT):
                                pool.wait_ge(normed, i + 1)
                                pool.tensor_tensor(xh[:, i, :], xh[:, i, :], g2[:], ALU.mult).then_inc(scaled, 1)
                                pool.wait_ge(scaled, i + 1)
                                pool.tensor_tensor(xh[:, i, :], xh[:, i, :], be2[:], ALU.add).then_inc(shifted, 1)
                        elif token == ("up", 0, 0):
                            for i in range(NT):
                                pool.tensor_tensor(x[:, b, i, :], x[:, b, i, :], b2[:], ALU.add).then_inc(added, 1)

                @block.tensor
                def _(pe):
                    for token in order:
                        what, *args = token
                        if not emptier(token):
                            continue
                        ring.wait_free(pe, token)
                        bk = ring.bank(token)
                        if what == "turn":
                            half, k = args
                            pe.wait_ge(normed, NT + 4 * (half + 1))
                            ins = turn_tiles(pe, bk, xh, half, k, ident)
                        elif what == "up":
                            f, half = args
                            for k in range(ND):
                                ins = pe.matmul(bk, w1[:, k, f * P:(f + 1) * P], xnT[:, k, half * BANK:(half + 1) * BANK],
                                                start=k == 0, stop=k == ND - 1)
                        else:
                            i, = args
                            pe.wait_ge(*ring.emptied(("up", nf - 1, i // 4)))
                            for f in range(nf):
                                ins = pe.matmul(bk[:, 0:D], hT[:, f, i * P:(i + 1) * P], w2[:, f, :],
                                                start=f == 0, stop=f == nf - 1)
                        ins.then_inc(ring_ready, 1)

                @block.scalar
                def _(act):
                    for token in order:
                        what, *args = token
                        if what == "root":
                            root_of(act, sem, sd, args[0])
                        if emptier(token) != "s":
                            continue
                        act.wait_ge(ring_ready, ring.filled(token))
                        bk = ring.bank(token)
                        if what == "turn":
                            half, k = args
                            ins = act.activation(xnT[:, k, half * BANK:(half + 1) * BANK], bk, ACT.Identity,
                                                 scale=gf[:, k:k + 1], bias=bf[:, k:k + 1])
                        else:
                            f, half = args
                            ins = act.activation(hT[:, f, half * BANK:(half + 1) * BANK], bk, ACT.Gelu,
                                                 bias=b1[:, f:f + 1])
                        ins.then_inc(emptied_s, 1)

                @block.vector
                def _(dve):
                    chain = Chain(dve, sem("chain"))
                    for token in order:
                        what, *args = token
                        if emptier(token) == "v":
                            dve.wait_ge(ring_ready, ring.filled(token))
                            bk = ring.bank(token)
                        if what in ("stats", "norm"):
                            time, = args
                            xin = (lambda i: xh[:, i, :]) if time else (lambda i: x[:, nxt, i, :])
                            if what == "stats":
                                take_moments(dve, sem, xin, st, mv, sd, chain, 1e-5, True, time,
                                             shifted if time else None)
                            else:
                                normalise_tiles(dve, sem, xin, lambda i: xh[:, i, :], mv, sd, chain, normed, True, time)
                        elif what == "turn" and args[1]:
                            half, k = args
                            dve.tensor_scalar(xnT[:, k, half * BANK:(half + 1) * BANK], bk, gf[:, k:k + 1],
                                              bf[:, k:k + 1], ALU.mult, ALU.add).then_inc(emptied_v, 1)
                        elif what == "down":
                            i, = args
                            dve.wait_ge(added, i + 1)
                            dve.tensor_tensor(x[:, b, i, :], bk[:, 0:D], x[:, b, i, :], ALU.add).then_inc(emptied_v, 1)
            clear(nc, [sem(n) for n in names])

        run(None, 0, True)
        with nc.Fori(0, B - 1) as b:
            run(b, b + 1, True)
        run(B - 1, None, False)


def context_schedule(last, this, following, closing):
    nu = 2 * NT
    pe, dve, act, pool = [], [], [], []

    def filled(time, token, engine):
        pe.append((time, token))
        {"v": dve, "s": act}[engine].append((time + {"v": 0.6, "s": 0.0}[engine], token))

    if this:
        for n in range(nu):
            pe.append((n, ("scores", n)))
            act.append((n + 1.5, ("exp", n)))
            dve.append((n + 2.2, ("invert", n)))
            pool.append((n + 3, ("weigh", n)))
            if last:
                dve.append((n, ("shift", n)))
            else:
                dve += [(n, ("take", n)), (n + 1.1, ("shift", n))]
                pool.append((n, ("mask", n)))
                if n % 2 == 0:
                    act.append((n - 2.4, ("lower", n // 2)))
        for c in range(VW_JOBS):
            filled((1.2, 1.4, 1.6, 3.2, 3.4)[c], ("vw", c), "sv"[c % 2])
        for i in range(NT):
            for j in range(3):
                filled(2 * i + 5.1 + j / 10, ("turned", i, j), "s")
            pe += [(2 * i + 7.9, ("out", i, 0)), (2 * i + 8.3, ("out", i, 1))]
            dve.append((2 * i + 9.1, ("out", i)))
    if closing:
        dve += [(1.5 + i / 2, ("stats", i)) for i in range(NT)] + [(5.7, ("spread",))]
        act.append((6.2, ("root",)))
        dve += [(7.5 + i / 2, ("norm", i)) for i in range(NT)]
        pool += [(8.2 + i, ("close", i)) for i in range(NT)]
    if following:
        dve.append((4.0, ("context",)))
        if last:
            dve += [(1.5 + i / 2, ("stats", i)) for i in range(NT)] + [(5.7, ("spread",))]
            act.append((6.2, ("root",)))
            dve += [(7.5 + i / 2, ("norm", i)) for i in range(NT)]
            for n in range(2):
                filled(8.05 + 2 * n, ("k", n), "v")
                filled(12.05 + 2 * n, ("v", n), "v")
            for n, (half, k) in enumerate((half, k) for half in range(2) for k in range(ND)):
                filled(15.2 + n / 10, ("turn", half, k), "sv"[k])
            for n, (kk, pp) in enumerate((kk, pp) for kk in range(ND) for pp in range(4)):
                filled((15.6, 15.7, 17.5, 17.6, 18.5, 18.6, 20.1, 20.2)[n], ("fold", kk, pp), "sv"[pp % 2])
        else:
            act += [(2.2 + i, ("copy", i)) for i in range(4)]
            pool += [(6.2 + i, ("bias", i)) for i in range(NT)]
            for n, (half, k) in enumerate((half, k) for half in range(2) for k in range(ND)):
                filled(8.05 + 2 * n, ("turn", half, k), "sv"[k])
            filled(6.05, ("v", 0), "v")
            filled(15.2, ("k", 0), "v")
            for n, (half, m) in enumerate((half, m) for half in range(2) for m in range(ND)):
                filled((15.6, 17.5, 18.5, 20.1)[n], ("q", m, half), "s")
    return {name: [token for _, token in sorted(steps, key=lambda step: step[0])]
            for name, steps in (("pe", pe), ("dve", dve), ("act", act), ("pool", pool))}


def context_attention(nc, a, sem, sb, x, ident, ctxT, banks, last):
    dk = 64 if last else DH
    hk = P // dk
    nk = H // hk
    wk_ = hk * S
    nu = 2
    UH = H // nu
    UW = UH * S
    npc = -(-HS // P)
    prefix = "L3_xattn_" if last else "L2_xattn_"
    weights = {k[len(prefix):].lower(): v for k, v in a.items() if k.startswith(prefix)}
    per = 4 if last else 2
    units = [(i, m) for i in range(NT) for m in range(nu)]
    nbuf = 4
    with ExitStack() as own:
        n_ = lambda s: f"{s}_ctx{int(last)}"
        wq = sb(own, n_("wq"), [P, nk if last else ND, D])
        wk = sb(own, n_("wk"), [P, ND, nk * P])
        wv = sb(own, n_("wv"), [P, ND, nk * P])
        wo = sb(own, n_("wo"), [P, nk, D])
        xh = sb(own, n_("xh"), [P, NT, D])
        xT = sb(own, n_("xT"), [P, ND, T])
        ctxb = sb(own, n_("ctxb"), [P, ND, S])
        kbd = sb(own, n_("kbd"), [P, nk, wk_])
        vbd = sb(own, n_("vbd"), [P, nk, wk_ + 2 * P])
        vw = sb(own, n_("vw"), [P, npc, D])
        pr = sb(own, n_("pr"), [P, nbuf, npc * P])
        pT = sb(own, n_("pT"), [P, 2, npc, P])
        st, mv, sd = sb(own, n_("st"), [P, NT, 6]), sb(own, n_("mv"), [P, NT, 2]), sb(own, n_("sd"), [P, 3, NT])
        top = sb(own, n_("top"), [P, 2, UH])
        tot = sb(own, n_("tot"), [P, 2, UH])
        inv = sb(own, n_("inv"), [P, 4, UH])
        if last:
            g = sb(own, n_("g"), [P, ND])
            fold = sb(own, n_("fold"), [P, ND, HS])
        else:
            fs = sb(own, n_("fs"), [P, nbuf, HS])
            mk = sb(own, n_("mk"), [P, nbuf, HS], U8)
            low = sb(own, n_("low"), [P, nbuf, HS])
            qT = sb(own, n_("qT"), [P, ND, T])
            bq, bk_, bv = (sb(own, n_(n), [P, ND]) for n in ("bq", "bk", "bv"))
            bo, gamma, beta = (sb(own, n_(n), [P, D]) for n in ("bo", "gamma", "beta"))
            heads = sb(own, n_("heads"), [P, UH])
            kv = sb(own, n_("kv"), [P, 2, ND, S])
        loaded, ready = sem("loaded"), sem("const_ready")
        with nc.Block() as block:
            @block.sync
            def _(sp):
                load_weight(sp, wq, weights["wq"], loaded)
                load_weight(sp, wk, weights["wk"], loaded)
                load_weight(sp, wv, weights["wv"], loaded)
                load_weight(sp, wo, weights["wo"], loaded)
                n = 4
                if last:
                    load_column(sp, g, weights["norm_w"], loaded)
                    n += 1
                else:
                    for tile, name in ((bq, "bq"), (bk_, "bk"), (bv, "bv")):
                        load_column(sp, tile, weights[name], loaded)
                    for tile, name in ((bo, "bo"), (gamma, "gamma"), (beta, "beta")):
                        load_row(sp, tile, weights[name], loaded)
                    n += 6
                sp.wait_ge(loaded, 16 * n)

            @block.gpsimd
            def _(pool):
                pool.memset(pr[:], 0.0).then_inc(ready, 1)
                pool.memset(vbd[:], 0.0).then_inc(ready, 1)
                pool.memset(kbd[:], 0.0).then_inc(ready, 1)
                if not last:
                    pool.memset(heads[:], 1.0).then_inc(ready, 1)
                    pool.wait_ge(ready, 4)
                    pool.affine_select(out=heads[:], in_=heads[:], compare_op=ALU.is_ge, fill=0.0, base=0,
                                       pattern=[[-dk, UH]], channel_multiplier=1).then_inc(ready, 1)
                    pool.wait_ge(ready, 5)
                    pool.affine_select(out=heads[:], in_=heads[:], compare_op=ALU.is_ge, fill=0.0, base=dk - 1,
                                       pattern=[[dk, UH]], channel_multiplier=-1).then_inc(ready, 1)
        clear(nc, [loaded, ready])

        def emptier(token):
            what = token[0]
            if what in ("turned", "q"):
                return "s"
            if what in ("turn", "fold", "vw"):
                return "sv"[token[-1] % 2]
            return "v" if what in ("k", "v") else None

        def half_of(tile, m):
            return tile[:, m * UW:(m + 1) * UW]

        def by_head(ap):
            return ap.rearrange("p (h s) -> p h s", s=S)

        def two(ap):
            return ap.rearrange("p (a c) -> p a c", a=2)

        def in_banks(n):
            r = 2 * (n % 2)
            return banks[:, r:r + 2, 0:UW // 2]

        def out_of(i):
            return banks[:, 6 + i % 2, 0:D]

        def chunks_of(j):
            return range(4 * j, min(4 * j + 4, npc))

        def run(b, nxt, following, closing):
            plan = context_schedule(last, b is not None, following, closing is not None)
            names = ("ring_ready", "emptied_v", "emptied_s", "normed", "scored", "taken", "masked", "lowered",
                     "shifted", "exped", "inverted", "weighted", "outs_ready", "added", "biased", "copied", "scaled", "closed",
                     "ctx_ready", "stats", "moments", "spread", "root", "chain")
            (ring_ready, emptied_v, emptied_s, normed, scored, taken, masked, lowered, shifted, exped, inverted,
             weighted, outs_ready, added, biased, copied, scaled, closed, ctx_ready) = map(sem, names[:19])
            side = [sem(f"side{n}") for n in range(nbuf)]
            ring = Ring(banks, (4, 5), plan["pe"], emptier, {"v": emptied_v, "s": emptied_s})

            with nc.Block() as block:
                if not last and b is not None:
                    @block.sync
                    def _(sp):
                        for i in range(NT):
                            if i >= nbuf:
                                sp.wait_ge(taken, 2 * (i - nbuf + 1))
                                sp.wait_ge(lowered, i - nbuf + 1)
                            sp.dma_start(fs[:, i % nbuf, :], a["fside"][b, i * P:(i + 1) * P, :]).then_inc(side[i % nbuf], 16)
                            sp.dma_start(mk[:, i % nbuf, :], a["mask"][b, i * P:(i + 1) * P, :]).then_inc(side[i % nbuf], 16)
                        for done in side:
                            sp.wait_ge(done, 32 * NT // nbuf)

                @block.gpsimd
                def _(pool):
                    for what, *args in plan["pool"]:
                        if what == "mask":
                            n, = args
                            i, m = units[n]
                            pool.wait_ge(taken, n + 1)
                            s_ = half_of(pr[:, i % nbuf, :], m)
                            pool.wait_ge(lowered, i + 1)
                            pool.tensor_tensor(s_, s_, half_of(low[:, i % nbuf, :], m), ALU.add).then_inc(masked, 1)
                        elif what == "weigh":
                            n, = args
                            i, m = units[n]
                            pool.wait_ge(inverted, n + 1)
                            s_ = by_head(half_of(pr[:, i % nbuf, :], m))
                            pool.tensor_tensor(s_, s_, inv[:, n % 4, :].unsqueeze(2).broadcast_to([P, UH, S]),
                                               ALU.mult).then_inc(weighted, 1)
                        elif what == "bias":
                            i, = args
                            pool.wait_ge(copied, i // 2 + 1)
                            pool.tensor_tensor(x[:, nxt, i, :], x[:, nxt, i, :], bo[:], ALU.add).then_inc(biased, 1)
                        elif what == "close":
                            i, = args
                            pool.wait_ge(normed, i + 1)
                            pool.tensor_tensor(x[:, closing, i, :], x[:, closing, i, :], gamma[:],
                                               ALU.mult).then_inc(scaled, 1)
                            pool.wait_ge(scaled, i + 1)
                            pool.tensor_tensor(x[:, closing, i, :], x[:, closing, i, :], beta[:],
                                               ALU.add).then_inc(closed, 1)

                @block.tensor
                def _(pe):
                    for token in plan["pe"]:
                        what, *args = token
                        if what == "scores":
                            n, = args
                            i, m = units[n]
                            if n >= 2:
                                pe.wait_ge(taken, n - 1)
                            for j in range(2):
                                dst = banks[:, 2 * (n % 2) + j, 0:UW // 2]
                                if last:
                                    for k in range(ND):
                                        c0 = m * UW + j * UW // 2
                                        ins = pe.matmul(dst, xT[:, k, i * P:(i + 1) * P], fold[:, k, c0:c0 + UW // 2],
                                                        start=k == 0, stop=k == ND - 1)
                                else:
                                    ins = pe.matmul(dst, qT[:, m, i * P:(i + 1) * P],
                                                    kbd[:, m, j * UW // 2:(j + 1) * UW // 2], start=True, stop=True)
                            ins.then_inc(scored, 1)
                            continue
                        if what == "out":
                            i, part = args
                            if part == 0:
                                for c in range(VW_JOBS):
                                    pe.wait_ge(*ring.emptied(("vw", c)))
                                if i >= 2:
                                    pe.wait_ge(added, i - 1)
                            for c in (range(3, npc) if part else range(3)):
                                if c % 4 == 0:
                                    pe.wait_ge(*ring.emptied(("turned", i, c // 4)))
                                ins = pe.matmul(out_of(i), pT[:, i % 2, c, :], vw[:, c, :],
                                                start=c == 0, stop=c == npc - 1)
                            if part:
                                ins.then_inc(outs_ready, 1)
                            continue
                        ring.wait_free(pe, token)
                        bk = ring.bank(token)
                        if what == "turned":
                            i, j = args
                            pe.wait_ge(weighted, 2 * (i + 1))
                            for c in chunks_of(j):
                                ins = pe.transpose(bk[:, c % 4 * P:(c % 4 + 1) * P],
                                                   pr[:, i % nbuf, c * P:(c + 1) * P], ident[:])
                        elif what == "turn":
                            half, k = args
                            pe.wait_ge(*((normed, 4 * (half + 1)) if last else (copied, 2 * (half + 1))))
                            ins = turn_tiles(pe, bk, xh, half, k, ident)
                        elif what in ("k", "v"):
                            w = wk if what == "k" else wv
                            pe.wait_ge(ctx_ready, 1)
                            for j in range(per):
                                m = args[0] * per + j
                                for k in range(ND):
                                    ins = pe.matmul(bk[:, j * S:(j + 1) * S], w[:, k, m * P:(m + 1) * P], ctxb[:, k, :],
                                                    start=k == 0, stop=k == ND - 1)
                        elif what == "fold":
                            kk, pp = args
                            pe.wait_ge(*ring.emptied(("k", pp // 2)))
                            for j in range(2):
                                p_ = 2 * pp + j
                                ins = pe.matmul(bk[:, j * wk_:(j + 1) * wk_], wq[:, p_, kk * P:(kk + 1) * P], kbd[:, p_, :],
                                                start=True, stop=True)
                        elif what == "q":
                            m, half = args
                            for k in range(ND):
                                pe.wait_ge(*ring.emptied(("turn", half, k)))
                            for k in range(ND):
                                ins = pe.matmul(bk, wq[:, k, m * P:(m + 1) * P], xT[:, k, half * BANK:(half + 1) * BANK],
                                                start=k == 0, stop=k == ND - 1)
                        elif what == "vw":
                            for j in range(2):
                                c = 2 * args[0] + j
                                over = [m for m in range(nk) if m * wk_ < (c + 1) * P and (m + 1) * wk_ > c * P]
                                for m in over:
                                    at = P + c * P - m * wk_
                                    ins = pe.matmul(bk[:, j * D:(j + 1) * D], vbd[:, m, at:at + P], wo[:, m, :],
                                                    start=m == over[0], stop=m == over[-1])
                        ins.then_inc(ring_ready, 1)

                @block.scalar
                def _(act):
                    for token in plan["act"]:
                        what, *args = token
                        if what == "root":
                            root_of(act, sem, sd)
                            continue
                        if what == "copy":
                            two_tiles = slice(2 * args[0], 2 * args[0] + 2)
                            act.activation(xh[:, two_tiles], x[:, nxt, two_tiles], ACT.Copy).then_inc(copied, 1)
                            continue
                        if what == "lower":
                            i, = args
                            act.wait_ge(side[i % nbuf], 32 * (i // nbuf + 1))
                            if i >= nbuf:
                                act.wait_ge(masked, 2 * (i - nbuf + 1))
                            act.activation(low[:, i % nbuf, :], mk[:, i % nbuf, :], ACT.Copy, scale=MASKED)\
                                .then_inc(lowered, 1)
                            continue
                        if what == "exp":
                            n, = args
                            i, m = units[n]
                            act.wait_ge(taken if last else shifted, n + 1)
                            s_ = half_of(pr[:, i % nbuf, :], m)
                            act.activation(s_, s_, ACT.Exp, scale=1.0 if last else DH ** -0.5).then_inc(exped, 1)
                            continue
                        act.wait_ge(ring_ready, ring.filled(token))
                        bk = ring.bank(token)
                        if what == "turned":
                            i, j = args
                            if i >= 2 and j == 0:
                                act.wait_ge(outs_ready, i - 1)
                            chunks = chunks_of(j)
                            ins = act.activation(pT[:, i % 2, chunks[0]:chunks[-1] + 1, :].rearrange("p c t -> p (c t)"),
                                                 bk[:, 0:len(chunks) * P], ACT.Copy)
                        elif what == "turn":
                            half, k = args
                            ins = act.activation(xT[:, k, half * BANK:(half + 1) * BANK], bk, ACT.Copy,
                                                 scale=g[:, k:k + 1] if last else 1.0)
                        elif what == "fold":
                            kk, pp = args
                            ins = act.activation(fold[:, kk, 2 * wk_ * pp:2 * wk_ * (pp + 1)], bk[:, 0:2 * wk_], ACT.Copy)
                        elif what == "q":
                            m, half = args
                            ins = act.activation(qT[:, m, half * BANK:(half + 1) * BANK], bk, ACT.Identity,
                                                 bias=bq[:, m:m + 1])
                        elif what == "vw":
                            c = 2 * args[0]
                            ins = act.activation(vw[:, c:c + 2, :].rearrange("p c d -> p (c d)"), bk, ACT.Copy)
                        ins.then_inc(emptied_s, 1)

                @block.vector
                def _(dve):
                    chain = Chain(dve, sem("chain"))
                    for token in plan["dve"]:
                        what, *args = token
                        if what == "context":
                            dve.tensor_copy(ctxb[:], ctxT[:, nxt]).then_inc(ctx_ready, 1)
                        elif what in ("stats", "spread", "norm"):
                            at = nxt if last else closing
                            xin = lambda i: x[:, at, i, :]
                            if what == "stats":
                                take_stats(dve, sem, xin, st, args)
                            elif what == "spread":
                                take_spread(dve, sem, st, mv, sd, chain, 1e-6 if last else 1e-5, not last)
                            else:
                                normalise_tiles(dve, sem, xin, (lambda i: xh[:, i, :]) if last else xin, mv, sd, chain,
                                                normed, not last, tiles=args)
                        elif what == "take":
                            n, = args
                            i, m = units[n]
                            dve.wait_ge(scored, n + 1)
                            dve.wait_ge(side[i % nbuf], 32 * (i // nbuf + 1))
                            if i >= nbuf:
                                dve.wait_ge(ring_ready, ring.filled(("turned", i - nbuf, 2)))
                            dve.tensor_tensor(two(half_of(pr[:, i % nbuf, :], m)), in_banks(n),
                                              two(half_of(fs[:, i % nbuf, :], m)), ALU.mult).then_inc(taken, 1)
                        elif what == "shift" and last:
                            n, = args
                            i, m = units[n]
                            dve.wait_ge(scored, n + 1)
                            if i >= nbuf:
                                dve.wait_ge(ring_ready, ring.filled(("turned", i - nbuf, 2)))
                            src = in_banks(n).rearrange("p a (h s) -> p a h s", s=S)
                            chain(dve.tensor_reduce(top[:, n % 2, :].rearrange("p (a h) -> p a h", a=2), src, AX.X, ALU.max))
                            halves = []
                            for j in range(2):
                                hs = slice(j * UH // 2, (j + 1) * UH // 2)
                                halves.append(dve.tensor_tensor(
                                    by_head(half_of(pr[:, i % nbuf, :], m))[:, hs, :], src[:, j],
                                    top[:, n % 2, hs].unsqueeze(2).broadcast_to([P, UH // 2, S]), ALU.subtract))
                            chain(halves[0])
                            halves[1].then_inc(taken, 1)
                        elif what == "shift":
                            n, = args
                            i, m = units[n]
                            dve.wait_ge(masked, n + 1)
                            s_ = by_head(half_of(pr[:, i % nbuf, :], m))
                            chain(dve.tensor_reduce(top[:, n % 2, :], s_, AX.X, ALU.max))
                            dve.tensor_tensor(s_, s_, top[:, n % 2, :].unsqueeze(2).broadcast_to([P, UH, S]),
                                              ALU.subtract).then_inc(shifted, 1)
                        elif what == "invert":
                            n, = args
                            i, m = units[n]
                            dve.wait_ge(exped, n + 1)
                            chain(dve.tensor_reduce(tot[:, n % 2, :], by_head(half_of(pr[:, i % nbuf, :], m)), AX.X, ALU.add))
                            if n >= 4:
                                dve.wait_ge(weighted, n - 3)
                            dve.reciprocal(inv[:, n % 4, :], tot[:, n % 2, :]).then_inc(inverted, 1)
                        elif what == "out":
                            i, = args
                            dve.wait_ge(outs_ready, i + 1)
                            dve.tensor_tensor(x[:, b, i, :], out_of(i), x[:, b, i, :], ALU.add).then_inc(added, 1)
                        else:
                            dve.wait_ge(ring_ready, ring.filled(token))
                            bk = ring.bank(token)
                            if what == "turn":
                                half, k = args
                                dst = xT[:, k, half * BANK:(half + 1) * BANK]
                                if last:
                                    ins = dve.tensor_scalar(dst, bk, g[:, k:k + 1], None, ALU.mult)
                                else:
                                    ins = dve.tensor_copy(dst, bk)
                            elif what in ("k", "v"):
                                dst, o = (kbd, 0) if what == "k" else (vbd, P)
                                if last:
                                    for h in range(hk):
                                        rows = slice(h * dk, (h + 1) * dk)
                                        ins = dve.tensor_copy(
                                            dst[rows, per * args[0]:per * (args[0] + 1), o + h * S:o + (h + 1) * S],
                                            bk[rows, 0:per * S].rearrange("p (c s) -> p c s", s=S))
                                else:
                                    for m in range(ND):
                                        t = kv[:, int(what == "v"), m, :]
                                        bias = (bk_ if what == "k" else bv)[:, m:m + 1]
                                        chain(dve.tensor_scalar(t, bk[:, m * S:(m + 1) * S], bias, None, ALU.add))
                                        ins = dve.tensor_tensor(by_head(dst[:, m, o:o + wk_]),
                                                                t.unsqueeze(1).broadcast_to([P, UH, S]),
                                                                heads[:].unsqueeze(2).broadcast_to([P, UH, S]), ALU.mult)
                            elif what == "fold":
                                kk, pp = args
                                ins = dve.tensor_copy(fold[:, kk, 2 * wk_ * pp:2 * wk_ * (pp + 1)], bk[:, 0:2 * wk_])
                            elif what == "vw":
                                c = 2 * args[0]
                                ins = dve.tensor_copy(vw[:, c:c + 2, :].rearrange("p c d -> p (c d)"), bk)
                            ins.then_inc(emptied_v, 1)
            clear(nc, [sem(n) for n in names] + side)

        run(None, 0, True, None)
        if last:
            with nc.Fori(0, B - 1) as b:
                run(b, b + 1, True, None)
            run(B - 1, None, False, None)
        else:
            run(0, 1, True, None)
            with nc.Fori(1, B - 1) as b:
                run(b, b + 1, True, b - 1)
            run(B - 1, None, False, B - 2)
            run(None, None, False, B - 1)


def arrays(inputs):
    import numpy as np
    t = lambda v, *axes: np.ascontiguousarray(np.transpose(v, axes or None))
    out = {k: np.ascontiguousarray(v) for k, v in inputs.items() if k[0:2] in ("L0", "L1", "L2", "L3")}
    out["x"] = np.ascontiguousarray(inputs["x"])
    out["ctxT"] = t(inputs["ctx_1024"], 0, 2, 1)
    out["fside"] = t(inputs["fside_Bx16xSxS2_0"], 0, 2, 1, 3).reshape(B, T, HS)
    out["mask"] = t(inputs["mask_Bx16xSxS2_bk0"], 0, 2, 1, 3).reshape(B, T, HS)
    for name in ("L1_xattn_Wqf", "L1_xattn_Wkf", "L2_xattn_Wq", "L2_xattn_Wk", "L2_xattn_Wv", "L2_xattn_Wo",
                 "L3_xattn_wq"):
        out[name] = t(inputs[name])
    return out


def kernel(**inputs):
    import numpy as np
    import concourse.bacc as bacc
    from concourse.bass_utils import run_bass_kernel_spmd

    nc = bacc.Bacc("TRN2", target_bir_lowering=False, num_devices=1)
    sent = {f"in_{k}": v for k, v in arrays(inputs).items()}
    a = {k[3:]: nc.dram_tensor(k, v.shape, mybir.dt.from_np(v.dtype), kind="ExternalInput").ap()
         for k, v in sent.items()}
    out = nc.dram_tensor("out", [B, T, D], F32, kind="ExternalOutput").ap()
    build(nc, a, out)
    return run_bass_kernel_spmd(nc, [sent], core_ids=[0]).results[0]["out"]
```

```python
from contextlib import ExitStack

import concourse.bass as bass
from concourse import mybir

F32 = mybir.dt.float32
BF16 = mybir.dt.bfloat16
F32R = mybir.dt.float32r
U8 = mybir.dt.uint8
ALU = mybir.AluOpType
ACT = mybir.ActivationFunctionType
AX = mybir.AxisListType

P = 128
B, T, D, H, S = 4, 1024, 256, 16, 77
NT, ND = T // P, D // P
DH = D // H
HS = H * S
FF = 1024
WINDOW = 64
MASKED = -1e30
UNUSED = 3e38

QH = 4
NQ = H // QH
KW = S + T
TERMS_Q = (0, 0, 0, 1, 1, 2)
TERMS_K = (0, 1, 2, 0, 1, 0)
KR = DH * len(TERMS_Q)
CH = 256
NCH = T // CH
BANK = 512
PARTS = ((0, 0), (0, 1), (1, 0))
VW_JOBS = -(-HS // P) // 2


def causal_ring_jobs():
    jobs = []
    for i in range(NT):
        end = S + P * (i + 1)
        for slot, c0 in enumerate(range(0, end, BANK)):
            n = min(BANK, end - c0)
            m0 = max(c0, end - P)
            mask = (m0 - (end - P), m0 - c0, c0 + n - m0) if m0 < c0 + n else None
            jobs.append((1, n, i, slot, ((i, 0, c0, n, mask),)))
    return jobs


def window_ring_jobs():
    w = P + WINDOW
    jobs = [(1, P, 0, 0, ((0, 0, S, P, (WINDOW, 0, P)),))]
    for i in range(1, NT, 2):
        tiles = [i, i + 1] if i + 1 < NT else [i]
        jobs.append((len(tiles), w, i, 0,
                     tuple((t, w * n, S + P * t - WINDOW, w, (0, w * n, w)) for n, t in enumerate(tiles))))
    return jobs


def causal_steps(c):
    steps = [("exp", 0, 0, CH, None)]
    steps.append(("exp", 2 + 2 * c, P, P, (0, P, P)))
    steps += [("exp", 1 + j, 0, CH, None) for j in range(2 * c)]
    steps.append(("exp", 1 + 2 * c, 0, CH, (0, 0, P)))
    return steps


def window_steps(c):
    steps = [("square", 0, 0, CH, None), ("exp", 1 + 2 * c, 0, CH, (P, 0, CH)), ("exp", 2 + 2 * c, P, P, (P, P, P))]
    if c:
        steps.append(("exp", 2 * c, 0, WINDOW, (2 * P, 0, WINDOW)))
    return steps


def spread(main, extra, start, stop):
    out, n = list(main[:start]), stop - start
    for k in range(n):
        out.append(main[start + k])
        out += extra[len(extra) * k // n:len(extra) * (k + 1) // n]
    return out + list(main[stop:])


def project_tokens(first, lag):
    tokens = [("stats", i) for i in range(NT)] + [("spread",), ("root",)] + [("norm", i) for i in range(NT)]
    tokens += [("flip", half, k) for half in range(2) for k in range(ND)]
    tokens += [("context",)] + ([] if first else [("ke", 0), ("ke", 1)])
    for u in range(4):
        if u % 2 == 0:
            tokens.append(("kc", u))
        tokens += [("qk", u, 0), ("qk", u, 1), ("high", u)]
        if u >= lag:
            tokens.append(("middle", u - lag))
    return tokens + [("middle", u) for u in range(4 - lag, 4)]


def attention_tokens(ring_jobs, steps_of, first, this, following):
    jobs = [(h, j) for h in range(QH) for j in ring_jobs]
    if not this:
        extra = project_tokens(first, 0)
        at = 1 + extra.index(("middle", 1))
        return extra[:at] + [("stack", NQ), ("stack", NQ + 1)] + extra[at:] \
            + [("ring", NQ, *job) for job in jobs] + [("shift", NQ)]
    steps = [(c, n, step) for c in range(NCH) for n, step in enumerate(steps_of(c))]
    order = [("stack", 2), ("stack", 3)]
    ends = []
    for q in range(NQ):
        main = []
        for k, (c, n, step) in enumerate(steps):
            main.append(("scores", q, c, n, step))
            if k:
                main.append(("values", q, *steps[k - 1]))
            elif q == 0:
                main += [("vals", i) for i in range(-1, NT)]
            if k >= 2 and steps[k - 2][0] != steps[k - 1][0]:
                main.append(("turn", q, steps[k - 2][0]))
        main.append(("values", q, *steps[-1]))
        main.append(("turn", q, NCH - 1))
        if q + 1 < NQ or following and first:
            ring = [("ring", q + 1, *job) for job in jobs]
            main = spread(main, ring, 0, len(main) - (9 if first else 7))
            main.insert(len(main) - (5 if first else 3), ("shift", q + 1))
        order += main
        ends.append(len(order))
    if not first:
        tail = [t for i in range(NT + 1) for t in ([("mix", i)] * (i < NT) + [("out", i - 1)] * (i > 0))]
        if following:
            tail = spread(tail, [("ring", NQ, *job) for job in jobs] + [("shift", NQ)], 0, len(tail))
        order += tail
    if following:
        extra = project_tokens(first, 1)
        order = spread(order, extra, 25, ends[2] - 36) if first else spread(order, extra, 18, ends[1] - 1)
        last_of = lambda q: max(n for n, t in enumerate(order) if t[0] == "scores" and t[1] == q)
        for q in (1, 0):
            order.insert(1 + max(order.index(("middle", 1)), last_of(q)), ("stack", NQ + q))
    return order


def build(nc, a, out):
    with ExitStack() as whole:
        sems = {}

        def sem(name):
            if name not in sems:
                sems[name] = whole.enter_context(nc.semaphore(name))
            return sems[name]

        def sb(stack, name, shape, dt=F32):
            return stack.enter_context(nc.sbuf_tensor(name, shape, dt))

        x = sb(whole, "x_tokens", [P, B, NT, D])
        ident = sb(whole, "ident", [P, P])
        identb = sb(whole, "identb", [P, P], BF16)
        mask_q = sb(whole, "mask_q", [P, P], BF16)
        mask_k = sb(whole, "mask_k", [P, P], BF16)
        win_q = sb(whole, "win_q", [P, P + WINDOW], BF16)
        win_k = sb(whole, "win_k", [P, P + CH], BF16)
        ctxT = sb(whole, "ctxT", [P, B, ND, S])
        banks = whole.enter_context(nc.psum_tensor("banks", [P, 8, BANK], F32))

        sem("x_loaded"), sem("loaded")
        arriving = setup(nc, a, sem, x, ident, identb, mask_q, mask_k, win_q, win_k, ctxT)
        attention_layer(nc, a, sem, sb, x, ident, identb, mask_q, mask_k, ctxT, banks, True, arriving)
        mlp(nc, a, sem, sb, x, ident, banks)
        attention_layer(nc, a, sem, sb, x, ident, identb, win_q, win_k, ctxT, banks, False)
        context_attention(nc, a, sem, sb, x, ident, ctxT, banks, False, None)
        context_attention(nc, a, sem, sb, x, ident, ctxT, banks, True, out)


def clear(nc, sems):
    numbers = [one.num for one in sems]
    nc.all_engine_barrier(sems_to_clear=range(min(numbers), max(numbers) + 1))


def setup(nc, a, sem, x, ident, identb, mask_q, mask_k, win_q, win_k, ctxT):
    first_loaded, x_loaded, filled, const_ready = map(sem, ("first_loaded", "x_loaded", "filled", "const_ready"))
    with nc.Block() as block:
        @block.sync
        def _(sp):
            sp.dma_start(x[:, 0], a["x"][0].rearrange("(i p) d -> p i d", p=P)).then_inc(first_loaded, 16)
            for b in range(B):
                sp.dma_start(ctxT[:, b], a["ctxT"][b].rearrange("(k p) s -> p k s", p=P)).then_inc(first_loaded, 16)
            for b in range(1, B):
                sp.dma_start(x[:, b], a["x"][b].rearrange("(i p) d -> p i d", p=P)).then_inc(x_loaded, 16)
            sp.wait_ge(first_loaded, (1 + B) * 16)

        @block.gpsimd
        def _(pool):
            pool.memset(ident[:], 0.0).then_inc(filled, 1)
            pool.memset(identb[:], 0.0).then_inc(filled, 1)
            for m in (mask_q, mask_k, win_q, win_k):
                pool.memset(m[:], 0.0).then_inc(filled, 1)
            pool.wait_ge(filled, 6)
            for m in (ident, identb):
                pool.affine_select(out=m[:], in_=m[:], compare_op=ALU.not_equal, fill=1.0, base=0,
                                   pattern=[[-1, P]], channel_multiplier=1).then_inc(const_ready, 1)
            pool.affine_select(out=mask_q[:], in_=mask_q[:], compare_op=ALU.is_ge, fill=MASKED, base=0,
                               pattern=[[-1, P]], channel_multiplier=1).then_inc(const_ready, 1)
            pool.affine_select(out=mask_k[:], in_=mask_k[:], compare_op=ALU.is_ge, fill=MASKED, base=0,
                               pattern=[[1, P]], channel_multiplier=-1).then_inc(const_ready, 1)
            pool.affine_select(out=win_q[:], in_=win_q[:], compare_op=ALU.is_ge, fill=MASKED, base=0,
                               pattern=[[1, P + WINDOW]], channel_multiplier=-1).then_inc(const_ready, 1)
            pool.wait_ge(const_ready, 5)
            pool.affine_select(out=win_q[:], in_=win_q[:], compare_op=ALU.is_ge, fill=MASKED, base=WINDOW,
                               pattern=[[-1, P + WINDOW]], channel_multiplier=1).then_inc(const_ready, 1)
            pool.affine_select(out=win_k[:], in_=win_k[:], compare_op=ALU.is_ge, fill=MASKED, base=-P,
                               pattern=[[1, P + CH]], channel_multiplier=-1).then_inc(const_ready, 1)
            pool.wait_ge(const_ready, 7)
            pool.affine_select(out=win_k[:], in_=win_k[:], compare_op=ALU.is_ge, fill=MASKED, base=WINDOW + P,
                               pattern=[[-1, P + CH]], channel_multiplier=1).then_inc(const_ready, 1)
    clear(nc, [first_loaded, filled, const_ready])
    return [(x_loaded, 16 * (B - 1))]


def load_weight(eng, tile, src, done):
    eng.dma_start(tile[:], src.rearrange("(k p) n -> p k n", p=P)).then_inc(done, 16)


def load_column(eng, tile, src, done):
    eng.dma_start(tile[:], src.rearrange("(k p) -> p k", p=P), allow_slow_non_contiguous=True).then_inc(done, 16)


def load_row(eng, tile, src, done):
    eng.dma_start(tile[:], src.partition_broadcast(P)).then_inc(done, 16)


def split_weights(dve, pairs, rounded):
    for n, (parts, whole) in enumerate(pairs):
        dve.tensor_copy(parts[:, 0], whole[:]).then_inc(rounded, 1)
        dve.wait_ge(rounded, 2 * n + 1)
        dve.tensor_tensor(parts[:, 1], whole[:], parts[:, 0].bitcast(F32), ALU.subtract).then_inc(rounded, 1)


def products(pe, out, pairs):
    terms = [(left[:, i], right[:, j]) for left, right in pairs for i, j in PARTS]
    for n, (left, right) in enumerate(terms):
        ins = pe.matmul(out, left, right, start=n == 0, stop=n == len(terms) - 1)
    return ins


class Chain:

    def __init__(self, eng, sem):
        self.eng, self.sem, self.n = eng, sem, 0

    def __call__(self, ins):
        self.n += 1
        ins.then_inc(self.sem, 1)
        self.eng.wait_ge(self.sem, self.n)


def take_stats(dve, sem, xin, st, tiles):
    for i in tiles:
        dve.bn_stats(st[:, i, :], xin(i)).then_inc(sem("stats"), 1)


def take_spread(dve, sem, st, mv, sd, chain, eps, centred, time=0):
    for i in range(NT):
        dve.wait_ge(sem("stats"), time * NT + i + 1)
        dve.bn_aggr(mv[:, i, :], st[:, i, :]).then_inc(sem("moments"), 1)
    dve.wait_ge(sem("moments"), (time + 1) * NT)
    if centred:
        dve.tensor_scalar(sd[:, 0, :], mv[:, :, 1], eps, None, ALU.add).then_inc(sem("spread"), 1)
    else:
        chain(dve.tensor_tensor(sd[:, 1, :], mv[:, :, 0], mv[:, :, 0], ALU.mult))
        chain(dve.tensor_tensor(sd[:, 2, :], sd[:, 1, :], mv[:, :, 1], ALU.add))
        dve.tensor_scalar(sd[:, 0, :], sd[:, 2, :], eps, None, ALU.add).then_inc(sem("spread"), 1)


def normalise_tiles(dve, sem, xin, xhat, mv, sd, chain, normed, centred, time=0, tiles=range(NT)):
    if 0 in tiles:
        dve.wait_ge(sem("root"), time + 1)
        chain(dve.reciprocal(sd[:, 2, :], sd[:, 1, :]))
    for i in tiles:
        if centred:
            ins = dve.tensor_scalar(xhat(i), xin(i), mv[:, i, 0:1], sd[:, 2, i:i + 1], ALU.subtract, ALU.mult)
        else:
            ins = dve.tensor_scalar(xhat(i), xin(i), sd[:, 2, i:i + 1], None, ALU.mult)
        ins.then_inc(normed, 1)


def root_of(act, sem, sd, time=0):
    act.wait_ge(sem("spread"), time + 1)
    act.activation(sd[:, 1, :], sd[:, 0, :], ACT.Sqrt).then_inc(sem("root"), 1)


def turn_tiles(pe, bank, xh, half, k, ident):
    for n in range(4):
        ins = pe.transpose(bank[:, n * P:(n + 1) * P], xh[:, 4 * half + n, k * P:(k + 1) * P], ident[:])
    return ins


class Ring:

    def __init__(self, banks, where, order, emptier, done):
        self.banks, self.where, self.emptier = banks, where, emptier
        tokens = [t for t in order if emptier(t)]
        self.at = {t: n for n, t in enumerate(tokens)}
        count, self.counts = dict.fromkeys(done, 0), []
        for t in tokens:
            count[emptier(t)] += 1
            self.counts.append((done[emptier(t)], count[emptier(t)]))

    def bank(self, token):
        return self.banks[:, self.where[self.at[token] % len(self.where)], :]

    def filled(self, token):
        return self.at[token] + 1

    def emptied(self, token):
        return self.counts[self.at[token]]

    def wait_free(self, pe, token):
        n = self.at[token] - len(self.where)
        if n >= 0:
            pe.wait_ge(*self.counts[n])


def attention_layer(nc, a, sem, sb, x, ident, identb, mq, mk, ctxT, banks, first, arriving=()):
    eps = 1e-5 if first else 1e-6
    ring_jobs = causal_ring_jobs() if first else window_ring_jobs()
    steps_of = causal_steps if first else window_steps
    per_quad = sum(len(steps_of(c)) for c in range(NCH))
    slots = 3 if first else 1
    zk = nc.dram_tensor(f"zk{int(first)}", [B, 3, D, KW], BF16, kind="Internal").ap()
    zq = nc.dram_tensor(f"zq{int(first)}", [B, 3, D, T], BF16, kind="Internal").ap()
    units = [(0, 0), (1, 0), (0, 1), (1, 1)]
    RING, PAIRS, OUT = (0, 1, 7), (2, 4), 6
    with ExitStack() as own:
        n_ = lambda s: f"{s}_{int(first)}"
        w = sb(own, n_("w"), [P, ND, 3 * D])
        wc = sb(own, n_("wc"), [P, ND, 2 * D])
        xh = sb(own, n_("xh"), [P, NT, D])
        xnT = sb(own, n_("xnT"), [P, ND, T])
        whole = sb(own, n_("whole"), [P, 2, KW])
        parts = sb(own, n_("parts"), [P, 2, 3, KW], BF16)
        qs = sb(own, n_("qs"), [KR + 1, NQ, QH, T], BF16)
        ks = sb(own, n_("ks"), [KR + 1, NQ, QH, KW], BF16)
        v1 = sb(own, n_("v1"), [P, 1 + NT, H, DH + 1])
        probs = sb(own, n_("probs"), [P, 3, QH * CH])
        oT = sb(own, n_("oT"), [P, 2, 2 * CH])
        nmx = sb(own, n_("nmx"), [P, 2, QH * NT, slots])
        nmb = sb(own, n_("nmb"), [P, 2, QH * NT], BF16)
        nmT = sb(own, n_("nmT"), [QH * NT, 2, P], BF16)
        st = sb(own, n_("st"), [P, NT, 6])
        mv = sb(own, n_("mv"), [P, NT, 2])
        sd = sb(own, n_("sd"), [P, 3, NT])
        den = sb(own, n_("den"), [P, 2, 2, QH])
        rcp = sb(own, n_("rcp"), [P, 2, 2, 2, QH])
        g = sb(own, n_("g"), [P, ND])
        ctxb = sb(own, n_("ctxb"), [P, ND, S])
        mixed = sb(own, n_("mixed"), [P, NT, D if first else 2 * D])
        if first:
            be = sb(own, "be", [P, ND])
            bcol = sb(own, "bcol", [P, 4])
            bcc = sb(own, "bcc", [P, ND])
            vrow, vcrow = sb(own, "vrow", [P, D]), sb(own, "vcrow", [P, D])
        else:
            wout = sb(own, "wout", [P, 4, D])
            wf = sb(own, "wf", [DH, 2, DH])
            both = sb(own, "both", [P, P])
            ke = sb(own, "ke", [P, ND, S])
            blockd = sb(own, "blockd", [P, P])
            mixedT = sb(own, "mixedT", [P, 2, 4, P])
        loaded, ready = sem("loaded"), sem("const_ready")
        folded, tiled, wf_loaded = sem("folded"), sem("tiled"), sem("wf_loaded")
        with nc.Block() as block:
            nload = 0

            @block.sync
            def _(sp):
                nonlocal nload
                if first:
                    load_weight(sp, w, a["L0_xattn_w_qkv"], loaded)
                    load_weight(sp, wc, a["L0_xattn_w_ckv"], loaded)
                    load_column(sp, g, a["L0_xattn_g1"], loaded)
                    load_column(sp, be, a["L0_xattn_be1"], loaded)
                    load_column(sp, bcol, a["L0_xattn_b_qkv"][0:2 * D], loaded)
                    load_column(sp, bcc, a["L0_xattn_b_ckv"][0:D], loaded)
                    load_row(sp, vrow, a["L0_xattn_b_qkv"][2 * D:3 * D], loaded)
                    load_row(sp, vcrow, a["L0_xattn_b_ckv"][D:2 * D], loaded)
                    nload = 8
                else:
                    sp.dma_start(wf[:, 0, :], a["L1_xattn_Wkf"]).then_inc(wf_loaded, 16)
                    sp.dma_start(wf[:, 1, :], a["L1_xattn_Wqf"]).then_inc(wf_loaded, 16)
                    load_weight(sp, w[:, :, 0:D], a["L1_xattn_Wq"], loaded)
                    load_weight(sp, w[:, :, D:3 * D], a["L1_xattn_Wwin"], loaded)
                    load_weight(sp, wc, a["L1_xattn_Wkv"], loaded)
                    load_column(sp, g, a["L1_xattn_norm_w"], loaded)
                    load_weight(sp, wout, a["L1_xattn_Wout"], loaded)
                    nload = 5

            @block.gpsimd
            def _(pool):
                pool.memset(v1[:], 0.0).then_inc(ready, 1)
                pool.wait_ge(ready, 1)
                pool.memset(v1[:, :, :, DH:DH + 1], 1.0).then_inc(ready, 1)
                if not first:
                    pool.memset(blockd[:], 1.0).then_inc(folded, 1)
                    pool.wait_ge(folded, 1)
                    v = blockd[:].rearrange("p (h d) -> p h d", d=DH)
                    pool.affine_select(out=v, in_=v, compare_op=ALU.is_ge, fill=0.0, base=0,
                                       pattern=[[-DH, P // DH], [0, DH]], channel_multiplier=1).then_inc(folded, 1)
                    pool.wait_ge(folded, 2)
                    pool.affine_select(out=v, in_=v, compare_op=ALU.is_ge, fill=0.0, base=DH - 1,
                                       pattern=[[DH, P // DH], [0, DH]], channel_multiplier=-1).then_inc(folded, 1)

            if not first:
                @block.tensor
                def _(pe):
                    pe.wait_ge(tiled, 1)
                    pe.matmul(banks[:, 0, 0:P], whole[0:DH, 0, 0:P], whole[0:DH, 0, P:2 * P],
                              start=True, stop=True).then_inc(sem("both_ready"), 1)

            @block.vector
            def _(dve):
                dve.memset(nmx[:], UNUSED).then_inc(sem("filled"), 1)
                dve.memset(banks[:, OUT, :], 0.0).then_inc(sem("filled"), 1)
                if not first:
                    dve.wait_ge(wf_loaded, 32)
                    n = P // DH
                    src = wf[:].unsqueeze(2).broadcast_to([DH, 2, n, DH])
                    dve.tensor_copy(whole[0:DH, 0, 0:2 * P].rearrange("p (a n d) -> p a n d", a=2, n=n),
                                    src).then_inc(tiled, 1)
                    dve.wait_ge(sem("both_ready"), 1)
                    dve.wait_ge(folded, 3)
                    dve.tensor_tensor(both[:], banks[:, 0, 0:P], blockd[:], ALU.mult).then_inc(tiled, 1)
        clear(nc, [ready, folded, tiled, wf_loaded, sem("both_ready"), sem("filled")])

        def emptier(token):
            what = token[0]
            if what in ("ring", "shift", "turn", "vals", "out"):
                return "v"
            if what in ("ke", "kc", "qk", "mix"):
                return "s"
            if what == "flip":
                return "vs"[token[2]]
            return None

        def run(b, nxt, following):
            order = attention_tokens(ring_jobs, steps_of, first, b is not None, following)
            names = ("ring_ready", "emptied_v", "emptied_s", "normed", "scores_ready", "probs_ready", "probs_used",
                     "out_copied", "high", "rest", "middle", "low", "max_ready", "shift_loaded", "added",
                     "ctx_ready", "stats", "moments", "spread", "root", "chain", "ones_ready")
            (ring_ready, emptied_v, emptied_s, normed, scores_ready, probs_ready, probs_used, out_copied, high, rest,
             middle, low, max_ready, shift_loaded, added, ctx_ready) = map(sem, names[:16])
            written = [sem("written0"), sem("written1")]
            stacked = [sem(f"stacked{q}") for q in range(NQ)]
            used = [sem(n) for n in names] + stacked + written
            ring = Ring(banks, RING, order, emptier, {"v": emptied_v, "s": emptied_s})

            def slot(q):
                return q % NQ

            shifts = [t[1] for t in order if t[0] == "shift"]
            opening = ("flip", 0, 0) if b is None else None
            turns_to = lambda q, c: ring.emptied(("turn", q, c))

            with nc.Block() as block:
                @block.sync
                def _(sp):
                    def write(u, part, cut):
                        is_q, m = units[u]
                        sp.wait_ge(cut, u + 1)
                        n = T if is_q else KW
                        sp.dma_start((zq if is_q else zk)[nxt, part, m * P:(m + 1) * P, :],
                                     parts[:, u % 2, part, 0:n]).then_inc(written[u % 2], 16)

                    for token in order:
                        what = token[0]
                        if what == "high":
                            write(token[1], 0, high)
                        elif what == "middle":
                            write(token[1], 1, middle)
                            write(token[1], 2, low)
                        elif what == "stack":
                            q = token[1]
                            of = b if q < NQ else nxt
                            if q == NQ:
                                for done in written:
                                    sp.wait_ge(done, 16 * 3)
                            if q >= NQ and b is not None:
                                sp.wait_ge(scores_ready, (q - NQ + 1) * per_quad)
                            rows = slice(slot(q) * QH * DH, (slot(q) + 1) * QH * DH)
                            for dst, z, terms in ((qs, zq, TERMS_Q), (ks, zk, TERMS_K)):
                                for j, part in enumerate(terms):
                                    sp.dma_start(dst[j * DH:(j + 1) * DH, slot(q)],
                                                 z[of, part, rows, :].rearrange("(h d) t -> d h t", d=DH))\
                                        .then_inc(stacked[slot(q)], 16)
                    for q in range(NQ):
                        n = sum(t[0] == "stack" and slot(t[1]) == q for t in order)
                        if n:
                            sp.wait_ge(stacked[q], 16 * 12 * n)
                    if following:
                        for done in written:
                            sp.wait_ge(done, 16 * 6)
                    if b is None:
                        for done, count in arriving:
                            sp.wait_ge(done, count)

                @block.gpsimd
                def _(pool):
                    for token in order:
                        what = token[0]
                        if what == "middle" or what == "high" and b is not None:
                            u = token[1]
                            n = T if units[u][0] else KW
                            part = int(what == "middle")
                            out = parts[:, u % 2, 2, 0:n] if part else whole[:, u % 2, 0:n]
                            pool.wait_ge(middle if part else high, u + 1)
                            if part and u >= 2:
                                pool.wait_ge(written[u % 2], 16 * 3)
                            pool.tensor_tensor(out, whole[:, u % 2, 0:n], parts[:, u % 2, part, 0:n],
                                               ALU.subtract).then_inc(low if part else rest, 1)
                        elif what == "turn" and first and token[2] == NCH - 1:
                            q = token[1]
                            pool.wait_ge(*turns_to(q, NCH - 1))
                            cols = slice(q * QH * DH, (q + 1) * QH * DH)
                            pool.tensor_tensor(x[:, b, :, cols], x[:, b, :, cols], mixed[:, :, cols],
                                               ALU.add).then_inc(added, 1)
                    if b is None:
                        pool.wait_ge(low, len(units))
                        pool.memset(ks[KR:KR + 1], 1.0).then_inc(sem("ones_ready"), 1)

                @block.tensor
                def _(pe):
                    steps = mixed_steps = 0
                    started = set()
                    for token in order:
                        what, *args = token
                        if b is None and what in ("ke", "kc"):
                            pe.wait_ge(loaded, 16 * nload)
                        if emptier(token):
                            ring.wait_free(pe, token)
                            bk = ring.bank(token)
                        if what == "flip":
                            half, k = args
                            pe.wait_ge(normed, 4 * (half + 1))
                            ins = turn_tiles(pe, bk, xh, half, k, ident)
                        elif what == "ke" or what == "kc" and first:
                            m = args[0] if what == "ke" else units[args[0]][1]
                            pe.wait_ge(ctx_ready, 1)
                            for k in range(ND):
                                ins = pe.matmul(bk[:, 0:S], wc[:, k, m * P:(m + 1) * P], ctxb[:, k, :],
                                                start=k == 0, stop=k == ND - 1)
                        elif what == "kc":
                            m = units[args[0]][1]
                            pe.wait_ge(*ring.emptied(("ke", m)))
                            ins = pe.matmul(bk[:, 0:S], both[:], ke[:, m, :], start=True, stop=True)
                        elif what == "qk":
                            u, half = args
                            for k in range(ND):
                                pe.wait_ge(*ring.emptied(("flip", half, k)))
                            is_q, m = units[u]
                            c0 = (0 if is_q else D) + m * P
                            for k in range(ND):
                                ins = pe.matmul(bk, w[:, k, c0:c0 + P], xnT[:, k, half * BANK:(half + 1) * BANK],
                                                start=k == 0, stop=k == ND - 1)
                        elif what == "vals":
                            i, = args
                            rows = S if i < 0 else P
                            for k in range(ND):
                                tokens_, wv = (ctxb[:, k, :], wc[:, k, D:2 * D]) if i < 0 else \
                                    (xnT[:, k, i * P:(i + 1) * P], w[:, k, 2 * D:3 * D])
                                ins = pe.matmul(bk[0:rows, 0:D], tokens_, wv, start=k == 0, stop=k == ND - 1)
                        elif what == "ring":
                            q, h, (tiles, n, i0, piece, pieces) = args
                            if q not in started and (q >= NQ or q >= 2):
                                pe.wait_ge(stacked[slot(q)], 16 * 12 * sum(
                                    t[0] == "stack" and slot(t[1]) == slot(q) and t[1] <= q for t in order))
                            started.add(q)
                            for t, c, key, m, mask in pieces:
                                if mask:
                                    m0, to, mn = mask
                                    pe.matmul(bk[:, to:to + mn], identb[:], mq[:, m0:m0 + mn], start=True,
                                              stop=False, skip_group_check=True)
                                ins = pe.matmul(bk[:, c:c + m], qs[0:KR, slot(q), h, t * P:(t + 1) * P],
                                                ks[0:KR, slot(q), h, key:key + m], start=mask is None, stop=True,
                                                skip_group_check=True)
                        elif what == "shift":
                            q, = args
                            pe.wait_ge(max_ready, shifts.index(q) + 1)
                            ins = pe.transpose(bk[0:QH * NT, 0:P // 2].bitcast(BF16), nmb[:, q % 2, :], identb[:])
                        elif what == "scores":
                            q, c, s, (func, blk, c0, n, mask) = args
                            if c == 0 and s == 0 and q:
                                pe.wait_ge(shift_loaded, 16 * (shifts.index(q) + 1))
                            if steps >= 2:
                                pe.wait_ge(probs_ready, steps - 1)
                            pair = PAIRS[steps % 2]
                            rows = S if blk == 0 else P
                            key = 0 if blk == 0 else S + P * (blk - 1)
                            kr = KR + (func == "exp")
                            for h in range(QH):
                                bk = banks[:, pair + h // 2, h % 2 * CH:(h % 2 + 1) * CH]
                                if mask:
                                    m0, to, mn = mask
                                    pe.matmul(bk[:, to:to + mn], identb[:], mk[:, m0:m0 + mn], start=True, stop=False,
                                              skip_group_check=True)
                                ins = pe.matmul(bk[0:rows, c0:c0 + n], ks[0:kr, slot(q), h, key:key + rows],
                                                qs[0:kr, slot(q), h, c * CH + c0:c * CH + c0 + n],
                                                start=mask is None, stop=True, skip_group_check=True)
                            ins.then_inc(scores_ready, 1)
                            steps += 1
                        elif what == "values":
                            q, c, s, (func, blk, c0, n, mask) = args
                            if s == 0 and (q or c):
                                pe.wait_ge(out_copied, q * NCH + c)
                            if (q, c, s) == (0, 0, 0):
                                pe.wait_ge(*ring.emptied(("vals", NT - 1)))
                            pe.wait_ge(probs_ready, mixed_steps + 1)
                            rows = S if blk == 0 else P
                            lin = func == "square"
                            o0 = (CH if lin else 0) + c0
                            begins = s == (0 if first else 1)
                            for h in range(QH):
                                ins = pe.matmul(banks[32 * h:32 * h + DH + 1, OUT, o0:o0 + n],
                                                v1[0:rows, blk, QH * q + h, :],
                                                probs[0:rows, mixed_steps % 3, h * CH + c0:h * CH + c0 + n],
                                                start=lin or begins, stop=True, skip_group_check=True)
                            ins.then_inc(probs_used, 1)
                            mixed_steps += 1
                        elif what == "turn":
                            q, c = args
                            k = q * NCH + c
                            pe.wait_ge(out_copied, k + 1)
                            for n in range(2 if first else 4):
                                ins = pe.transpose(bk[:, n * P:(n + 1) * P], oT[:, k % 2, n * P:(n + 1) * P], ident[:])
                        elif what == "mix":
                            i, = args
                            if i == 0:
                                pe.wait_ge(*turns_to(NQ - 1, NCH - 1))
                            for k in range(4):
                                ins = pe.transpose(bk[:, k * P:(k + 1) * P], mixed[:, i, k * P:(k + 1) * P], ident[:])
                        elif what == "out":
                            i, = args
                            pe.wait_ge(*ring.emptied(("mix", i)))
                            for k in range(4):
                                ins = pe.matmul(bk[:, 0:D], mixedT[:, i % 2, k, :], wout[:, k, :],
                                                start=k == 0, stop=k == 3)
                        if emptier(token):
                            ins.then_inc(ring_ready, 1)

                @block.scalar
                def _(act):
                    steps = 0
                    for token in order:
                        what, *args = token
                        if token == opening:
                            act.wait_ge(loaded, 16 * nload)
                        if emptier(token) == "s":
                            act.wait_ge(ring_ready, ring.filled(token))
                            bk = ring.bank(token)
                        if what == "root":
                            root_of(act, sem, sd)
                        elif what == "shift":
                            q = token[1]
                            act.wait_ge(*ring.emptied(token))
                            if q >= NQ and b is not None:
                                act.wait_ge(scores_ready, (q - NQ + 1) * per_quad)
                            act.dma_start(qs[KR:KR + 1, slot(q)].rearrange("o h t -> o (h t)"),
                                           nmT[:, q % 2, :]).then_inc(shift_loaded, 16)
                        elif what == "flip" and args[1]:
                            half, k = args
                            dst = xnT[:, k, half * BANK:(half + 1) * BANK]
                            if first:
                                ins = act.activation(dst, bk, ACT.Identity, scale=g[:, k:k + 1], bias=be[:, k:k + 1])
                            else:
                                ins = act.activation(dst, bk, ACT.Copy, scale=g[:, k:k + 1])
                            ins.then_inc(emptied_s, 1)
                        elif what == "ke":
                            act.activation(ke[:, args[0], :], bk[:, 0:S], ACT.Copy).then_inc(emptied_s, 1)
                        elif what in ("kc", "qk"):
                            u = args[0]
                            is_q, m = units[u]
                            if u >= 2:
                                act.wait_ge(low, u - 1)
                            if what == "kc":
                                dst, src, bias = whole[:, u % 2, 0:S], bk[:, 0:S], (bcc if first else None, m)
                            else:
                                o = (0 if is_q else S) + args[1] * BANK
                                dst, src, bias = whole[:, u % 2, o:o + BANK], bk, (bcol if first else None,
                                                                                  2 * (1 - is_q) + m)
                            if first:
                                ins = act.activation(dst, src, ACT.Identity, bias=bias[0][:, bias[1]:bias[1] + 1])
                            else:
                                ins = act.activation(dst, src, ACT.Copy)
                            ins.then_inc(emptied_s, 1)
                        elif what == "mix":
                            i = args[0]
                            if i >= 2:
                                act.wait_ge(ring_ready, ring.filled(("out", i - 2)))
                            act.activation(mixedT[:, i % 2].rearrange("p k c -> p (k c)"), bk,
                                           ACT.Copy).then_inc(emptied_s, 1)
                        elif what == "scores":
                            q, c, s, (func, blk, c0, n, mask) = args
                            act.wait_ge(scores_ready, steps + 1)
                            if steps >= 3:
                                act.wait_ge(probs_used, steps - 2)
                            rows = S if blk == 0 else P
                            pair = PAIRS[steps % 2]
                            src = banks[0:rows, pair:pair + 2, :].rearrange("p a (g n) -> p (a g) n", g=2)[:, :, c0:c0 + n]
                            dst = probs[0:rows, steps % 3, :].rearrange("p (h n) -> p h n", h=QH)[:, :, c0:c0 + n]
                            if func == "exp":
                                ins = act.activation(dst, src, ACT.Exp, scale=DH ** -0.5)
                            else:
                                ins = act.activation(dst, src, ACT.Square, scale=0.5, bias=1.0)
                            ins.then_inc(probs_ready, 1)
                            steps += 1
                        elif what == "values" and args[2] == len(steps_of(args[1])) - 1:
                            q, c = args[0:2]
                            k = q * NCH + c
                            act.wait_ge(probs_used, q * per_quad + sum(len(steps_of(j)) for j in range(c + 1)))
                            if k >= 2:
                                act.wait_ge(ring_ready, ring.filled(("turn", (k - 2) // NCH, (k - 2) % NCH)))
                            wd = CH if first else 2 * CH
                            act.activation(oT[:, k % 2, 0:wd], banks[:, OUT, 0:wd], ACT.Copy).then_inc(out_copied, 1)
                    if shifts:
                        act.wait_ge(shift_loaded, 16 * len(shifts))

                @block.vector
                def _(dve):
                    chain = Chain(dve, sem("chain"))
                    for token in order:
                        what, *args = token
                        if token == opening:
                            dve.wait_ge(loaded, 16 * nload)
                        if emptier(token) == "v":
                            dve.wait_ge(ring_ready, ring.filled(token))
                            bk = ring.bank(token)
                        if what == "stats":
                            take_stats(dve, sem, lambda i: x[:, nxt, i, :], st, args)
                        elif what == "spread":
                            take_spread(dve, sem, st, mv, sd, chain, eps, first)
                        elif what == "norm":
                            normalise_tiles(dve, sem, lambda i: x[:, nxt, i, :], lambda i: xh[:, i, :], mv, sd, chain,
                                            normed, first, tiles=args)
                        elif what == "context":
                            if b is not None:
                                dve.wait_ge(*ring.emptied(("vals", -1)))
                            dve.tensor_copy(ctxb[:], ctxT[:, nxt]).then_inc(ctx_ready, 1)
                        elif what == "flip" and not args[1]:
                            half, k = args
                            dst = xnT[:, k, half * BANK:(half + 1) * BANK]
                            if first:
                                ins = dve.tensor_scalar(dst, bk, g[:, k:k + 1], be[:, k:k + 1], ALU.mult, ALU.add)
                            else:
                                ins = dve.tensor_scalar(dst, bk, g[:, k:k + 1], None, ALU.mult)
                            ins.then_inc(emptied_v, 1)
                        elif what == "vals":
                            i, = args
                            rows = S if i < 0 else P
                            dst = v1[0:rows, 1 + i, :, 0:DH]
                            src = bk[0:rows, 0:D].rearrange("p (h d) -> p h d", d=DH)
                            if first:
                                row = (vcrow if i < 0 else vrow)[0:rows, :].rearrange("p (h d) -> p h d", d=DH)
                                ins = dve.tensor_tensor(dst, src, row, ALU.add)
                            else:
                                ins = dve.tensor_copy(dst, src)
                            ins.then_inc(emptied_v, 1)
                        elif what == "high":
                            u, = args
                            n = T if units[u][0] else KW
                            for half in range(2):
                                dve.wait_ge(*ring.emptied(("qk", u, half)))
                            if u >= 2:
                                dve.wait_ge(written[u % 2], 16 * 3)
                            dve.tensor_copy(parts[:, u % 2, 0, 0:n], whole[:, u % 2, 0:n]).then_inc(high, 1)
                            if b is None:
                                dve.wait_ge(high, u + 1)
                                dve.tensor_tensor(whole[:, u % 2, 0:n], whole[:, u % 2, 0:n],
                                                  parts[:, u % 2, 0, 0:n], ALU.subtract).then_inc(rest, 1)
                        elif what == "middle":
                            u, = args
                            n = T if units[u][0] else KW
                            dve.wait_ge(rest, u + 1)
                            dve.tensor_copy(parts[:, u % 2, 1, 0:n], whole[:, u % 2, 0:n]).then_inc(middle, 1)
                        elif what == "ring":
                            q, h, (tiles, n, i0, piece, pieces) = args
                            dst = nmx[:, q % 2, h * NT + i0:h * NT + i0 + tiles, piece]
                            src = bk[:, 0:tiles * n].rearrange("p (t n) -> p t n", t=tiles)
                            dve.tensor_reduce(dst, src, AX.X, ALU.max, negate=True).then_inc(emptied_v, 1)
                            if h == QH - 1 and pieces == ring_jobs[-1][4]:
                                dve.wait_ge(*ring.emptied(token))
                                dve.tensor_reduce(nmb[:, q % 2, :], nmx[:, q % 2], AX.X, ALU.min).then_inc(max_ready, 1)
                        elif what == "shift":
                            q, = args
                            if shifts.index(q) >= 2:
                                dve.wait_ge(shift_loaded, 16 * (shifts.index(q) - 1))
                            dve.tensor_copy(nmT[:, q % 2, :], bk[0:QH * NT, 0:P // 2].bitcast(BF16))\
                               .then_inc(emptied_v, 1)
                        elif what == "turn":
                            q, c = args
                            nt = 1 if first else 2
                            tv = bk[:, 0:nt * 2 * P].rearrange("p (w i h d) -> p w i h d", w=nt, i=2, h=QH)
                            for linear in range(nt):
                                s_ = tv[:, linear, :, :, DH]
                                if linear:
                                    chain(dve.tensor_scalar(den[:, c % 2], s_, 1e-6, None, ALU.add))
                                    s_ = den[:, c % 2]
                                chain(dve.reciprocal(rcp[:, c % 2, linear], s_))
                                c0 = (D if not first and not linear else 0) + q * QH * DH
                                dst = mixed[:, 2 * c:2 * c + 2, c0:c0 + QH * DH].rearrange("p i (h d) -> p i h d", d=DH)
                                ins = dve.tensor_tensor(dst, tv[:, linear, :, :, 0:DH],
                                                        rcp[:, c % 2, linear].unsqueeze(3).broadcast_to([P, 2, QH, DH]), ALU.mult)
                                if linear < nt - 1:
                                    chain(ins)
                            ins.then_inc(emptied_v, 1)
                        elif what == "out":
                            i, = args
                            dve.tensor_tensor(x[:, b, i, :], bk[:, 0:D], x[:, b, i, :], ALU.add).then_inc(emptied_v, 1)
            clear(nc, used)
            if b is None:
                clear(nc, [loaded] + [done for done, _ in arriving])

        run(None, 0, True)
        with nc.Fori(0, B - 1) as b:
            run(b, b + 1, True)
        run(B - 1, None, False)


def mlp_tokens(this, following):
    nf = FF // P
    timed = []
    if this:
        timed += [(f, ("up", f, 0)) for f in range(nf)] + [(8.5 + 1.5 * f, ("up", f, 1)) for f in range(nf)]
        timed += [(11.3 + 3 * i, ("down", i)) for i in range(NT // 2)]
        timed += [(22 + i, ("down", NT // 2 + i)) for i in range(NT // 2)]
    if following:
        for time, (stats, norm) in enumerate(((-0.5, 4.5), (6.6, 10.6))):
            timed += [(stats + i / 2, ("stats", time, i)) for i in range(NT)]
            timed += [(norm - 0.3, ("spread", time)), (norm - 0.2, ("root", time))]
            timed += [(norm + i / 2, ("norm", time, i)) for i in range(NT)]
        for n, t in enumerate((16.6, 17.6, 20.6, 22.6)):
            timed.append((t, ("turn", n // ND, n % ND)))
    return [token for _, token in sorted(timed, key=lambda step: step[0])]


def mlp(nc, a, sem, sb, x, ident, banks):
    nf = FF // P
    with ExitStack() as own:
        w1 = sb(own, "w1", [P, 2, ND, FF], F32R)
        w2 = sb(own, "w2", [P, 2, nf, D], F32R)
        g2, be2, b2 = (sb(own, n, [P, D]) for n in ("g2", "be2", "b2"))
        gf, bf, b1 = sb(own, "gf", [P, ND]), sb(own, "bf", [P, ND]), sb(own, "b1", [P, nf])
        xh = sb(own, "xh_mlp", [P, NT, D])
        xnT = sb(own, "xnT_mlp", [P, 2, ND, T], F32R)
        full = sb(own, "full", [P, 3, BANK])
        st, mv, sd = ([sb(own, f"{n}_mlp{time}", [P, *shape]) for time in range(2)]
                      for n, shape in (("st", (NT, 6)), ("mv", (NT, 2)), ("sd", (3, NT))))
        loaded = sem("loaded")
        def emptier(token):
            return {"turn": "s", "up": "s", "down": "v"}.get(token[0])

        def run(b, nxt, following):
            order = mlp_tokens(b is not None, following)
            names = ("ring_ready", "emptied_v", "emptied_s", "normed", "scaled", "shifted", "added", "wholes", "lows",
                     "stats", "moments", "spread", "root", "chain", "rounded")
            ring_ready, emptied_v, emptied_s, normed, scaled, shifted, added, wholes, lows = map(sem, names[:9])
            ring = Ring(banks, range(8), order, emptier, {"v": emptied_v, "s": emptied_s})
            cut = [token for token in order if emptier(token) == "s"]

            def split_of(token):
                what, *args = token
                half, n = (args[0], args[1]) if what == "turn" else (args[1], args[0])
                return (xnT if what == "turn" else hT)[:, :, n, half * BANK:(half + 1) * BANK]

            with nc.Block() as block:
                @block.gpsimd
                def _(pool):
                    for token in order:
                        if b is None and token == ("norm", 0, 0):
                            pool.wait_ge(loaded, 16 * 8)
                        if token[:2] == ("norm", 0):
                            i = token[2]
                            pool.wait_ge(normed, i + 1)
                            pool.tensor_tensor(xh[:, i, :], xh[:, i, :], g2[:], ALU.mult).then_inc(scaled, 1)
                            pool.wait_ge(scaled, i + 1)
                            pool.tensor_tensor(xh[:, i, :], xh[:, i, :], be2[:], ALU.add).then_inc(shifted, 1)
                        elif token == ("up", 0, 0):
                            for i in range(NT):
                                pool.tensor_tensor(x[:, b, i, :], x[:, b, i, :], b2[:], ALU.add).then_inc(added, 1)

                @block.tensor
                def _(pe):
                    for token in order:
                        what, *args = token
                        if not emptier(token):
                            continue
                        ring.wait_free(pe, token)
                        bk = ring.bank(token)
                        if what == "turn":
                            half, k = args
                            pe.wait_ge(normed, NT + 4 * (half + 1))
                            ins = turn_tiles(pe, bk, xh, half, k, ident)
                        elif what == "up":
                            f, half = args
                            ins = products(pe, bk, [(w1[:, :, k, f * P:(f + 1) * P],
                                                     xnT[:, :, k, half * BANK:(half + 1) * BANK]) for k in range(ND)])
                        else:
                            i, = args
                            pe.wait_ge(lows, cut.index(("up", nf - 1, i // 4)) + 1)
                            ins = products(pe, bk[:, 0:D], [(hT[:, :, f, i * P:(i + 1) * P], w2[:, :, f, :])
                                                            for f in range(nf)])
                        ins.then_inc(ring_ready, 1)

                @block.scalar
                def _(act):
                    for token in order:
                        what, *args = token
                        if what == "root":
                            root_of(act, sem, sd[args[0]], args[0])
                        if emptier(token) != "s":
                            continue
                        if b is None:
                            act.wait_ge(loaded, 16 * 8)
                        act.wait_ge(ring_ready, ring.filled(token))
                        bk = ring.bank(token)
                        n = cut.index(token)
                        if n >= 3:
                            act.wait_ge(lows, n - 2)
                        for dst, done in ((full[:, n % 3, :], wholes), (split_of(token)[:, 0], emptied_s)):
                            if what == "turn":
                                k = args[1]
                                ins = act.activation(dst, bk, ACT.Identity, scale=gf[:, k:k + 1], bias=bf[:, k:k + 1])
                            else:
                                f = args[0]
                                ins = act.activation(dst, bk, ACT.Gelu, bias=b1[:, f:f + 1])
                            ins.then_inc(done, 1)

                @block.vector
                def _(dve):
                    chain = Chain(dve, sem("chain"))
                    for token in order:
                        what, *args = token
                        if emptier(token) == "v":
                            dve.wait_ge(ring_ready, ring.filled(token))
                            bk = ring.bank(token)
                        if what in ("stats", "spread", "norm"):
                            time = args[0]
                            xin = (lambda i: xh[:, i, :]) if time else (lambda i: x[:, nxt, i, :])
                            if what == "stats":
                                if time:
                                    dve.wait_ge(shifted, args[1] + 1)
                                take_stats(dve, sem, xin, st[time], args[1:])
                            elif what == "spread":
                                take_spread(dve, sem, st[time], mv[time], sd[time], chain, 1e-5, True, time)
                            else:
                                normalise_tiles(dve, sem, xin, lambda i: xh[:, i, :], mv[time], sd[time], chain, normed,
                                                True, time, args[1:])
                        elif emptier(token) == "s":
                            n = cut.index(token)
                            dve.wait_ge(wholes, n + 1)
                            dve.wait_ge(*ring.emptied(token))
                            dst = split_of(token)
                            dve.tensor_tensor(dst[:, 1], full[:, n % 3, :], dst[:, 0].bitcast(F32), ALU.subtract)\
                                .then_inc(lows, 1)
                        elif what == "down":
                            i, = args
                            dve.wait_ge(added, i + 1)
                            dve.tensor_tensor(x[:, b, i, :], bk[:, 0:D], x[:, b, i, :], ALU.add).then_inc(emptied_v, 1)
                    if b is None:
                        dve.wait_ge(loaded, 16 * 8)
                        split_weights(dve, ((w1, whole1), (w2, whole2)), sem("rounded"))
            clear(nc, [sem(n) for n in names])
            if b is None:
                clear(nc, [loaded])

        with ExitStack() as setting_up:
            whole1, whole2 = sb(setting_up, "whole1", [P, ND, FF]), sb(setting_up, "whole2", [P, nf, D])
            with nc.Block() as block:
                @block.sync
                def _(sp):
                    for tile, name in ((g2, "g2"), (be2, "be2"), (b2, "b2")):
                        load_row(sp, tile, a["L0_xattn_" + name], loaded)
                    for tile, name in ((gf, "gf"), (bf, "bf"), (b1, "b1")):
                        load_column(sp, tile, a["L0_xattn_" + name], loaded)
                    load_weight(sp, whole1, a["L0_xattn_w1"], loaded)
                    load_weight(sp, whole2, a["L0_xattn_w2"], loaded)
            run(None, 0, True)
        hT = sb(own, "hT", [P, 2, nf, T], F32R)
        with nc.Fori(0, B - 1) as b:
            run(b, b + 1, True)
        run(B - 1, None, False)


def context_schedule(last, this, following, closing):
    nu = 2 * NT
    pe, dve, act, pool = [], [], [], []

    def filled(time, token, engine):
        pe.append((time, token))
        if "v" in engine:
            dve.append((time + (0.6 if last else 0.2), token))
        if "s" in engine:
            act.append((time, token))
        if "p" in engine:
            pool.append((time + 0.1, token))

    if this:
        for n in range(nu):
            pe.append((n - (0.75 if last else 1.25), ("scores", n)))
            act.append((n + (0.5 if last else 1.5), ("exp", n)))
            dve.append((n + (1.2 if last else 2.3), ("invert", n)))
            pool.append((n + (1.5 if last else 3), ("weigh", n)))
            if last:
                dve.append((n, ("shift", n)))
            else:
                dve += [(n, ("take", n)), (n + 1.1, ("shift", n))]
                pool.append((n, ("mask", n)))
                if n % 2 == 0:
                    act.append((n - 2.4, ("lower", n // 2)))
        for c in range(VW_JOBS):
            filled((1.2, 1.4, 1.6, 3.2, 3.4)[c], ("vw", c), "sv" if last else "sv"[c % 2])
        for i in range(NT):
            for j in range(3):
                filled(2 * i + (5.1 if last else 4.75) + j / 10, ("turned", i, j), "sp" if last else "s")
            pe += [(2 * i + (7.25 if last else 6.9), ("out", i, 0)), (2 * i + 8.05, ("out", i, 1))]
            dve.append((2 * i + (8.85 if last else 9.1), ("out", i)))
    if closing:
        dve += [(1.5 + i / 2, ("stats", i)) for i in range(NT)] + [(5.7, ("spread",))]
        act.append((6.2, ("root",)))
        dve += [(7.5 + i / 2, ("norm", i)) for i in range(NT)]
        dve += [(8.5 + i / 2, ("close", i)) for i in range(NT)]
    if following:
        dve.append((4.0, ("context",)))
        if last:
            dve += [(1.5 + i / 2, ("stats", i)) for i in range(NT)] + [(5.7, ("spread",))]
            act.append((6.2, ("root",)))
            dve += [(7.5 + i / 2, ("norm", i)) for i in range(NT)]
            for n in range(2):
                filled(8.05 + 2 * n, ("k", n), "v")
                filled(12.05 + 2 * n, ("v", n), "v")
            for n, (half, k) in enumerate((half, k) for half in range(2) for k in range(ND)):
                filled(15.2 + n / 10, ("turn", half, k), "sv")
            for n, (kk, pp) in enumerate((kk, pp) for kk in range(ND) for pp in range(4)):
                filled((15.6, 15.7, 17.5, 17.6, 18.5, 18.6, 20.1, 20.2)[n], ("fold", kk, pp), "sv")
        else:
            act += [(2.2 + i, ("copy", i)) for i in range(4)]
            pool += [(6.2 + i, ("bias", i)) for i in range(NT)]
            for n, (half, k) in enumerate((half, k) for half in range(2) for k in range(ND)):
                filled(8.05 + 2 * n, ("turn", half, k), "sv"[k])
            filled(6.05, ("v", 0), "v")
            filled(15.2, ("k", 0), "v")
            for n, (half, m) in enumerate((half, m) for half in range(2) for m in range(ND)):
                filled((15.6, 17.5, 18.5, 20.1)[n], ("q", m, half), "s")
    return {name: [token for _, token in sorted(steps, key=lambda step: step[0])]
            for name, steps in (("pe", pe), ("dve", dve), ("act", act), ("pool", pool))}


def context_attention(nc, a, sem, sb, x, ident, ctxT, banks, last, result):
    dk = 64 if last else DH
    hk = P // dk
    nk = H // hk
    wk_ = hk * S
    nu = 2
    UH = H // nu
    UW = UH * S
    npc = -(-HS // P)
    prefix = "L3_xattn_" if last else "L2_xattn_"
    weights = {k[len(prefix):].lower(): v for k, v in a.items() if k.startswith(prefix)}
    per = 4 if last else 2
    units = [(i, m) for i in range(NT) for m in range(nu)]
    nbuf = 4
    nfull = 4
    ne = 2 if last else 1
    with ExitStack() as own:
        n_ = lambda s: f"{s}_ctx{int(last)}"
        wq = sb(own, n_("wq"), [P, nk if last else ND, D])
        wk = sb(own, n_("wk"), [P, ND, nk * P])
        wv = sb(own, n_("wv"), [P, ND, nk * P])
        wo = sb(own, n_("wo"), [P, nk, D])
        xh = sb(own, n_("xh"), [P, NT, D])
        xT = sb(own, n_("xT"), [P, ne, ND, T], F32R if last else F32)
        ctxb = sb(own, n_("ctxb"), [P, ND, S])
        kbd = sb(own, n_("kbd"), [P, nk, wk_])
        vbd = sb(own, n_("vbd"), [P, nk, wk_ + 2 * P])
        vw = sb(own, n_("vw"), [P, ne, npc, D], F32R if last else F32)
        pr = sb(own, n_("pr"), [P, nbuf, npc * P])
        pT = sb(own, n_("pT"), [P, ne, 2, npc, P], F32R if last else F32)
        st, mv, sd = sb(own, n_("st"), [P, NT, 6]), sb(own, n_("mv"), [P, NT, 2]), sb(own, n_("sd"), [P, 3, NT])
        top = sb(own, n_("top"), [P, 2, UH])
        tot = sb(own, n_("tot"), [P, 2, UH])
        inv = sb(own, n_("inv"), [P, 4, UH])
        if last:
            g = sb(own, n_("g"), [P, ND])
            full = sb(own, n_("full"), [P, nfull, BANK])
            fold = sb(own, n_("fold"), [P, 2, ND, HS], F32R)
        else:
            fs = sb(own, n_("fs"), [P, nbuf, HS])
            mk = sb(own, n_("mk"), [P, nbuf, HS], U8)
            low = sb(own, n_("low"), [P, nbuf, HS])
            qT = sb(own, n_("qT"), [P, ND, T])
            bq, bk_, bv = (sb(own, n_(n), [P, ND]) for n in ("bq", "bk", "bv"))
            bo, gamma, beta = (sb(own, n_(n), [P, D]) for n in ("bo", "gamma", "beta"))
            heads = sb(own, n_("heads"), [P, UH])
            kv = sb(own, n_("kv"), [P, 2, ND, S])
        loaded, ready = sem("loaded"), sem("const_ready")
        nload = 5 if last else 10
        with nc.Block() as block:
            @block.sync
            def _(sp):
                load_weight(sp, wq, weights["wq"], loaded)
                load_weight(sp, wk, weights["wk"], loaded)
                load_weight(sp, wv, weights["wv"], loaded)
                load_weight(sp, wo, weights["wo"], loaded)
                if last:
                    load_column(sp, g, weights["norm_w"], loaded)
                else:
                    for tile, name in ((bq, "bq"), (bk_, "bk"), (bv, "bv")):
                        load_column(sp, tile, weights[name], loaded)
                    for tile, name in ((bo, "bo"), (gamma, "gamma"), (beta, "beta")):
                        load_row(sp, tile, weights[name], loaded)

            @block.gpsimd
            def _(pool):
                pool.memset(pr[:], 0.0).then_inc(ready, 1)
                pool.memset(vbd[:], 0.0).then_inc(ready, 1)
                pool.memset(kbd[:], 0.0).then_inc(ready, 1)
                if not last:
                    pool.memset(heads[:], 1.0).then_inc(ready, 1)
                    pool.wait_ge(ready, 4)
                    pool.affine_select(out=heads[:], in_=heads[:], compare_op=ALU.is_ge, fill=0.0, base=0,
                                       pattern=[[-dk, UH]], channel_multiplier=1).then_inc(ready, 1)
                    pool.wait_ge(ready, 5)
                    pool.affine_select(out=heads[:], in_=heads[:], compare_op=ALU.is_ge, fill=0.0, base=dk - 1,
                                       pattern=[[dk, UH]], channel_multiplier=-1).then_inc(ready, 1)
        clear(nc, [ready])

        def emptier(token):
            what = token[0]
            if not last and what in ("turn", "vw"):
                return "sv"[token[-1] % 2]
            return {"turned": "s", "q": "s", "turn": "v", "fold": "v", "vw": "v", "k": "v", "v": "v"}.get(what)

        def is_split(token):
            return last and token[0] in ("vw", "fold", "turn")

        def full_of(token):
            return (3 * token[1] + token[2]) % nfull

        def split_of(token):
            what, *args = token
            if what == "turned":
                i, j = args
                n = len(chunks_of(j))
                return pT[:, :, i % 2, 4 * j:4 * j + n, :].rearrange("p e c t -> p e (c t)"), n * P, 1.0
            if what == "vw":
                c = 2 * args[0]
                return vw[:, :, c:c + 2, :].rearrange("p e c d -> p e (c d)"), 2 * D, 1.0
            if what == "turn":
                half, k = args
                return xT[:, :, k, half * BANK:(half + 1) * BANK], BANK, 1.0
            kk, pp = args
            return fold[:, :, kk, 2 * wk_ * pp:2 * wk_ * (pp + 1)], 2 * wk_, g[:, kk:kk + 1]

        def half_of(tile, m):
            return tile[:, m * UW:(m + 1) * UW]

        def by_head(ap):
            return ap.rearrange("p (h s) -> p h s", s=S)

        def two(ap):
            return ap.rearrange("p (a c) -> p a c", a=2)

        def in_banks(n):
            r = 2 * (n % 2)
            return banks[:, r:r + 2, 0:UW // 2]

        def out_of(i):
            return banks[:, 6 + i % 2, 0:D]

        def chunks_of(j):
            return range(4 * j, min(4 * j + 4, npc))

        def run(b, nxt, following, closing):
            plan = context_schedule(last, b is not None, following, not last and closing is not None)
            names = ("ring_ready", "emptied_v", "emptied_s", "normed", "scored", "taken", "masked", "lowered",
                     "shifted", "exped", "inverted", "weighted", "outs_ready", "rounded", "wholes", "lows", "added", "biased", "copied", "scaled", "closed",
                     "ctx_ready", "stats", "moments", "spread", "root", "chain")
            (ring_ready, emptied_v, emptied_s, normed, scored, taken, masked, lowered, shifted, exped, inverted,
             weighted, outs_ready, rounded, wholes, lows, added, biased, copied, scaled, closed, ctx_ready) = map(sem, names[:22])
            side = [sem(f"side{n}") for n in range(nbuf)]
            ring = Ring(banks, (4, 5), plan["pe"], emptier, {"v": emptied_v, "s": emptied_s})
            splits = [token for token in plan["act"] if is_split(token)]

            with nc.Block() as block:
                if not last and b is not None:
                    @block.sync
                    def _(sp):
                        for i in range(NT):
                            if i >= nbuf:
                                sp.wait_ge(taken, 2 * (i - nbuf + 1))
                                sp.wait_ge(lowered, i - nbuf + 1)
                            sp.dma_start(fs[:, i % nbuf, :], a["fside"][b, i * P:(i + 1) * P, :]).then_inc(side[i % nbuf], 16)
                            sp.dma_start(mk[:, i % nbuf, :], a["mask"][b, i * P:(i + 1) * P, :]).then_inc(side[i % nbuf], 16)
                        for done in side:
                            sp.wait_ge(done, 32 * NT // nbuf)

                if last and closing is not None:
                    @block.sync
                    def _(sp):
                        sp.dma_start(result[closing].rearrange("(i p) d -> p i d", p=P), x[:, closing])\
                            .then_inc(sem("stored"), 16)
                        sp.wait_ge(sem("stored"), 16)

                @block.gpsimd
                def _(pool):
                    for what, *args in plan["pool"]:
                        if what == "mask":
                            n, = args
                            i, m = units[n]
                            pool.wait_ge(taken, n + 1)
                            s_ = half_of(pr[:, i % nbuf, :], m)
                            pool.wait_ge(lowered, i + 1)
                            pool.tensor_tensor(s_, s_, half_of(low[:, i % nbuf, :], m), ALU.add).then_inc(masked, 1)
                        elif what == "weigh":
                            n, = args
                            i, m = units[n]
                            pool.wait_ge(inverted, n + 1)
                            s_ = by_head(half_of(pr[:, i % nbuf, :], m))
                            pool.tensor_tensor(s_, s_, inv[:, n % 4, :].unsqueeze(2).broadcast_to([P, UH, S]),
                                               ALU.mult).then_inc(weighted, 1)
                        elif what == "turned":
                            token = (what, *args)
                            pool.wait_ge(*ring.emptied(token))
                            dst, n, _ = split_of(token)
                            pool.tensor_tensor(dst[:, 1], full[:, full_of(token), 0:n], dst[:, 0].bitcast(F32),
                                               ALU.subtract).then_inc(lows, 1)
                        elif what == "bias":
                            i, = args
                            if b is None:
                                pool.wait_ge(loaded, 16 * nload)
                            pool.wait_ge(copied, i // 2 + 1)
                            pool.tensor_tensor(x[:, nxt, i, :], x[:, nxt, i, :], bo[:], ALU.add).then_inc(biased, 1)

                @block.tensor
                def _(pe):
                    for token in plan["pe"]:
                        what, *args = token
                        if b is None and what in ("k", "v", "fold", "q"):
                            pe.wait_ge(loaded, 16 * nload)
                        if what == "scores":
                            n, = args
                            i, m = units[n]
                            if n >= 2:
                                pe.wait_ge(taken, n - 1)
                            for j in range(2):
                                dst = banks[:, 2 * (n % 2) + j, 0:UW // 2]
                                if last:
                                    c0 = m * UW + j * UW // 2
                                    ins = products(pe, dst, [(xT[:, :, k, i * P:(i + 1) * P],
                                                              fold[:, :, k, c0:c0 + UW // 2]) for k in range(ND)])
                                else:
                                    ins = pe.matmul(dst, qT[:, m, i * P:(i + 1) * P],
                                                    kbd[:, m, j * UW // 2:(j + 1) * UW // 2], start=True, stop=True)
                            ins.then_inc(scored, 1)
                            continue
                        if what == "out":
                            i, part = args
                            if part == 0:
                                for c in range(VW_JOBS):
                                    pe.wait_ge(*ring.emptied(("vw", c)))
                                if i >= 2:
                                    pe.wait_ge(added, i - 1)
                            for c in (range(3, npc) if part else range(3)):
                                if c % 4 == 0:
                                    pe.wait_ge(*((lows, 3 * i + c // 4 + 1) if last else
                                                 ring.emptied(("turned", i, c // 4))))
                                terms = PARTS[:1 if ne == 1 else None]
                                for term in terms:
                                    ins = pe.matmul(out_of(i), pT[:, term[0], i % 2, c, :], vw[:, term[1], c, :],
                                                    start=c == 0 and term == terms[0],
                                                    stop=c == npc - 1 and term == terms[-1])
                            if part:
                                ins.then_inc(outs_ready, 1)
                            continue
                        ring.wait_free(pe, token)
                        bk = ring.bank(token)
                        if what == "turned":
                            i, j = args
                            pe.wait_ge(weighted, 2 * (i + 1))
                            for c in chunks_of(j):
                                ins = pe.transpose(bk[:, c % 4 * P:(c % 4 + 1) * P],
                                                   pr[:, i % nbuf, c * P:(c + 1) * P], ident[:])
                        elif what == "turn":
                            half, k = args
                            pe.wait_ge(*((normed, 4 * (half + 1)) if last else (copied, 2 * (half + 1))))
                            ins = turn_tiles(pe, bk, xh, half, k, ident)
                        elif what in ("k", "v"):
                            w = wk if what == "k" else wv
                            pe.wait_ge(ctx_ready, 1)
                            for j in range(per):
                                m = args[0] * per + j
                                for k in range(ND):
                                    ins = pe.matmul(bk[:, j * S:(j + 1) * S], w[:, k, m * P:(m + 1) * P], ctxb[:, k, :],
                                                    start=k == 0, stop=k == ND - 1)
                        elif what == "fold":
                            kk, pp = args
                            pe.wait_ge(*ring.emptied(("k", pp // 2)))
                            for j in range(2):
                                p_ = 2 * pp + j
                                ins = pe.matmul(bk[:, j * wk_:(j + 1) * wk_], wq[:, p_, kk * P:(kk + 1) * P], kbd[:, p_, :],
                                                start=True, stop=True)
                        elif what == "q":
                            m, half = args
                            for k in range(ND):
                                pe.wait_ge(*ring.emptied(("turn", half, k)))
                            for k in range(ND):
                                ins = pe.matmul(bk, wq[:, k, m * P:(m + 1) * P], xT[:, 0, k, half * BANK:(half + 1) * BANK],
                                                start=k == 0, stop=k == ND - 1)
                        elif what == "vw":
                            for j in range(2):
                                c = 2 * args[0] + j
                                over = [m for m in range(nk) if m * wk_ < (c + 1) * P and (m + 1) * wk_ > c * P]
                                for m in over:
                                    at = P + c * P - m * wk_
                                    ins = pe.matmul(bk[:, j * D:(j + 1) * D], vbd[:, m, at:at + P], wo[:, m, :],
                                                    start=m == over[0], stop=m == over[-1])
                        ins.then_inc(ring_ready, 1)

                @block.scalar
                def _(act):
                    for token in plan["act"]:
                        what, *args = token
                        if what == "root":
                            root_of(act, sem, sd)
                            continue
                        if what == "copy":
                            two_tiles = slice(2 * args[0], 2 * args[0] + 2)
                            act.activation(xh[:, two_tiles], x[:, nxt, two_tiles], ACT.Copy).then_inc(copied, 1)
                            continue
                        if what == "lower":
                            i, = args
                            act.wait_ge(side[i % nbuf], 32 * (i // nbuf + 1))
                            if i >= nbuf:
                                act.wait_ge(masked, 2 * (i - nbuf + 1))
                            act.activation(low[:, i % nbuf, :], mk[:, i % nbuf, :], ACT.Copy, scale=MASKED)\
                                .then_inc(lowered, 1)
                            continue
                        if what == "exp":
                            n, = args
                            i, m = units[n]
                            act.wait_ge(taken if last else shifted, n + 1)
                            s_ = half_of(pr[:, i % nbuf, :], m)
                            act.activation(s_, s_, ACT.Exp, scale=1.0 if last else DH ** -0.5).then_inc(exped, 1)
                            continue
                        if b is None:
                            act.wait_ge(loaded, 16 * nload)
                        act.wait_ge(ring_ready, ring.filled(token))
                        bk = ring.bank(token)
                        if what == "turned" and args[0] >= 2 and args[1] == 0:
                            act.wait_ge(outs_ready, args[0] - 1)
                        if is_split(token):
                            dst, n, factor = split_of(token)
                            act.activation(dst[:, 0], bk[:, 0:n], ACT.Copy, scale=factor).then_inc(rounded, 1)
                            continue
                        if what in ("turned", "turn", "vw"):
                            dst, n, _ = split_of(token)
                            if what == "turned" and last:
                                k = 3 * args[0] + args[1]
                                if k >= nfull:
                                    act.wait_ge(lows, k - nfull + 1)
                                act.activation(full[:, full_of(token), 0:n], bk[:, 0:n], ACT.Copy).then_inc(wholes, 1)
                            ins = act.activation(dst[:, 0], bk[:, 0:n], ACT.Copy)
                        elif what == "q":
                            m, half = args
                            ins = act.activation(qT[:, m, half * BANK:(half + 1) * BANK], bk, ACT.Identity,
                                                 bias=bq[:, m:m + 1])
                        ins.then_inc(emptied_s, 1)

                @block.vector
                def _(dve):
                    chain = Chain(dve, sem("chain"))
                    for token in plan["dve"]:
                        what, *args = token
                        if what == "context":
                            dve.tensor_copy(ctxb[:], ctxT[:, nxt]).then_inc(ctx_ready, 1)
                        elif what in ("stats", "spread", "norm"):
                            at = nxt if last else closing
                            xin = lambda i: x[:, at, i, :]
                            if what == "stats":
                                take_stats(dve, sem, xin, st, args)
                            elif what == "spread":
                                take_spread(dve, sem, st, mv, sd, chain, 1e-6 if last else 1e-5, not last)
                            elif last:
                                normalise_tiles(dve, sem, xin, lambda i: xh[:, i, :], mv, sd, chain, normed, False,
                                                tiles=args)
                            else:
                                i, = args
                                if i == 0:
                                    dve.wait_ge(sem("root"), 1)
                                    chain(dve.reciprocal(sd[:, 2, :], sd[:, 1, :]))
                                dve.scalar_tensor_tensor(xin(i), xin(i), mv[:, i, 0:1], gamma[:], ALU.subtract,
                                                         ALU.mult).then_inc(scaled, 1)
                        elif what == "close":
                            i, = args
                            dve.wait_ge(scaled, i + 1)
                            dve.scalar_tensor_tensor(x[:, closing, i, :], x[:, closing, i, :], sd[:, 2, i:i + 1], beta[:],
                                                     ALU.mult, ALU.add).then_inc(closed, 1)
                        elif what == "take":
                            n, = args
                            i, m = units[n]
                            dve.wait_ge(scored, n + 1)
                            dve.wait_ge(side[i % nbuf], 32 * (i // nbuf + 1))
                            if i >= nbuf:
                                dve.wait_ge(ring_ready, ring.filled(("turned", i - nbuf, 2)))
                            dve.tensor_tensor(two(half_of(pr[:, i % nbuf, :], m)), in_banks(n),
                                              two(half_of(fs[:, i % nbuf, :], m)), ALU.mult).then_inc(taken, 1)
                        elif what == "shift" and last:
                            n, = args
                            i, m = units[n]
                            dve.wait_ge(scored, n + 1)
                            if i >= nbuf:
                                dve.wait_ge(ring_ready, ring.filled(("turned", i - nbuf, 2)))
                            src = in_banks(n).rearrange("p a (h s) -> p a h s", s=S)
                            chain(dve.tensor_reduce(top[:, n % 2, :].rearrange("p (a h) -> p a h", a=2), src, AX.X, ALU.max))
                            halves = []
                            for j in range(2):
                                hs = slice(j * UH // 2, (j + 1) * UH // 2)
                                halves.append(dve.tensor_tensor(
                                    by_head(half_of(pr[:, i % nbuf, :], m))[:, hs, :], src[:, j],
                                    top[:, n % 2, hs].unsqueeze(2).broadcast_to([P, UH // 2, S]), ALU.subtract))
                            chain(halves[0])
                            halves[1].then_inc(taken, 1)
                        elif what == "shift":
                            n, = args
                            i, m = units[n]
                            dve.wait_ge(masked, n + 1)
                            s_ = by_head(half_of(pr[:, i % nbuf, :], m))
                            chain(dve.tensor_reduce(top[:, n % 2, :], s_, AX.X, ALU.max))
                            dve.tensor_tensor(s_, s_, top[:, n % 2, :].unsqueeze(2).broadcast_to([P, UH, S]),
                                              ALU.subtract).then_inc(shifted, 1)
                        elif what == "invert":
                            n, = args
                            i, m = units[n]
                            dve.wait_ge(exped, n + 1)
                            chain(dve.tensor_reduce(tot[:, n % 2, :], by_head(half_of(pr[:, i % nbuf, :], m)), AX.X, ALU.add))
                            if n >= 4:
                                dve.wait_ge(weighted, n - 3)
                            dve.reciprocal(inv[:, n % 4, :], tot[:, n % 2, :]).then_inc(inverted, 1)
                        elif what == "out":
                            i, = args
                            dve.wait_ge(outs_ready, i + 1)
                            dve.tensor_tensor(x[:, b, i, :], out_of(i), x[:, b, i, :], ALU.add).then_inc(added, 1)
                        else:
                            if b is None:
                                dve.wait_ge(loaded, 16 * nload)
                            dve.wait_ge(ring_ready, ring.filled(token))
                            bk = ring.bank(token)
                            if is_split(token):
                                dve.wait_ge(rounded, splits.index(token) + 1)
                                dst, n, factor = split_of(token)
                                ins = dve.scalar_tensor_tensor(dst[:, 1], bk[:, 0:n], factor, dst[:, 0].bitcast(F32),
                                                               ALU.mult, ALU.subtract)
                            elif what in ("turn", "vw"):
                                dst, n, _ = split_of(token)
                                ins = dve.tensor_copy(dst[:, 0], bk[:, 0:n])
                            elif what in ("k", "v"):
                                dst, o = (kbd, 0) if what == "k" else (vbd, P)
                                if last:
                                    for h in range(hk):
                                        rows = slice(h * dk, (h + 1) * dk)
                                        ins = dve.tensor_copy(
                                            dst[rows, per * args[0]:per * (args[0] + 1), o + h * S:o + (h + 1) * S],
                                            bk[rows, 0:per * S].rearrange("p (c s) -> p c s", s=S))
                                else:
                                    for m in range(ND):
                                        t = kv[:, int(what == "v"), m, :]
                                        bias = (bk_ if what == "k" else bv)[:, m:m + 1]
                                        chain(dve.tensor_scalar(t, bk[:, m * S:(m + 1) * S], bias, None, ALU.add))
                                        ins = dve.tensor_tensor(by_head(dst[:, m, o:o + wk_]),
                                                                t.unsqueeze(1).broadcast_to([P, UH, S]),
                                                                heads[:].unsqueeze(2).broadcast_to([P, UH, S]), ALU.mult)
                            ins.then_inc(emptied_v, 1)
            clear(nc, [sem(n) for n in names] + side + [sem("stored")])
            if b is None and following:
                clear(nc, [loaded])

        run(None, 0, True, None)
        run(0, 1, True, None)
        with nc.Fori(1, B - 1) as b:
            run(b, b + 1, True, b - 1)
        run(B - 1, None, False, B - 2)
        run(None, None, False, B - 1)


def arrays(inputs):
    import numpy as np
    t = lambda v, *axes: np.ascontiguousarray(np.transpose(v, axes or None))
    out = {k: np.ascontiguousarray(v) for k, v in inputs.items() if k[0:2] in ("L0", "L1", "L2", "L3")}
    out["x"] = np.ascontiguousarray(inputs["x"])
    out["ctxT"] = t(inputs["ctx_1024"], 0, 2, 1)
    out["fside"] = t(inputs["fside_Bx16xSxS2_0"], 0, 2, 1, 3).reshape(B, T, HS)
    out["mask"] = t(inputs["mask_Bx16xSxS2_bk0"], 0, 2, 1, 3).reshape(B, T, HS)
    for name in ("L1_xattn_Wqf", "L1_xattn_Wkf", "L2_xattn_Wq", "L2_xattn_Wk", "L2_xattn_Wv", "L2_xattn_Wo",
                 "L3_xattn_wq"):
        out[name] = t(inputs[name])
    return out


def kernel(**inputs):
    import numpy as np
    import concourse.bacc as bacc
    from concourse.bass_utils import run_bass_kernel_spmd

    nc = bacc.Bacc("TRN2", target_bir_lowering=False, num_devices=1)
    sent = {f"in_{k}": v for k, v in arrays(inputs).items()}
    a = {k[3:]: nc.dram_tensor(k, v.shape, mybir.dt.from_np(v.dtype), kind="ExternalInput").ap()
         for k, v in sent.items()}
    out = nc.dram_tensor("out", [B, T, D], F32, kind="ExternalOutput").ap()
    build(nc, a, out)
    return run_bass_kernel_spmd(nc, [sent], core_ids=[0]).results[0]["out"]
```
